# Optimizing a Trainium2 kernel written in Bass

```python
import numpy as np
import jax
import jax.numpy as jnp

def _softmax(x, axis=-1):
    return jax.nn.softmax(x, axis=axis)
def _gelu(x):
    return jax.nn.gelu(x, approximate=True)
def _silu(x):
    return jax.nn.silu(x)
def _sigmoid(x):
    return jax.nn.sigmoid(x)
def _layernorm(x, axis=-1, eps=1e-5):
    m = jnp.mean(x, axis=axis, keepdims=True)
    v = jnp.var(x, axis=axis, keepdims=True)
    return (x - m) / jnp.sqrt(v + eps)
def _scatter_add(tgt, idx, src, axis=0):
    return tgt.at[idx].add(src)
def _segment_sum(src, seg, n):
    return jax.ops.segment_sum(src, seg, n)

kernel_name = 'mk_adj_resnorm_d4_adj_256_a24c0c'

def setup_inputs(seed: int = 0):
    np.random.seed(seed)
    _w = jnp.asarray
    def _rec_inputs():
        import jax
        import jax.numpy as jnp
        _gk = jax.random.key(seed)
        x = -0.000929 + 1 * jax.random.normal(jax.random.fold_in(_gk, 1), (4096, 256), jnp.float32)
        _w = (1.0 + jnp.arange(4096, dtype=jnp.float32)) ** -0.5
        _w = _w / _w.mean()
        _pij = jnp.clip(0.0078125 * _w[:, None] * _w[None, :], 0.0, 1.0)
        _a = jax.random.uniform(jax.random.fold_in(_gk, 2), (4096, 4096)) < _pij
        adj = _a.astype(jnp.int32)
        return x, adj
    x, adj = _rec_inputs()
    def _L0_gnn_setup():
        import jax, jax.numpy as jnp
        import numpy as np
        N = 4096
        F_IN = 256
        H = 4
        DH = 64
        key = jax.random.key(seed)
        k1, k2, k3, k4 = jax.random.split(key, 4)
        x = jax.random.normal(k1, (N, F_IN), dtype=jnp.float32)
        adj = jax.random.randint(k2, (N, N), 0, 2, dtype=jnp.int32)
        lim_w = float(np.sqrt(6.0 / (F_IN + DH)))
        W = jax.random.uniform(k3, (H, F_IN, DH), jnp.float32, -lim_w, lim_w)
        lim_a = float(np.sqrt(6.0 / (2 * DH + 1)))
        a = jax.random.uniform(k4, (H, 2 * DH, 1), jnp.float32, -lim_a, lim_a)
        return {'x': x, 'adj': adj, 'W': W, 'a': a}
    _L0_gnn_all = _L0_gnn_setup()
    _L0_gnn_in = {k: v for k, v in _L0_gnn_all.items() if k in ('W', 'a', )}
    del _L0_gnn_all

    def _L1_gnn_setup():
        import jax, jax.numpy as jnp
        import numpy as np
        N, IN_F, H, D = (4096, 256, 4, 64)
        NEG_BIG = -9000000000000000.0
        key = jax.random.key(seed)
        k1, k2, k3, k4, k5 = jax.random.split(key, 5)
        x = jax.random.normal(k1, (N, IN_F), dtype=jnp.float32)
        adj = jax.random.randint(k2, (N, N), 0, 2, dtype=jnp.int32)
        lim_w = float(np.sqrt(6.0 / (IN_F + H * D)))
        W = jax.random.uniform(k3, (IN_F, H * D), minval=-lim_w, maxval=lim_w, dtype=jnp.float32)
        lim_a = float(np.sqrt(6.0 / (2 * D + 1)))
        a1 = jax.random.uniform(k4, (D,), minval=-lim_a, maxval=lim_a, dtype=jnp.float32)
        a2 = jax.random.uniform(k5, (D,), minval=-lim_a, maxval=lim_a, dtype=jnp.float32)
        return {'x': x, 'adj': adj, 'W': W, 'a1': a1, 'a2': a2}
    _L1_gnn_all = _L1_gnn_setup()
    _L1_gnn_in = {k: v for k, v in _L1_gnn_all.items() if k in ('W', 'a1', 'a2', )}
    del _L1_gnn_all

    def _L2_gnn_setup():
        import jax, jax.numpy as jnp
        import numpy as np
        N = 8192
        F_IN = 256
        F_OUT = 256
        S = 128
        D_INNER = 512

        def _ln(x, g, b, eps=1e-05):
            m = x.mean(-1, keepdims=True)
            v = ((x - m) ** 2).mean(-1, keepdims=True)
            return (x - m) / jnp.sqrt(v + eps) * g + b
        key = jax.random.key(seed)
        ks = jax.random.split(key, 20)
        s = 0.05
        d = {}
        d['h'] = jax.random.normal(ks[0], (N, F_IN), dtype=jnp.float32)
        d['adj'] = jax.random.randint(ks[1], (N, N), 0, 2, dtype=jnp.int32)
        d['W'] = jax.random.normal(ks[2], (F_IN, F_OUT), dtype=jnp.float32) * s
        d['a_src'] = jax.random.normal(ks[3], (F_OUT, 1), dtype=jnp.float32) * s
        d['a_dst'] = jax.random.normal(ks[4], (F_OUT, 1), dtype=jnp.float32) * s
        d['W_bcdt'] = jax.random.normal(ks[5], (F_OUT, 3 * S), dtype=jnp.float32) * s
        d['b_bcdt'] = jnp.zeros((3 * S,), jnp.float32)
        d['abp_w'] = jax.random.normal(ks[6], (S, F_OUT), dtype=jnp.float32) * s
        d['abp_b'] = jnp.zeros((F_OUT,), jnp.float32)
        d['cp_w'] = jax.random.normal(ks[7], (S, 1), dtype=jnp.float32) * s
        d['cp_b'] = jnp.zeros((1,), jnp.float32)
        d['W_hz'] = jax.random.normal(ks[8], (F_OUT, 2 * D_INNER), dtype=jnp.float32) * s
        d['b_hz'] = jnp.zeros((2 * D_INNER,), jnp.float32)
        d['out_w'] = jax.random.normal(ks[9], (D_INNER, F_OUT), dtype=jnp.float32) * s
        d['out_b'] = jnp.zeros((F_OUT,), jnp.float32)
        d['fe1_w'] = jax.random.normal(ks[10], (F_OUT, D_INNER), dtype=jnp.float32) * s
        d['fe1_b'] = jnp.zeros((D_INNER,), jnp.float32)
        d['fe_ln_g'] = jnp.ones((D_INNER,), jnp.float32)
        d['fe_ln_b'] = jnp.zeros((D_INNER,), jnp.float32)
        d['fe2_w'] = jax.random.normal(ks[11], (D_INNER, F_OUT), dtype=jnp.float32) * s
        d['fe2_b'] = jnp.zeros((F_OUT,), jnp.float32)
        d['A'] = jax.random.uniform(ks[12], (S,), minval=1.0, maxval=64.0, dtype=jnp.float32)
        d['D'] = jnp.ones((1,), jnp.float32)
        d['g1_w'] = jax.random.normal(ks[13], (2 * F_OUT, 2 * F_OUT), dtype=jnp.float32) * s
        d['g1_b'] = jnp.zeros((2 * F_OUT,), jnp.float32)
        d['g_ln_g'] = jnp.ones((2 * F_OUT,), jnp.float32)
        d['g_ln_b'] = jnp.zeros((2 * F_OUT,), jnp.float32)
        d['g2_w'] = jax.random.normal(ks[14], (2 * F_OUT, F_OUT), dtype=jnp.float32) * s
        d['g2_b'] = jnp.zeros((F_OUT,), jnp.float32)
        d['ln_g'] = jnp.ones((F_OUT,), jnp.float32)
        d['ln_b'] = jnp.zeros((F_OUT,), jnp.float32)
        return d
    _L2_gnn_all = _L2_gnn_setup()
    _L2_gnn_in = {k: v for k, v in _L2_gnn_all.items() if k in ('W', 'a_src', 'a_dst', 'W_bcdt', 'b_bcdt', 'abp_w', 'abp_b', 'cp_w', 'cp_b', 'W_hz', 'b_hz', 'out_w', 'out_b', 'fe1_w', 'fe1_b', 'fe_ln_g', 'fe_ln_b', 'fe2_w', 'fe2_b', 'A', 'D', 'g1_w', 'g1_b', 'g_ln_g', 'g_ln_b', 'g2_w', 'g2_b', 'ln_g', 'ln_b', )}
    del _L2_gnn_all

    def _L3_gnn_setup():
        import jax, jax.numpy as jnp
        import numpy as np
        N, D_IN, D_OUT = (10000, 256, 256)
        key = jax.random.key(seed)
        k1, k2, k3, k4 = jax.random.split(key, 4)

        def xavier(k, shape, gain=1.414):
            fan_in, fan_out = (shape[0], shape[1])
            bound = gain * np.sqrt(6.0 / (fan_in + fan_out))
            return jax.random.uniform(k, shape, jnp.float32, -bound, bound)
        return {'input': jax.random.normal(k1, (N, D_IN), jnp.float32), 'adj': jax.random.randint(k2, (N, N), 0, 2, jnp.int32), 'M': N, 'W': xavier(k3, (D_IN, D_OUT)), 'b': jnp.zeros((D_OUT,), jnp.float32), 'a': xavier(k4, (D_OUT, 1))}
    _L3_gnn_all = _L3_gnn_setup()
    _L3_gnn_in = {k: v for k, v in _L3_gnn_all.items() if k in ('W', 'b', 'a', )}
    del _L3_gnn_all

    return {
        "x": x,
        "adj": adj,
        "L0_gnn_W": _L0_gnn_in["W"],
        "L0_gnn_a": _L0_gnn_in["a"],
        "L1_gnn_W": _L1_gnn_in["W"],
        "L1_gnn_a1": _L1_gnn_in["a1"],
        "L1_gnn_a2": _L1_gnn_in["a2"],
        "L2_gnn_W": _L2_gnn_in["W"],
        "L2_gnn_a_src": _L2_gnn_in["a_src"],
        "L2_gnn_a_dst": _L2_gnn_in["a_dst"],
        "L2_gnn_W_bcdt": _L2_gnn_in["W_bcdt"],
        "L2_gnn_b_bcdt": _L2_gnn_in["b_bcdt"],
        "L2_gnn_abp_w": _L2_gnn_in["abp_w"],
        "L2_gnn_abp_b": _L2_gnn_in["abp_b"],
        "L2_gnn_cp_w": _L2_gnn_in["cp_w"],
        "L2_gnn_cp_b": _L2_gnn_in["cp_b"],
        "L2_gnn_W_hz": _L2_gnn_in["W_hz"],
        "L2_gnn_b_hz": _L2_gnn_in["b_hz"],
        "L2_gnn_out_w": _L2_gnn_in["out_w"],
        "L2_gnn_out_b": _L2_gnn_in["out_b"],
        "L2_gnn_fe1_w": _L2_gnn_in["fe1_w"],
        "L2_gnn_fe1_b": _L2_gnn_in["fe1_b"],
        "L2_gnn_fe_ln_g": _L2_gnn_in["fe_ln_g"],
        "L2_gnn_fe_ln_b": _L2_gnn_in["fe_ln_b"],
        "L2_gnn_fe2_w": _L2_gnn_in["fe2_w"],
        "L2_gnn_fe2_b": _L2_gnn_in["fe2_b"],
        "L2_gnn_A": _L2_gnn_in["A"],
        "L2_gnn_D": _L2_gnn_in["D"],
        "L2_gnn_g1_w": _L2_gnn_in["g1_w"],
        "L2_gnn_g1_b": _L2_gnn_in["g1_b"],
        "L2_gnn_g_ln_g": _L2_gnn_in["g_ln_g"],
        "L2_gnn_g_ln_b": _L2_gnn_in["g_ln_b"],
        "L2_gnn_g2_w": _L2_gnn_in["g2_w"],
        "L2_gnn_g2_b": _L2_gnn_in["g2_b"],
        "L2_gnn_ln_g": _L2_gnn_in["ln_g"],
        "L2_gnn_ln_b": _L2_gnn_in["ln_b"],
        "L3_gnn_W": _L3_gnn_in["W"],
        "L3_gnn_b": _L3_gnn_in["b"],
        "L3_gnn_a": _L3_gnn_in["a"],
    }

def reference(x, adj, L0_gnn_W, L0_gnn_a, L1_gnn_W, L1_gnn_a1, L1_gnn_a2, L2_gnn_W, L2_gnn_a_src, L2_gnn_a_dst, L2_gnn_W_bcdt, L2_gnn_b_bcdt, L2_gnn_abp_w, L2_gnn_abp_b, L2_gnn_cp_w, L2_gnn_cp_b, L2_gnn_W_hz, L2_gnn_b_hz, L2_gnn_out_w, L2_gnn_out_b, L2_gnn_fe1_w, L2_gnn_fe1_b, L2_gnn_fe_ln_g, L2_gnn_fe_ln_b, L2_gnn_fe2_w, L2_gnn_fe2_b, L2_gnn_A, L2_gnn_D, L2_gnn_g1_w, L2_gnn_g1_b, L2_gnn_g_ln_g, L2_gnn_g_ln_b, L2_gnn_g2_w, L2_gnn_g2_b, L2_gnn_ln_g, L2_gnn_ln_b, L3_gnn_W, L3_gnn_b, L3_gnn_a):
    import jax
    import jax.numpy as jnp
    def _L0_gnn_ref(x, adj, W, a):
        import jax, jax.numpy as jnp
        import numpy as np
        N = 4096
        F_IN = 256
        H = 4
        DH = 64
        h = jnp.einsum('nf,hfd->hnd', x, W)
        a1 = a[:, :DH, 0]
        a2 = a[:, DH:, 0]
        s_src = jnp.einsum('hnd,hd->hn', h, a1)
        s_dst = jnp.einsum('hnd,hd->hn', h, a2)
        e = jax.nn.leaky_relu(s_src[:, :, None] + s_dst[:, None, :], 0.01)
        e = jnp.where(adj[None, :, :] == 0, -jnp.inf, e)
        alpha = jax.nn.softmax(e, axis=-1)
        out = jnp.einsum('hij,hjd->hid', alpha, h)
        out = out.transpose(1, 0, 2).reshape(N, H * DH)
        return jax.nn.elu(out)

    def _L1_gnn_ref(x, adj, W, a1, a2):
        import jax, jax.numpy as jnp
        import numpy as np
        N, IN_F, H, D = (4096, 256, 4, 64)
        NEG_BIG = -9000000000000000.0
        n = x.shape[0]
        h = (x @ W).reshape(n, H, D)
        si = jnp.einsum('nhd,d->nh', h, a1)
        sj = jnp.einsum('nhd,d->nh', h, a2)
        e = jax.nn.leaky_relu(si[:, None, :] + sj[None, :, :], negative_slope=0.2)
        e = jnp.where(adj[:, :, None] > 0, e, NEG_BIG)
        att = jax.nn.softmax(e, axis=1)
        out = jnp.einsum('ijh,jhd->ihd', att, h)
        return out.reshape(n, H * D)

    def _L2_gnn_ref(h, adj, W, a_src, a_dst, W_bcdt, b_bcdt, abp_w, abp_b, cp_w, cp_b, W_hz, b_hz, out_w, out_b, fe1_w, fe1_b, fe_ln_g, fe_ln_b, fe2_w, fe2_b, A, D, g1_w, g1_b, g_ln_g, g_ln_b, g2_w, g2_b, ln_g, ln_b):
        import jax, jax.numpy as jnp
        import numpy as np
        N = 8192
        F_IN = 256
        F_OUT = 256
        S = 128
        D_INNER = 512

        def _ln(x, g, b, eps=1e-05):
            m = x.mean(-1, keepdims=True)
            v = ((x - m) ** 2).mean(-1, keepdims=True)
            return (x - m) / jnp.sqrt(v + eps) * g + b
        Wh = h @ W
        e = Wh @ a_src + (Wh @ a_dst).T
        e = jnp.where(e > 0, e, 0.2 * e)
        e = jnp.where(adj > 0, e, jnp.float32(-9000000000000000.0))
        attn = jax.nn.softmax(e, axis=1)
        h_attn = attn @ Wh
        h_enh = jax.nn.silu(_ln(Wh @ fe1_w + fe1_b, fe_ln_g, fe_ln_b)) @ fe2_w + fe2_b
        BCdt = Wh @ W_bcdt + b_bcdt
        B, C, dt = jnp.split(BCdt, 3, axis=1)
        Asm = jax.nn.softmax(dt + A[None, :], axis=1)
        ab = Asm * B @ abp_w + abp_b
        hs = Wh * ab
        hz = hs @ W_hz + b_hz
        h_part, z = jnp.split(hz, 2, axis=1)
        hs = (h_part * jax.nn.silu(z) + h_part * D) @ out_w + out_b
        c_proj = C @ cp_w + cp_b
        hs = hs * (1.0 + c_proj)
        comb = jnp.concatenate([h_attn, hs], axis=1)
        g = jax.nn.sigmoid(jax.nn.silu(_ln(comb @ g1_w + g1_b, g_ln_g, g_ln_b)) @ g2_w + g2_b)
        fused = g * h_attn + (1.0 - g) * hs + h_enh
        return _ln(fused, ln_g, ln_b)

    def _L3_gnn_ref(input, adj, M, W, b, a):
        import jax, jax.numpy as jnp
        import numpy as np
        N, D_IN, D_OUT = (10000, 256, 256)
        h = jnp.tanh(input @ W + b)
        inp = input @ W
        e = (h @ a)[:, 0]
        valid = jnp.sum(h, axis=1) != 0
        mask = (adj[:M] > 0) & valid[None, :]
        neg = jnp.asarray(-1e+30, h.dtype)
        scores = jnp.where(mask, e[None, :], neg)
        m = jnp.max(scores, axis=1, keepdims=True)
        w = jnp.where(mask, jnp.exp(scores - m), 0.0)
        denom = jnp.sum(w, axis=1, keepdims=True)
        att = w / jnp.maximum(denom, 1e-30)
        return att @ inp

    x = _layernorm(x + _L0_gnn_ref(x, adj, L0_gnn_W, L0_gnn_a), axis=-1)
    x = _layernorm(x + _L1_gnn_ref(x, adj, L1_gnn_W, L1_gnn_a1, L1_gnn_a2), axis=-1)
    x = _layernorm(x + _L2_gnn_ref(x, adj, L2_gnn_W, L2_gnn_a_src, L2_gnn_a_dst, L2_gnn_W_bcdt, L2_gnn_b_bcdt, L2_gnn_abp_w, L2_gnn_abp_b, L2_gnn_cp_w, L2_gnn_cp_b, L2_gnn_W_hz, L2_gnn_b_hz, L2_gnn_out_w, L2_gnn_out_b, L2_gnn_fe1_w, L2_gnn_fe1_b, L2_gnn_fe_ln_g, L2_gnn_fe_ln_b, L2_gnn_fe2_w, L2_gnn_fe2_b, L2_gnn_A, L2_gnn_D, L2_gnn_g1_w, L2_gnn_g1_b, L2_gnn_g_ln_g, L2_gnn_g_ln_b, L2_gnn_g2_w, L2_gnn_g2_b, L2_gnn_ln_g, L2_gnn_ln_b), axis=-1)
    x = _layernorm(x + _L3_gnn_ref(x, adj, 4096, L3_gnn_W, L3_gnn_b, L3_gnn_a), axis=-1)
    return x


_drawn_inputs = setup_inputs


def setup_inputs(seed=0):
    import zlib

    import numpy as np

    out = dict(_drawn_inputs(seed))
    spreads = {'L2_gnn_b_bcdt': (0.0, 0.8),
     'L2_gnn_abp_b': (0.0, 0.1),
     'L2_gnn_b_hz': (0.0, 0.1),
     'L2_gnn_out_b': (0.0, 0.1),
     'L2_gnn_fe1_b': (0.0, 0.1),
     'L2_gnn_fe_ln_g': (1.0, 0.2),
     'L2_gnn_fe_ln_b': (0.0, 0.1),
     'L2_gnn_fe2_b': (0.0, 0.1),
     'L2_gnn_g1_b': (0.0, 0.379),
     'L2_gnn_g_ln_g': (1.0, 0.6),
     'L2_gnn_g_ln_b': (0.0, 0.8),
     'L2_gnn_g2_b': (0.0, 0.8),
     'L2_gnn_ln_g': (1.0, 0.2),
     'L2_gnn_ln_b': (0.0, 0.1),
     'L3_gnn_b': (0.0, 0.407)}
    factors = {'L2_gnn_a_src': 4.372, 'L2_gnn_abp_w': 8.0, 'L2_gnn_A': 8.0}
    for name, (base, spread) in spreads.items():
        noise = np.random.default_rng([zlib.crc32(name.encode()), seed]).standard_normal(out[name].shape)
        drawn = base * np.exp(spread * noise) if base else spread * noise
        out[name] = jnp.asarray(drawn.astype(out[name].dtype))
    for name, factor in factors.items():
        out[name] = (out[name] * factor).astype(out[name].dtype)
    return out
```

```python
from contextlib import ExitStack

import concourse.bass as bass
from concourse import mybir

ds = bass.ds
ALU = mybir.AluOpType
ACT = mybir.ActivationFunctionType
AX = mybir.AxisListType
RMAX = bass.bass_isa.ReduceOp.max
F32 = mybir.dt.float32
BF16 = mybir.dt.bfloat16
FP8 = mybir.dt.float8e4
U8 = mybir.dt.uint8
U32 = mybir.dt.uint32
I32 = mybir.dt.int32

P = 128
N = 4096
F = 256
T = N // P
PAIRS = T // 2
H = 4
D = F // H
C = D + 1
PARTS = 3
KW = PARTS * C
GT = 4
GI = GT * P
NG = N // GI
BITS = 8
Q = T // BITS
WORDS = GI // 4
ONE = 0x40404040
BIG = 2.0 ** 60
SLOPES = (0.01, 0.2, 0.2)
EPS = 1e-5
CHUNK = 8
FIRST_CHUNKS = T // CHUNK
CHUNKS = FIRST_CHUNKS + H * NG
UNITS = NG * BITS
DI = 512
SD = 128
ET = 2
EI = ET * P
EG = T // ET
CREDIT = 2


NORM_LINKS = {1: 8, 2: 4, 3: 2, 4: 4}


class Chain:

    def __init__(self, sem):
        self.sem, self.start, self.local, self.base = sem, 0, 0, 0

    def enter(self, i, per):
        self.base, self.per, self.local = self.start + i * per, per, 0

    def settle(self):
        self.start += self.local
        self.base, self.local = self.start, 0

    def leave(self, trips):
        assert self.local == self.per, (self.local, self.per)
        self.start += trips * self.per
        self.base, self.local = self.start, 0

    def next(self):
        self.local += 1
        return self.base + self.local


def gnn_kernel(nc, A, out, last_layer=3):
    with ExitStack() as ctx:
        def sb(name, shape, dt=F32):
            return ctx.enter_context(nc.sbuf_tensor(name, shape, dt))

        def sem(name):
            return ctx.enter_context(nc.semaphore(name))

        packed = sb("packed", [P, Q, N // 4], U32)
        x = sb("x", [P, T, F])
        h = sb("h", [P, T, F])
        values = sb("values", [P, 2, T, 2 * KW], BF16)
        above = sb("above", [P, 2, Q, GI], FP8)
        rings = sb("rings", [P, CHUNK * 2 * C + 2 * (2 * Q * WORDS)], U32)
        ring = rings[:, CHUNK * 2 * C:].rearrange("p (o s q w) -> p o s q w", o=2, s=2, q=Q)
        edge = rings[:, 0:2 * Q * WORDS].rearrange("p (s q w) -> p s q w", s=2, q=Q)
        pos = ring[:, 0]
        neg = ring[:, 1]
        srow = sb("srow", [P, 2, GI])
        arena = sb("arena", [P, T * F])
        weights = sb("weights", [P, 2, F + 2 * H])
        avec = sb("avec", [P, 2, F])
        bvec = sb("bvec", [P, F])
        scores = sb("scores", [P, 2 * H, T])
        kscores = sb("kscores", [P, H, T])
        kpass = sb("kpass", [P, 2, T])
        emul = sb("emul", [P, 2, H, T])
        cmul = sb("cmul", [P, 2, H, T])
        zrow = sb("zrow", [P, 3, H, T])
        smax = sb("smax", [P, 2, H])
        srcT = sb("srcT", [P, P])
        sums = sb("sums", [P, 2, GT, 2, C])
        quot = sb("quot", [P, 3, GT, C])
        vtmp_pool = sb("vtmp_pool", [P, 2, CHUNK, C])
        vtmp_dve = rings[:, 0:CHUNK * 2 * C].bitcast(F32).rearrange("p (a n c) -> p a n c", a=2, c=C)
        xT = pos[:, 0].rearrange("p q w -> p (q w)").bitcast(F32).rearrange("p (s k n) -> p s k n", s=2, k=2)
        xs = pos[:, 1].rearrange("p q w -> p (q w)").bitcast(F32).rearrange("p (s f) -> p s f", s=2)
        tmpx = neg[:, :].rearrange("p s q w -> p (s q w)").bitcast(F32).rearrange("p (s a f) -> p s a f", s=2, a=2)
        lnst = sb("lnst", [P, 2, 16])
        exponents = sb("exponents", [P, 1 + GT])
        minus_half, minus_one = exponents[:, 0:1], exponents[:, 1:1 + GT].unsqueeze(2)
        credits = sb("credits", [P, 16])
        ident = sb("ident", [P, P])
        powers = sb("powers", [P, BITS, P], BF16)

        adj_in = arena[:, 0:4096].bitcast(I32).rearrange("p (s n) -> p s n", s=2)
        adj_bf = arena[:, 4096:6144].bitcast(BF16).rearrange("p (s n) -> p s n", s=2)
        attn2 = arena[:, :].rearrange("p (t f) -> p t f", f=F)
        packed_bytes = packed[:, :, :].bitcast(U8)

        vroom = values[:, :, :, :].rearrange("p s t c -> p (s t c)").bitcast(F32)
        rroom = rings[:, :].bitcast(F32)
        aroom = above[:, :, :, :].rearrange("p s q n -> p (s q n)").bitcast(F32)
        sroom = srow[:, :, :].rearrange("p s n -> p (s n)")
        proom = vtmp_pool[:, :, :, :].rearrange("p a n c -> p (a n c)")

        class Room:

            def __init__(self, view):
                self.view, self.at = view, 0

            def take(self, *shape):
                n = 1
                for d in shape:
                    n *= d
                piece = self.view[:, self.at:self.at + n]
                self.at += n
                assert self.at <= self.view.shape[1]
                names = "abc"[:len(shape)]
                if len(shape) == 1:
                    return piece
                return piece.rearrange(f"p ({' '.join(names)}) -> p {' '.join(names)}", **dict(zip(names, shape)))

        room = Room(vroom)
        m_fe1, m_fe2 = room.take(2, DI), room.take(4, F)
        m_bcdt, m_abp = room.take(2, 3 * SD), room.take(F)
        m_hz, m_out = room.take(2, 2 * DI), room.take(4, F)
        m_g1, m_g2 = room.take(4, DI), room.take(4, F)
        wide, wide_tanh, wideT = room.take(ET, DI), room.take(ET, DI), room.take(ET, 4, P)
        room = Room(arena[:, :])
        row_widths = {"b_bcdt": 3 * SD, "cp_w": SD, "out_b": F, "fe1_b": DI, "fe_ln_g": DI, "fe_ln_b": DI,
                      "fe2_b": F, "g1_b": DI, "g_ln_g": DI, "g_ln_b": DI, "g2_b": F, "ln_g": F, "ln_b": F,
                      "A": SD}
        row = {name: room.take(w) for name, w in row_widths.items()}
        hatt, hs2, henh, gate, fused = (room.take(ET, F) for _ in range(5))
        whs = room.take(ET, F)
        room = Room(rroom)
        whT, hsT, uT = room.take(2, EI), room.take(2, EI), room.take(4, EI)
        bcdt, baT = room.take(ET, 3 * SD), room.take(EI)
        room = Room(aroom)
        z_tanh, h_part = room.take(2, EI), room.take(2, EI)
        room = Room(sroom)
        z_sig, dt_exp = room.take(2, EI), room.take(ET, SD)
        room = Room(proom)
        ba, c_prod, est = room.take(ET, SD), room.take(SD), room.take(3, ET, 16)
        ecol = sb("ecol", [P, 32])
        c_abp, c_hz, c_hz_half = ecol[:, 0:2], ecol[:, 2:10], ecol[:, 10:14]
        c_d, c_cp, top_dt, sum_dt, inv_dt, one_c = (ecol[:, i:i + 1] for i in (14, 15, 16, 18, 20, 22))
        attn_dram = nc.dram_tensor("attn_dram", [N, F], F32)[:, :]

        bank = [ctx.enter_context(nc.psum_tensor(f"bank{i}", [P, 512], F32)) for i in range(8)]

        src_dram = [nc.dram_tensor(f"src_dram{l}", [H * T, P], F32)[:, :] for l in range(3)]

        s_x = sem("x_loaded")
        s_w = sem("weights_loaded")
        s_wfix = sem("weights_fixed")
        s_adj = [sem("adj_loaded0"), sem("adj_loaded1")]
        s_adjbf = sem("adj_is_bf16")
        s_packmm = sem("pack_matmul")
        s_packed = sem("packed_stored")
        s_const = sem("constants_made")
        s_dve = sem("dve_chain")
        s_pool = sem("pool_chain")
        s_elumin = sem("elu_min")
        s_eluexp = sem("elu_exp")
        s_var = sem("variance_made")
        s_rstd = sem("rstd_made")
        s_xmade = sem("x_made")
        s_xkept = sem("x_kept")
        s_xtps = sem("xt_in_psum")
        s_xt = sem("xt_made")
        s_hps = sem("h_in_psum")
        s_h = sem("h_made")
        s_tanhin = sem("tanh_in_made")
        s_tanh = sem("tanh_made")
        s_srcps = sem("src_in_psum")
        s_src = sem("src_transposed")
        s_srcst = sem("src_stored")
        s_pmax = sem("partition_max")
        s_max = sem("max_made")
        s_shift = sem("shifts_made")
        s_exps = sem("exps_made")
        s_emul = sem("layer3_weights_made")
        s_vfirst = sem("dve_values_made")
        s_vals = sem("values_made")
        s_srow = [sem("srow_loaded0"), sem("srow_loaded1")]
        s_above = sem("above_made")
        s_sides = sem("sides_made")
        s_unit = sem("unit_multiplied")
        s_sums = sem("sums_made")
        s_quot = sem("quotients_made")
        s_out = sem("out_stored")

        s_kpass = sem("pass_scores_made")


        class E:
            pass
        E.weights, E.rows, E.stored = sem("e_weights_loaded"), sem("e_rows_loaded"), sem("e_attention_stored")
        E.hatt, E.whs, E.ready = sem("e_attention_loaded"), sem("e_wh_staged"), sem("e_constants_ready")
        E.whT_ps, E.whT = sem("e_whT_in_psum"), sem("e_whT_made")
        E.bc_ps, E.top, E.exp, E.ba = (sem(n) for n in ("e_bcdt_in_psum", "e_dt_max", "e_dt_exp", "e_ba_made"))
        E.baT_ps, E.baT, E.ab_ps, E.hsT = (sem(n) for n in ("e_baT_in_psum", "e_baT_made", "e_abT_in_psum",
                                                            "e_hsT_made"))
        E.hz_ps, E.z_tanh, E.z_sig, E.uT = (sem(n) for n in ("e_hz_in_psum", "e_z_tanh", "e_z_sigmoid", "e_uT_made"))
        E.out_ps, E.hs2 = sem("e_out_in_psum"), sem("e_hs2_made")
        E.wide_ps, E.var, E.rstd, E.norm = (sem(n) for n in ("e_wide_in_psum", "e_wide_var", "e_wide_rstd",
                                                             "e_wide_normed"))
        E.lin, E.tanh, E.silu = (sem(n) for n in ("e_wide_scaled", "e_wide_tanh", "e_wide_silu"))
        E.T_ps, E.T = sem("e_wideT_in_psum"), sem("e_wideT_made")
        E.fe2_ps, E.henh, E.g2_ps, E.gate_in, E.gate = (sem(n) for n in (
            "e_fe2_in_psum", "e_henh_made", "e_g2_in_psum", "e_gate_in", "e_gate_tanh"))
        E.fused, E.fvar, E.frstd, E.fnorm, E.x = (sem(n) for n in (
            "e_fused", "e_fused_var", "e_fused_rstd", "e_fused_normed", "e_x_made"))

        block = ctx.enter_context(nc.Block())
        SUMS = NG * H + 1

        @block.sync
        def _(sp):
            def load_vector(dst, src):
                sp.dma_start(dst, src.partition_broadcast(P)).then_inc(s_w, 16)

            def load_weights(l):
                if l == 0:
                    for k in range(2):
                        sp.dma_start(weights[:, k, 0:F].rearrange("p (h d) -> p h d", h=H),
                                     A["L0_gnn_W"][:, k * P:(k + 1) * P, :].rearrange("h p d -> p h d"))\
                            .then_inc(s_w, 16)
                    for s in range(2):
                        for hd in range(H):
                            load_vector(avec[:, s, hd * D:(hd + 1) * D], A["L0_gnn_a"][hd, s * D:(s + 1) * D, 0])
                    return
                sp.dma_start(weights[:, :, 0:F], A[f"L{l}_gnn_W"].rearrange("(k p) f -> p k f", p=P))\
                    .then_inc(s_w, 16)
                if l == 1:
                    for s, name in enumerate(("L1_gnn_a1", "L1_gnn_a2")):
                        for hd in range(H):
                            load_vector(avec[:, s, hd * D:(hd + 1) * D], A[name])
                elif l == 2:
                    load_vector(avec[:, 0, :], A["L2_gnn_a_src"][:, 0])
                    load_vector(avec[:, 1, :], A["L2_gnn_a_dst"][:, 0])
                else:
                    load_vector(avec[:, 0, :], A["L3_gnn_a"][:, 0])
                    load_vector(bvec[:, :], A["L3_gnn_b"])

            def score_rows(l):
                sp.wait_ge(s_src, l + 1)
                sp.dma_start(src_dram[l], srcT[:, :]).then_inc(s_srcst, 16)
                sp.wait_ge(s_srcst, 16 * (l + 1))
                flat = src_dram[l].rearrange("a b -> (a b)")

                def load(slot, grp):
                    sp.dma_start(srow[:, slot, :], flat[ds(grp * GI, GI)].partition_broadcast(P))\
                        .then_inc(s_srow[slot], 16)

                first = 0
                if l == 0:
                    load(0, 0)
                    load(1, 1)
                    first = 1
                with sp.Fori(first, H * NG // 2) as gg:
                    for slot in range(2):
                        sp.wait_ge(s_above, (gg * 2 + (l * H * NG + slot - 1)) * BITS)
                        load(slot, gg * 2 + slot)

            def dense2():
                sp.wait_ge(s_quot, 3 * H * NG + CREDIT)
                sp.dma_start(attn_dram.rearrange("(t p) f -> p t f", p=P), attn2).then_inc(E.stored, 16)
                sp.wait_ge(s_vals, 3 * CHUNKS)
                sp.wait_ge(s_unit, 3 * H * UNITS + CREDIT)
                for name, m in (("W_bcdt", m_bcdt), ("fe1_w", m_fe1), ("W_hz", m_hz), ("fe2_w", m_fe2),
                                ("out_w", m_out), ("g1_w", m_g1), ("g2_w", m_g2)):
                    sp.dma_start(m, A[f"L2_gnn_{name}"].rearrange("(k p) f -> p k f", p=P)).then_inc(E.weights, 16)
                sp.dma_start(m_abp, A["L2_gnn_abp_w"]).then_inc(E.weights, 16)
                for name, c in (("abp_b", c_abp), ("b_hz", c_hz)):
                    sp.dma_start(c, A[f"L2_gnn_{name}"].rearrange("(c p) -> p c", p=P),
                                 allow_slow_non_contiguous=True).then_inc(E.rows, 16)
                for name, c in (("D", c_d), ("cp_b", c_cp)):
                    sp.dma_start(c, A[f"L2_gnn_{name}"].partition_broadcast(P)).then_inc(E.rows, 16)
                sp.wait_ge(E.stored, 16)
                for name, r in row.items():
                    src = A[f"L2_gnn_{name}"]
                    src = src[:, 0] if name == "cp_w" else src
                    sp.dma_start(r, src.partition_broadcast(P)).then_inc(E.rows, 16)

                def load_attention(g):
                    sp.dma_start(hatt, attn_dram[ds(g * EI, EI), :].rearrange("(t p) f -> p t f", p=P))\
                        .then_inc(E.hatt, 16)

                load_attention(0)
                with sp.Fori(1, EG) as g:
                    sp.wait_ge(E.fused, g)
                    load_attention(g)

            sp.dma_start(x[:, :, :], A["x"].rearrange("(t p) f -> p t f", p=P)).then_inc(s_x, 16)
            load_weights(0)
            for half in range(2):
                sp.dma_start(adj_in[:, half, :], A["adj"][0:P, half * 2048:(half + 1) * 2048])\
                    .then_inc(s_adj[half], 16)
            with sp.Fori(1, T) as t:
                for half in range(2):
                    sp.wait_ge(s_adjbf, t * 2 + (half - 1))
                    sp.dma_start(adj_in[:, half, :], A["adj"][ds(t * P, P), half * 2048:(half + 1) * 2048])\
                        .then_inc(s_adj[half], 16)
            for l in range(4):
                if l < 3:
                    score_rows(l)
                if l < min(3, last_layer):
                    sp.wait_ge(s_h, T * (l + 1) + 1)
                    load_weights(l + 1)
                if l == 2:
                    dense2()
                if l == last_layer:
                    break
            sp.wait_ge(s_xmade, T * (last_layer + 2))
            sp.dma_start(out.rearrange("(t p) f -> p t f", p=P), x[:, :, :]).then_inc(s_out, 16)
            sp.wait_ge(s_out, 16)

        loaded_weights = [16 * 10, 16 * 19, 16 * 22, 16 * 25]

        def value_parts(eng, chain, vtmp, kind, j0, n, p, slot):
            big, rest = vtmp[:, 0, 0:n, :], vtmp[:, 1, 0:n, :]
            e = emul[:, kind, ds(p, 1), ds(j0, n)].rearrange("p a n -> p n a")
            part = [values[:, slot, ds(j0, n), kind * KW + i * C:kind * KW + (i + 1) * C] for i in range(PARTS)]
            eng.tensor_copy(big[:, :, D:C], e)
            eng.tensor_tensor(big[:, :, 0:D], h[:, ds(j0, n), ds(p * D, D)],
                              e.to_broadcast([P, n, D]), ALU.mult).then_inc(chain.sem, 1)
            eng.wait_ge(chain.sem, chain.next())
            eng.nop(nofuse=True)
            eng.tensor_copy(part[0], big).then_inc(chain.sem, 1)
            eng.wait_ge(chain.sem, chain.next())
            eng.nop(nofuse=True)
            eng.tensor_tensor(rest, big, part[0], ALU.subtract).then_inc(chain.sem, 1)
            eng.wait_ge(chain.sem, chain.next())
            eng.nop(nofuse=True)
            eng.tensor_copy(part[1], rest).then_inc(chain.sem, 1)
            eng.wait_ge(chain.sem, chain.next())
            eng.nop(nofuse=True)
            return eng.tensor_tensor(part[2], rest, part[1], ALU.subtract)

        VALUE_LINKS = 4

        @block.gpsimd
        def _(pool):
            chain = Chain(s_pool)
            pool.memset(exponents[:, 1:1 + GT], -1.0)
            for i, signal in enumerate((s_quot, s_quot, s_xkept)):
                pool.memset(credits[:, i:i + 1], 0.0).then_inc(signal, 1)
            pool.memset(ident[:, :], 0.0).then_inc(s_pool, 1)
            pool.wait_ge(s_pool, chain.next())
            pool.affine_select(out=ident[:, :], in_=ident[:, :], compare_op=ALU.not_equal, fill=1.0,
                               base=0, pattern=[[-1, P]], channel_multiplier=1).then_inc(s_pool, 1)
            pool.wait_ge(s_pool, chain.next())
            pool.memset(minus_half, -0.5).then_inc(s_pool, 1)
            pool.wait_ge(s_pool, chain.next())
            for k in range(BITS):
                last = pool.tensor_scalar(powers[:, k, :], ident[:, :], float(2 ** k), None, ALU.mult)
            last.then_inc(s_const, 1)
            chain.settle()

            def rstd_of_pairs(l):
                with pool.Fori(0, PAIRS) as tt:
                    chain.enter(tt, 2)
                    for par in range(2):
                        pool.wait_ge(s_var, tt * 2 + ((l - 1) * T + par + 1))
                        pool.nop(nofuse=True)
                        pool.tensor_scalar(lnst[:, par, 8:9], lnst[:, par, 7:8], EPS, None, ALU.add).then_inc(s_pool, 1)
                        pool.wait_ge(s_pool, chain.next())
                        pool.nop(nofuse=True)
                        pool.tensor_tensor(lnst[:, par, 9:10], lnst[:, par, 8:9], minus_half, ALU.pow)\
                            .then_inc(s_rstd, 1)
                    if l <= last_layer:
                        for par in range(2):
                            t = tt * 2 + par
                            pool.wait_ge(s_xmade, t + (l * T + 1))
                            pool.nop(nofuse=True)
                            pool.tensor_copy(x[:, ds(t, 1), :], xs[:, par:par + 1, :]).then_inc(s_xkept, 1)
                chain.leave(PAIRS)

            def stage_x():
                pool.wait_ge(s_x, 16)
                with pool.Fori(0, PAIRS) as tt:
                    pool.wait_ge(s_xtps, tt * 2 + 1)
                    pool.nop(nofuse=True)
                    for par in range(2):
                        pool.tensor_copy(xs[:, par:par + 1, :], x[:, ds(tt * 2 + par, 1), :]).then_inc(s_xmade, 1)

            def global_max(l):
                n = H if l < 3 else 1
                pool.wait_ge(s_pmax, l + 1)
                pool.partition_all_reduce(smax[:, 1, 0:n], smax[:, 0, 0:n], P, RMAX).then_inc(s_max, 1)

            def first_values(l):
                if l < 3:
                    pool.wait_ge(s_exps, l + 1)
                else:
                    pool.wait_ge(s_emul, 1)
                with pool.Fori(0, FIRST_CHUNKS) as c:
                    chain.enter(c, VALUE_LINKS)
                    value_parts(pool, chain, vtmp_pool, 0, c * CHUNK, CHUNK, 0, 0).then_inc(s_vals, 1)
                chain.leave(FIRST_CHUNKS)

            def attention(l):
                kinds = 2 if l < 3 else 1
                per_group = VALUE_LINKS * kinds + (3 if l < 3 else 2)
                target = attn2 if l == 2 else h
                with pool.Fori(0, H // 2) as pp:
                    for slot in range(2):
                        p = pp * 2 + slot
                        nxt = p + 1 if slot == 0 else (2 - pp * 2)
                        pool.wait_ge(s_unit, p * UNITS + (CREDIT + l * H * UNITS))
                        pool.nop(nofuse=True)
                        with pool.Fori(0, NG // 2) as gg:
                            for par in range(2):
                                g = gg * 2 + par
                                chain.enter(p * NG + g, per_group)
                                for kind in range(kinds):
                                    made = value_parts(pool, chain, vtmp_pool, kind, g * GT, GT, nxt, 1 - slot)
                                made.then_inc(s_vals, 1)
                                pool.wait_ge(s_sums, p * NG + g + (l * SUMS + 3))
                                pool.nop(nofuse=True)
                                dst = target[:, ds(g * GT, GT), ds(p * D, D)]
                                if l < 3:
                                    c = [cmul[:, s, ds(p, 1), ds(g * GT, GT)].rearrange("p a n -> p n a")
                                         .to_broadcast([P, GT, C]) for s in range(2)]
                                    pool.tensor_tensor(quot[:, 0], sums[:, par, :, 0, :], c[0], ALU.mult)
                                    pool.tensor_tensor(quot[:, 1], sums[:, par, :, 1, :], c[1], ALU.mult)\
                                        .then_inc(s_pool, 1)
                                    pool.wait_ge(s_pool, chain.next())
                                    pool.nop(nofuse=True)
                                    pool.tensor_tensor(quot[:, 2], quot[:, 0], quot[:, 1], ALU.add).then_inc(s_pool, 1)
                                    pool.wait_ge(s_pool, chain.next())
                                    pool.nop(nofuse=True)
                                    total, inverse = quot[:, 2], quot[:, 0, :, 0:1]
                                    pool.tensor_tensor(inverse, total[:, :, D:C], minus_one, ALU.pow)\
                                        .then_inc(s_pool, 1)
                                    pool.wait_ge(s_pool, chain.next())
                                    pool.nop(nofuse=True)
                                else:
                                    total, inverse = sums[:, par, :, 0, :], quot[:, 1, :, 0:1]
                                    pool.tensor_scalar(quot[:, 0, :, 0:1], total[:, :, D:C],
                                                       2e-38, None, ALU.max).then_inc(s_pool, 1)
                                    pool.wait_ge(s_pool, chain.next())
                                    pool.nop(nofuse=True)
                                    pool.tensor_tensor(inverse, quot[:, 0, :, 0:1], minus_one, ALU.pow)\
                                        .then_inc(s_pool, 1)
                                    pool.wait_ge(s_pool, chain.next())
                                    pool.nop(nofuse=True)
                                done = pool.tensor_tensor(dst, total[:, :, 0:D],
                                                          inverse.to_broadcast([P, GT, D]), ALU.mult)
                                done.then_inc(s_quot, 1)
                chain.leave(H * NG)

            def rstd(stats, waits, at, signal):
                pool.wait_ge(waits, at)
                pool.nop(nofuse=True)
                pool.tensor_scalar(stats[:, 8:9], stats[:, 7:8], EPS, None, ALU.add).then_inc(s_pool, 1)
                pool.wait_ge(s_pool, chain.next())
                pool.nop(nofuse=True)
                pool.tensor_tensor(stats[:, 9:10], stats[:, 8:9], minus_half, ALU.pow).then_inc(signal, 1)

            def dense2():
                pool.wait_ge(E.stored, 16)
                pool.wait_ge(E.rows, 16 * (4 + len(row)))

                def wide_scale(g, which, gain, shift):
                    for t in range(ET):
                        rstd(est[:, which, t, :], E.var, g * (2 * ET) + (which * ET + t + 1), E.rstd)
                    for t in range(ET):
                        pool.wait_ge(E.norm, g * (2 * ET) + (which * ET + t + 1))
                        pool.nop(nofuse=True)
                        pool.tensor_tensor(wide[:, t, :], wide[:, t, :], row[gain], ALU.mult).then_inc(s_pool, 1)
                        pool.wait_ge(s_pool, chain.next())
                        pool.nop(nofuse=True)
                        pool.tensor_tensor(wide[:, t, :], wide[:, t, :], row[shift], ALU.add).then_inc(E.lin, 1)

                with pool.Fori(0, EG) as g:
                    chain.enter(g, 4 * ET + 3 + 3 * ET)
                    pool.tensor_copy(whs, h[:, ds(g * ET, ET), :]).then_inc(E.whs, 1)
                    wide_scale(g, 0, "fe_ln_g", "fe_ln_b")
                    for b in range(4):
                        pool.wait_ge(E.z_tanh, g * 4 + b + 1)
                        pool.nop(nofuse=True)
                        pool.tensor_scalar(z_sig[:, b % 2, :], z_tanh[:, b % 2, :], 0.5, 0.5, ALU.mult, ALU.add)\
                            .then_inc(E.z_sig, 1)
                    wide_scale(g, 1, "g_ln_g", "g_ln_b")
                    pool.wait_ge(E.henh, g + 1)
                    pool.nop(nofuse=True)
                    pool.wait_ge(E.hatt, (g + 1) * 16)
                    pool.nop(nofuse=True)
                    pool.tensor_tensor(fused, hatt, hs2, ALU.subtract)
                    pool.tensor_tensor(henh, henh, hs2, ALU.add).then_inc(s_pool, 1)
                    pool.wait_ge(s_pool, chain.next())
                    pool.nop(nofuse=True)
                    pool.wait_ge(E.gate, g + 1)
                    pool.nop(nofuse=True)
                    pool.tensor_scalar(gate, gate, 0.5, 0.5, ALU.mult, ALU.add).then_inc(s_pool, 1)
                    pool.wait_ge(s_pool, chain.next())
                    pool.nop(nofuse=True)
                    pool.tensor_tensor(fused, fused, gate, ALU.mult).then_inc(s_pool, 1)
                    pool.wait_ge(s_pool, chain.next())
                    pool.nop(nofuse=True)
                    pool.tensor_tensor(fused, fused, henh, ALU.add).then_inc(E.fused, 1)
                    for t in range(ET):
                        rstd(est[:, 2, t, :], E.fvar, g * ET + (t + 1), E.frstd)
                    for t in range(ET):
                        pool.wait_ge(E.fnorm, g * ET + (t + 1))
                        pool.nop(nofuse=True)
                        pool.tensor_tensor(fused[:, t, :], fused[:, t, :], row["ln_g"], ALU.mult).then_inc(s_pool, 1)
                        pool.wait_ge(s_pool, chain.next())
                        pool.nop(nofuse=True)
                        pool.tensor_tensor(fused[:, t, :], fused[:, t, :], row["ln_b"], ALU.add).then_inc(s_pool, 1)
                        pool.wait_ge(s_pool, chain.next())
                        pool.nop(nofuse=True)
                        xt = x[:, ds(g * ET + t, 1), :]
                        pool.tensor_tensor(xt, xt, fused[:, t:t + 1, :], ALU.add).then_inc(E.x, 1)
                chain.leave(EG)

            for l in range(last_layer + 1):
                if l == 3:
                    dense2()
                if l > 0:
                    rstd_of_pairs(l)
                else:
                    stage_x()
                global_max(l)
                first_values(l)
                attention(l)
            if last_layer == 2:
                dense2()
            rstd_of_pairs(last_layer + 1)

        @block.scalar
        def _(act):
            def dense(l, tt):
                if l == 1:
                    for par in range(2):
                        act.wait_ge(s_elumin, tt * 2 + par + 1)
                        act.nop(nofuse=True)
                        act.activation(tmpx[:, par, 1, :], tmpx[:, par, 0, :], ACT.Exp).then_inc(s_eluexp, 1)
                for par in range(2):
                    act.wait_ge(s_xtps, tt * 2 + (l * T + par + 2))
                    act.nop(nofuse=True)
                    act.activation(xT[:, par].rearrange("p k n -> p (k n)"), bank[par][:, 0:F], ACT.Copy)\
                        .then_inc(s_xt, 1)
                for par in range(2):
                    t = tt * 2 + par
                    act.wait_ge(s_hps, t + (l * T + 1))
                    act.nop(nofuse=True)
                    to_h = act.activation(h[:, ds(t, 1), :], bank[2 + par][:, 0:F].unsqueeze(1), ACT.Copy)
                    if l < 3:
                        to_h = act.activation(scores[:, :, ds(t, 1)], bank[2 + par][:, F:F + 2 * H].unsqueeze(2),
                                              ACT.Copy)
                    to_h.then_inc(s_h, 1)
                if l == 3:
                    for par in range(2):
                        t = tt * 2 + par
                        act.wait_ge(s_tanhin, t + 1)
                        act.nop(nofuse=True)
                        act.activation(tmpx[:, par, 1, :], tmpx[:, par, 0, :], ACT.Tanh,
                                       accum_out=scores[:, 0, ds(t, 1)]).then_inc(s_tanh, 1)

            def stats(l):
                if l < 3:
                    act.wait_ge(s_srcps, l + 1)
                    act.activation(srcT[:, :], bank[4][:, 0:P], ACT.Copy).then_inc(s_src, 1)
                act.wait_ge(s_shift, l + 1)
                e, c = (m[:, :, :, :].rearrange("p k h t -> p k (h t)") for m in (emul, cmul))
                if l < 3:
                    act.activation(e[:, 1], e[:, 0], ACT.Exp, scale=SLOPES[l])
                    act.activation(e[:, 0], e[:, 0], ACT.Exp)
                    act.activation(c, c, ACT.Exp).then_inc(s_exps, 1)
                else:
                    act.activation(emul[:, 0, 0, :], emul[:, 0, 0, :], ACT.Exp).then_inc(s_exps, 1)

            def attention(l):
                with act.Fori(0, H // 2) as pp:
                    for slot in range(2):
                        p = pp * 2 + slot
                        act.activation(kpass[:, slot:slot + 1, :], kscores[:, ds(p, 1), :], ACT.Copy)\
                            .then_inc(s_kpass, 1)
                        act.wait_ge(s_kpass, p + (l * H + 1))
                        act.nop(nofuse=True)
                        with act.Fori(0, NG // 2) as gg:
                            for par in range(2):
                                act.wait_ge(s_srow[par], (p * (NG // 2) + gg + (l * H * NG // 2 + 1)) * 16)
                                act.nop(nofuse=True)
                                for k in range(BITS):
                                    act.wait_ge(s_sides, (p * NG + gg * 2) * BITS + (l * H * UNITS + par * BITS + k - 1 + CREDIT))
                                    act.nop(nofuse=True)
                                    for q in range(Q):
                                        last = act.activation(
                                            above[:, k % 2, q, :], srow[:, par, :], ACT.Relu, scale=BIG,
                                            bias=kpass[:, slot, q * BITS + k:q * BITS + k + 1], saturate=False)
                                    last.then_inc(s_above, 1)

            def dense2():
                act.wait_ge(E.ready, 1)
                with act.Fori(0, EG) as g:
                    def copy_T(n, scale):
                        for t in range(ET):
                            act.wait_ge(E.T_ps, g * (3 * ET) + (n * ET + t + 1))
                            act.nop(nofuse=True)
                            act.activation(wideT[:, t].rearrange("p k n -> p (k n)"), bank[(7, 5)[t]][:, :],
                                           ACT.Copy, scale=scale).then_inc(E.T, 1)

                    def wide_tanhs(n):
                        for t in range(ET):
                            act.wait_ge(E.lin, g * (2 * ET) + (n * ET + t + 1))
                            act.nop(nofuse=True)
                            act.activation(wide_tanh[:, t, :], wide[:, t, :], ACT.Tanh, scale=0.5)\
                                .then_inc(E.tanh, 1)

                    act.wait_ge(E.whT_ps, g + 1)
                    act.nop(nofuse=True)
                    act.activation(whT.rearrange("p k n -> p (k n)"), bank[0][:, :], ACT.Copy).then_inc(E.whT, 1)
                    for t in range(ET):
                        act.wait_ge(E.top, g * ET + t + 1)
                        act.nop(nofuse=True)
                        act.activation(dt_exp[:, t, :], bcdt[:, t, 2 * SD:3 * SD], ACT.Exp,
                                       bias=ecol[:, 16 + t:17 + t], accum_out=ecol[:, 18 + t:19 + t])\
                            .then_inc(E.exp, 1)
                    act.wait_ge(E.baT_ps, g + 1)
                    act.nop(nofuse=True)
                    act.activation(baT, bank[5][:, 0:EI], ACT.Copy).then_inc(E.baT, 1)
                    for b in range(4):
                        act.wait_ge(E.hz_ps, g * 4 + b + 1)
                        act.nop(nofuse=True)
                        act.activation(h_part[:, b % 2, :], bank[1 + b % 2][:, 0:EI], ACT.Identity,
                                       bias=c_hz[:, b:b + 1])
                        act.activation(z_tanh[:, b % 2, :], bank[1 + b % 2][:, EI:2 * EI], ACT.Tanh, scale=0.5,
                                       bias=c_hz_half[:, b:b + 1]).then_inc(E.z_tanh, 1)
                        if b == 1:
                            wide_tanhs(0)
                    copy_T(0, 0.5)
                    copy_T(1, 1.0)
                    wide_tanhs(1)
                    copy_T(2, 0.5)
                    act.wait_ge(E.gate_in, g + 1)
                    act.nop(nofuse=True)
                    act.activation(gate, gate, ACT.Tanh, scale=0.5).then_inc(E.gate, 1)

            for l in range(last_layer + 1):
                if l == 3:
                    dense2()
                with act.Fori(0, PAIRS) as tt:
                    dense(l, tt)
                stats(l)
                if l < 3:
                    attention(l)
            if last_layer == 2:
                dense2()
            if last_layer == 0:
                with act.Fori(0, PAIRS) as tt:
                    for par in range(2):
                        act.wait_ge(s_elumin, tt * 2 + par + 1)
                        act.activation(tmpx[:, par, 1, :], tmpx[:, par, 0, :], ACT.Exp).then_inc(s_eluexp, 1)

        @block.tensor
        def _(pe):
            def dense(l, tt):
                for par in range(2):
                    pe.wait_ge(s_xmade, tt * 2 + (l * T + par + 1))
                    pe.nop(nofuse=True)
                    for k in range(2):
                        last = pe.transpose(bank[par][:, k * P:(k + 1) * P], xs[:, par, k * P:(k + 1) * P],
                                            ident[:, :])
                    last.then_inc(s_xtps, 1)
                pe.wait_ge(s_h, tt * 2 + (l * T + 1))
                pe.nop(nofuse=True)
                width = F + 2 * H if l < 3 else F
                for par in range(2):
                    pe.wait_ge(s_xt, tt * 2 + (l * T + par + 1))
                    pe.nop(nofuse=True)
                    for k in range(2):
                        last = pe.matmul(bank[2 + par][:, 0:width], xT[:, par, k, :], weights[:, k, 0:width],
                                         start=(k == 0), stop=(k == 1))
                    last.then_inc(s_hps, 1)

            def pack(tt):
                for par in range(2):
                    t = tt * 2 + par
                    pe.wait_ge(s_packed, tt * 2 + 1)
                    pe.nop(nofuse=True)
                    for half in range(2):
                        pe.wait_ge(s_adjbf, t * 2 + half + 1)
                        pe.nop(nofuse=True)
                        for q in range(2 * half, 2 * half + 2):
                            for k in range(BITS):
                                j = (q - 2 * half) * BITS + k
                                last = pe.matmul(bank[6 + par][:, q * P:(q + 1) * P],
                                                 adj_bf[:, half, j * P:(j + 1) * P], powers[:, k, :],
                                                 start=(k == 0), stop=(k == BITS - 1))
                        last.then_inc(s_packmm, 1)

            def src_rows(l):
                pe.wait_ge(s_h, T * (l + 1) + 1)
                pe.transpose(bank[4][:, 0:P], scores[:, 0:H, :].rearrange("p h t -> p (h t)"), ident[:, :])\
                    .then_inc(s_srcps, 1)

            def attention(l):
                if l < 3:
                    pe.wait_ge(s_vfirst, l + 1)
                with pe.Fori(0, H // 2) as pp:
                    for slot in range(2):
                        p = pp * 2 + slot
                        pe.wait_ge(s_vals, p * NG + (l * CHUNKS + FIRST_CHUNKS))
                        pe.nop(nofuse=True)
                        with pe.Fori(0, NG // 2) as gg:
                            for par in range(2):
                                pe.wait_ge(s_sums, p * NG + gg * 2 + (l * SUMS + par + 1))
                                pe.nop(nofuse=True)
                                for k in range(BITS):
                                    pe.wait_ge(s_sides, (p * NG + gg * 2) * BITS + (l * H * UNITS + par * BITS + k + 1 + CREDIT))
                                    pe.nop(nofuse=True)
                                    for q in range(Q):
                                        v = values[:, slot, q * BITS + k, :]
                                        first, final = (k == 0 and q == 0), (k == BITS - 1 and q == Q - 1)
                                        for it in range(GT):
                                            acc = bank[GT * par + it]
                                            rows = slice(it * P, (it + 1) * P)
                                            if l < 3:
                                                last = pe.matmul(acc[:, 0:KW], pos[:, k % 2, q, :].bitcast(FP8)[:, rows],
                                                                 v[:, 0:KW], start=first, stop=final,
                                                                 skip_group_check=True)
                                                last = pe.matmul(acc[:, KW:2 * KW],
                                                                 neg[:, k % 2, q, :].bitcast(FP8)[:, rows],
                                                                 v[:, KW:2 * KW], start=False, stop=final,
                                                                 skip_group_check=True)
                                            else:
                                                last = pe.matmul(acc[:, 0:KW],
                                                                 edge[:, k % 2, q, :].bitcast(FP8)[:, rows],
                                                                 v[:, 0:KW], start=first, stop=final)
                                    last.then_inc(s_unit, 1)

            def dense2():
                pe.wait_ge(E.weights, 16 * 8)

                def product(dst, lhsT, rhs):
                    for k in range(len(lhsT)):
                        last = pe.matmul(dst, lhsT[k], rhs[k], start=(k == 0), stop=(k == len(lhsT) - 1))
                    return last

                def rows(m, t):
                    return [m[:, k, t * P:(t + 1) * P] for k in range(m.shape[1])]

                def blocks(m, a=None, b=None):
                    return [m[:, k, a:b] for k in range(m.shape[1])]

                with pe.Fori(0, EG) as g:
                    def transposes(t, sources):
                        for i, src in enumerate(sources):
                            last = pe.transpose(bank[(7, 5)[t]][:, i * P:(i + 1) * P], src, ident[:, :])
                        last.then_inc(E.T_ps, 1)

                    def cut(tile, n):
                        return [tile[:, i * P:(i + 1) * P] for i in range(n)]

                    pe.wait_ge(E.whs, g + 1)
                    pe.nop(nofuse=True)
                    for k in range(2):
                        for t in range(ET):
                            last = pe.transpose(bank[0][:, k * EI + t * P:k * EI + (t + 1) * P],
                                                whs[:, t, k * P:(k + 1) * P], ident[:, :])
                    last.then_inc(E.whT_ps, 1)
                    pe.wait_ge(E.whT, g + 1)
                    pe.nop(nofuse=True)
                    for t in range(ET):
                        product(bank[1 + t][:, 0:3 * SD], rows(whT, t), blocks(m_bcdt)).then_inc(E.bc_ps, 1)
                    for t in range(ET):
                        product(bank[3 + t][:, :], rows(whT, t), blocks(m_fe1)).then_inc(E.wide_ps, 1)
                    pe.wait_ge(E.ba, (g + 1) * ET)
                    pe.nop(nofuse=True)
                    for t in range(ET):
                        last = pe.transpose(bank[5][:, t * P:(t + 1) * P], ba[:, t, :], ident[:, :])
                    last.then_inc(E.baT_ps, 1)
                    pe.wait_ge(E.baT, g + 1)
                    pe.nop(nofuse=True)
                    for b in range(2):
                        last = pe.matmul(bank[6][:, b * EI:(b + 1) * EI], m_abp[:, b * P:(b + 1) * P], baT,
                                         start=True, stop=True)
                    last.then_inc(E.ab_ps, 1)
                    pe.wait_ge(E.hsT, g + 1)
                    pe.nop(nofuse=True)
                    for b in range(4):
                        if b >= 2:
                            pe.wait_ge(E.uT, g * 4 + (b - 1))
                            pe.nop(nofuse=True)
                        for part in range(2):
                            c = part * DI + b * P
                            last = product(bank[1 + b % 2][:, part * EI:(part + 1) * EI],
                                           blocks(m_hz, c, c + P), blocks(hsT))
                        last.then_inc(E.hz_ps, 1)
                    for t in range(ET):
                        pe.wait_ge(E.silu, g * (2 * ET) + (t + 1))
                        pe.nop(nofuse=True)
                        transposes(t, cut(wide[:, t, :], 4))
                    for t in range(ET):
                        pe.wait_ge(E.T, g * (3 * ET) + (t + 1))
                        pe.nop(nofuse=True)
                        last = product(bank[6][:, t * F:(t + 1) * F], blocks(wideT[:, t]), blocks(m_fe2))
                    last.then_inc(E.fe2_ps, 1)
                    pe.wait_ge(E.uT, (g + 1) * 4)
                    pe.nop(nofuse=True)
                    for t in range(ET):
                        last = product(bank[0][:, t * F:(t + 1) * F], rows(uT, t), blocks(m_out))
                    last.then_inc(E.out_ps, 1)
                    pe.wait_ge(E.hatt, (g + 1) * 16)
                    pe.nop(nofuse=True)
                    pe.wait_ge(E.hs2, g + 1)
                    pe.nop(nofuse=True)
                    for t in range(ET):
                        transposes(t, cut(hatt[:, t, :], 2) + cut(hs2[:, t, :], 2))
                    for t in range(ET):
                        pe.wait_ge(E.T, g * (3 * ET) + (ET + t + 1))
                        pe.nop(nofuse=True)
                        product(bank[3 + t][:, :], blocks(wideT[:, t]), blocks(m_g1)).then_inc(E.wide_ps, 1)
                    for t in range(ET):
                        pe.wait_ge(E.silu, g * (2 * ET) + (ET + t + 1))
                        pe.nop(nofuse=True)
                        transposes(t, cut(wide[:, t, :], 4))
                    pe.wait_ge(E.henh, g + 1)
                    pe.nop(nofuse=True)
                    for t in range(ET):
                        pe.wait_ge(E.T, g * (3 * ET) + (2 * ET + t + 1))
                        pe.nop(nofuse=True)
                        last = product(bank[6][:, t * F:(t + 1) * F], blocks(wideT[:, t]), blocks(m_g2))
                    last.then_inc(E.g2_ps, 1)

            pe.wait_ge(s_const, 2)
            pe.wait_ge(s_x, 16)
            for i, signal in enumerate((s_unit, s_unit, s_packmm, s_packmm, s_xtps)):
                pe.transpose(bank[i][:, 0:P], ident[:, :], ident[:, :]).then_inc(signal, 1)
            for l in range(last_layer + 1):
                if l == 0:
                    pe.wait_ge(s_wfix, 1)
                    with pe.Fori(0, PAIRS) as tt:
                        dense(0, tt)
                        pack(tt)
                else:
                    if l == 3:
                        dense2()
                    pe.wait_ge(s_wfix, l + 1)
                    with pe.Fori(0, PAIRS) as tt:
                        dense(l, tt)
                if l < 3:
                    src_rows(l)
                attention(l)
            if last_layer == 2:
                dense2()

        @block.vector
        def _(dve):
            chain = Chain(s_dve)

            def fold_weights(l):
                dve.wait_ge(s_w, loaded_weights[l])
                for k in range(2):
                    for s in range(2):
                        if l < 3:
                            prod = tmpx[:, 0, s, :]
                            dve.tensor_tensor(prod, weights[:, k, 0:F], avec[:, s, :], ALU.mult).then_inc(s_dve, 1)
                            dve.wait_ge(s_dve, chain.next())
                            col = F + s * H
                            if l < 2:
                                dve.tensor_reduce(weights[:, k, col:col + H],
                                                  prod.rearrange("p (h d) -> p h d", h=H), AX.X, ALU.add)\
                                    .then_inc(s_dve, 1)
                                dve.wait_ge(s_dve, chain.next())
                            else:
                                for hd in range(H):
                                    dve.tensor_reduce(weights[:, k, col + hd:col + hd + 1], prod,
                                                      AX.X, ALU.add).then_inc(s_dve, 1)
                                    dve.wait_ge(s_dve, chain.next())
                chain.settle()
                dve.memset(credits[:, 8 + l:9 + l], 0.0).then_inc(s_wfix, 1)

            def pack(tt):
                for par in range(2):
                    t = tt * 2 + par
                    for half in range(2):
                        dve.wait_ge(s_adj[half], (t + 1) * 16)
                        dve.wait_ge(s_packmm, t * 2 + (half + 1))
                        dve.tensor_scalar(adj_bf[:, half, :], adj_in[:, half, :], 0, None, ALU.is_gt)\
                            .then_inc(s_adjbf, 1)
                    dve.wait_ge(s_packmm, t * 2 + (2 + CREDIT))
                    dve.tensor_copy(packed_bytes[:, :, ds(t * P, P)],
                                    bank[6 + par][:, :].rearrange("p (q n) -> p q n", q=Q)).then_inc(s_packed, 1)

            def norm(l, tt):
                xt = [x[:, ds(tt * 2 + par, 1), :] for par in range(2)]
                ht = [h[:, ds(tt * 2 + par, 1), :] for par in range(2)]
                low, ex = [[tmpx[:, par, i:i + 1, :] for par in range(2)] for i in range(2)]
                if l == 1:
                    for par in range(2):
                        dve.tensor_scalar(low[par], ht[par], 0.0, None, ALU.min).then_inc(s_elumin, 1)
                    for par in range(2):
                        dve.wait_ge(s_eluexp, tt * 2 + par + 1)
                        dve.tensor_tensor(low[par], ht[par], low[par], ALU.subtract).then_inc(s_dve, 1)
                        dve.wait_ge(s_dve, chain.next())
                        dve.scalar_tensor_tensor(out=ex[par], in0=ex[par], scalar=-1.0, in1=low[par],
                                                 op0=ALU.add, op1=ALU.add).then_inc(s_dve, 1)
                        dve.wait_ge(s_dve, chain.next())
                        dve.tensor_tensor(xt[par], xt[par], ex[par], ALU.add).then_inc(s_dve, 1)
                        dve.wait_ge(s_dve, chain.next())
                        dve.nop(nofuse=True)
                elif l in (2, 4):
                    for par in range(2):
                        dve.tensor_tensor(xt[par], xt[par], ht[par], ALU.add).then_inc(s_dve, 1)
                        dve.wait_ge(s_dve, chain.next())
                        dve.nop(nofuse=True)
                for par in range(2):
                    dve.bn_stats(lnst[:, par, 0:6], x[:, ds(tt * 2 + par, 1), :].squeeze(1)).then_inc(s_dve, 1)
                    dve.wait_ge(s_dve, chain.next())
                    dve.nop(nofuse=True)
                    dve.bn_aggr(lnst[:, par, 6:8], lnst[:, par, 0:6]).then_inc(s_var, 1)
                if l <= last_layer:
                    dve.wait_ge(s_xtps, tt * 2 + (l * T + 1))
                    dve.wait_ge(s_xkept, tt * 2 + ((l - 1) * T + 1))
                for par in range(2):
                    dve.wait_ge(s_rstd, tt * 2 + ((l - 1) * T + par + 1))
                    normed = xs[:, par:par + 1, :] if l <= last_layer else xt[par]
                    dve.tensor_scalar(normed, xt[par], lnst[:, par, 6:7], lnst[:, par, 9:10], ALU.subtract,
                                      ALU.mult).then_inc(s_xmade, 1)

            def tanh_scores(tt):
                for par in range(2):
                    t = tt * 2 + par
                    dve.wait_ge(s_h, t + (3 * T + 2))
                    dve.tensor_tensor(tmpx[:, par, 0:1, :], h[:, ds(t, 1), :], bvec[:, :].unsqueeze(1), ALU.add)\
                        .then_inc(s_tanhin, 1)
                for par in range(2):
                    t = tt * 2 + par
                    dve.wait_ge(s_tanh, t + 1)
                    dve.tensor_tensor(tmpx[:, par, 0, :], tmpx[:, par, 1, :], avec[:, 0, :], ALU.mult)\
                        .then_inc(s_dve, 1)
                    dve.wait_ge(s_dve, chain.next())
                    dve.tensor_reduce(scores[:, H, ds(t, 1)], tmpx[:, par, 0, :], AX.X, ALU.add).then_inc(s_dve, 1)
                    dve.wait_ge(s_dve, chain.next())

            def stats(l):
                n = H if l < 3 else 1
                if l < 3:
                    dve.wait_ge(s_h, T * (l + 1) + 1)
                src, dst = scores[:, 0:H, :], scores[:, H:H + n, :]
                dve.tensor_reduce(smax[:, 0, 0:n], dst, AX.X, ALU.max).then_inc(s_pmax, 1)
                dve.wait_ge(s_max, l + 1)
                top = smax[:, 1, 0:n].unsqueeze(2).to_broadcast([P, n, T])
                shifted = dve.tensor_tensor(emul[:, 0, 0:n, :], dst, top, ALU.subtract)
                if l == 3:
                    shifted.then_inc(s_shift, 1)
                    dve.tensor_scalar(zrow[:, 0, 0, :], scores[:, 0, :], 0.0, None, ALU.not_equal).then_inc(s_dve, 1)
                    dve.wait_ge(s_dve, chain.next())
                    dve.wait_ge(s_exps, 4)
                    for hd in range(1, H):
                        last = dve.tensor_tensor(emul[:, 0, hd, :], emul[:, 0, 0, :], zrow[:, 0, 0, :], ALU.mult)
                    last.then_inc(s_dve, 1)
                    dve.wait_ge(s_dve, chain.next())
                    dve.tensor_copy(emul[:, 0, 0, :], emul[:, 0, 1, :]).then_inc(s_emul, 1)
                    chain.settle()
                    return
                z, az, m = (zrow[:, i] for i in range(3))
                dve.tensor_tensor(z, src, top, ALU.add).then_inc(s_dve, 1)
                dve.wait_ge(s_dve, chain.next())
                dve.tensor_scalar(az, z, SLOPES[l], None, ALU.mult).then_inc(s_dve, 1)
                dve.wait_ge(s_dve, chain.next())
                dve.tensor_tensor(m, z, az, ALU.max).then_inc(s_dve, 1)
                dve.wait_ge(s_dve, chain.next())
                dve.tensor_tensor(cmul[:, 0], z, m, ALU.subtract)
                dve.tensor_tensor(cmul[:, 1], az, m, ALU.subtract)
                dve.tensor_scalar(kscores[:, :, :], dst, BIG, None, ALU.mult).then_inc(s_shift, 1)
                chain.settle()
                dve.wait_ge(s_exps, l + 1)
                with dve.Fori(0, FIRST_CHUNKS) as c:
                    chain.enter(c, VALUE_LINKS + 1)
                    value_parts(dve, chain, vtmp_dve, 1, c * CHUNK, CHUNK, 0, 0).then_inc(s_dve, 1)
                    dve.wait_ge(s_dve, chain.next())
                chain.leave(FIRST_CHUNKS)
                dve.memset(credits[:, 12 + l:13 + l], 0.0).then_inc(s_vfirst, 1)

            def evacuate(l, par, count):
                kinds = 2 if l < 3 else 1
                dve.wait_ge(s_unit, count * BITS + (l * H * UNITS + CREDIT))
                dve.wait_ge(s_quot, count + (l * H * NG + CREDIT - 1))
                for it in range(GT):
                    parts = bank[GT * par + it][:, 0:kinds * KW].rearrange("p (k a c) -> p k c a", k=kinds, a=PARTS)
                    last = dve.tensor_reduce(sums[:, par, it, 0:kinds, :], parts, AX.X, ALU.add)
                last.then_inc(s_sums, 1)

            def attention(l):
                per_group = 2 * BITS if l < 3 else 0
                with dve.Fori(0, H // 2) as pp:
                    for slot in range(2):
                        p = pp * 2 + slot
                        with dve.Fori(0, NG // 2) as gg:
                            for par in range(2):
                                g = p * NG + gg * 2 + par
                                chain.enter(g, per_group)
                                for k in range(BITS):
                                    unit = g * BITS + (l * H * UNITS + k)
                                    r = k % 2
                                    shift = (6 - k, ALU.logical_shift_left) if k <= 6 else (1, ALU.logical_shift_right)
                                    words = packed[:, :, ds(gg * (2 * WORDS) + par * WORDS, WORDS)]
                                    if l == 3:
                                        dve.wait_ge(s_unit, unit - 1 + CREDIT)
                                    edges = dve.tensor_scalar(edge[:, r], words, shift[0], ONE, shift[1],
                                                              ALU.bitwise_and)
                                    if l == 3:
                                        edges.then_inc(s_sides, 1)
                                    else:
                                        edges.then_inc(s_dve, 1)
                                        dve.wait_ge(s_dve, chain.next())
                                        dve.wait_ge(s_above, unit + 1)
                                        dve.wait_ge(s_unit, unit - 1 + CREDIT)
                                        dve.tensor_tensor(pos[:, r], edge[:, r],
                                                          above[:, r].bitcast(U32), ALU.bitwise_and).then_inc(s_dve, 1)
                                        dve.wait_ge(s_dve, chain.next())
                                        dve.tensor_tensor(neg[:, r], edge[:, r], pos[:, r], ALU.bitwise_xor)\
                                            .then_inc(s_sides, 1)
                                    if k == 1:
                                        evacuate(l, 1 - par, g)
                if per_group:
                    chain.leave(H * NG)
                evacuate(l, 1, H * NG)

            def dense2():
                dve.wait_ge(E.rows, 16 * (4 + len(row)))
                dve.tensor_tensor(row["b_bcdt"][:, 2 * SD:], row["b_bcdt"][:, 2 * SD:], row["A"], ALU.add)\
                    .then_inc(s_dve, 1)
                dve.wait_ge(s_dve, chain.next())
                dve.tensor_scalar(ecol[:, 24:25], c_cp, 1.0, None, ALU.add).then_inc(s_dve, 1)
                dve.wait_ge(s_dve, chain.next())
                dve.tensor_scalar(c_hz_half, c_hz[:, 4:8], 0.5, None, ALU.mult).then_inc(E.ready, 1)
                chain.settle()

                def both(name):
                    return row[name].unsqueeze(1).to_broadcast([P, ET, row_widths[name]])

                def stats(tile, st, signal):
                    n = tile.shape[-1]
                    dve.bn_stats(st[:, 0:6], tile).then_inc(s_dve, 1)
                    dve.wait_ge(s_dve, chain.next())
                    dve.nop(nofuse=True)
                    dve.bn_aggr(st[:, 6:8], st[:, 0:6]).then_inc(signal, 1)

                with dve.Fori(0, EG) as g:
                    chain.enter(g, 5 * ET + 2 * ET * 2 + 4 + 1 + ET)

                    def wide_in(n, bias):
                        for t in range(ET):
                            dve.wait_ge(E.wide_ps, g * (2 * ET) + (n * ET + t + 1))
                            dve.tensor_tensor(wide[:, t, :], bank[3 + t][:, :], row[bias], ALU.add).then_inc(s_dve, 1)
                            dve.wait_ge(s_dve, chain.next())
                            dve.nop(nofuse=True)
                            stats(wide[:, t, :], est[:, n, t, :], E.var)

                    def wide_norm(n):
                        for t in range(ET):
                            dve.wait_ge(E.rstd, g * (2 * ET) + (n * ET + t + 1))
                            dve.tensor_scalar(wide[:, t, :], wide[:, t, :], est[:, n, t, 6:7], est[:, n, t, 9:10],
                                              ALU.subtract, ALU.mult).then_inc(E.norm, 1)

                    def wide_silu(n):
                        for t in range(ET):
                            dve.wait_ge(E.tanh, g * (2 * ET) + (n * ET + t + 1))
                            dve.scalar_tensor_tensor(out=wide[:, t, :], in0=wide_tanh[:, t, :], scalar=1.0,
                                                     in1=wide[:, t, :], op0=ALU.add, op1=ALU.mult)\
                                .then_inc(E.silu, 1)

                    for t in range(ET):
                        dve.wait_ge(E.bc_ps, g * ET + t + 1)
                        dve.tensor_tensor(bcdt[:, t, :], bank[1 + t][:, 0:3 * SD], row["b_bcdt"], ALU.add)\
                            .then_inc(s_dve, 1)
                        dve.wait_ge(s_dve, chain.next())
                        dve.tensor_reduce(ecol[:, 16 + t:17 + t], bcdt[:, t, 2 * SD:3 * SD], AX.X, ALU.max,
                                          negate=True).then_inc(E.top, 1)
                    for t in range(ET):
                        dve.tensor_tensor(c_prod, bcdt[:, t, SD:2 * SD], row["cp_w"], ALU.mult).then_inc(s_dve, 1)
                        dve.wait_ge(s_dve, chain.next())
                        dve.tensor_reduce(ecol[:, 26 + t:27 + t], c_prod, AX.X, ALU.add).then_inc(s_dve, 1)
                        dve.wait_ge(s_dve, chain.next())
                        dve.tensor_tensor(ecol[:, 22 + t:23 + t], ecol[:, 26 + t:27 + t],
                                          ecol[:, 24:25], ALU.add).then_inc(s_dve, 1)
                        dve.wait_ge(s_dve, chain.next())
                    for t in range(ET):
                        dve.wait_ge(E.exp, g * ET + t + 1)
                        dve.reciprocal(ecol[:, 20 + t:21 + t], ecol[:, 18 + t:19 + t]).then_inc(s_dve, 1)
                        dve.wait_ge(s_dve, chain.next())
                        dve.scalar_tensor_tensor(out=ba[:, t, :], in0=dt_exp[:, t, :], scalar=ecol[:, 20 + t:21 + t],
                                                 in1=bcdt[:, t, 0:SD], op0=ALU.mult, op1=ALU.mult)\
                            .then_inc(E.ba, 1)
                    wide_in(0, "fe1_b")
                    dve.wait_ge(E.ab_ps, g + 1)
                    for b in range(2):
                        last = dve.scalar_tensor_tensor(out=hsT[:, b, :], in0=bank[6][:, b * EI:(b + 1) * EI],
                                                        scalar=c_abp[:, b:b + 1], in1=whT[:, b, :],
                                                        op0=ALU.add, op1=ALU.mult)
                    last.then_inc(E.hsT, 1)
                    wide_norm(0)
                    for b in range(4):
                        dve.wait_ge(E.z_sig, g * 4 + b + 1)
                        dve.scalar_tensor_tensor(
                 out=z_sig[:, b % 2, :], in0=bank[1 + b % 2][:, EI:2 * EI], scalar=c_hz[:, 4 + b:5 + b],
                 in1=z_sig[:, b % 2, :], op0=ALU.add, op1=ALU.mult).then_inc(s_dve, 1)
                        dve.wait_ge(s_dve, chain.next())
                        dve.scalar_tensor_tensor(out=uT[:, b, :], in0=z_sig[:, b % 2, :], scalar=c_d,
                                                 in1=h_part[:, b % 2, :], op0=ALU.add, op1=ALU.mult)\
                            .then_inc(E.uT, 1)
                        if b == 1:
                            wide_silu(0)
                    dve.wait_ge(E.fe2_ps, g + 1)
                    dve.tensor_tensor(henh, bank[6][:, :].rearrange("p (t f) -> p t f", t=ET), both("fe2_b"), ALU.add)\
                        .then_inc(E.henh, 1)
                    dve.wait_ge(E.out_ps, g + 1)
                    dve.tensor_tensor(hs2, bank[0][:, :].rearrange("p (t f) -> p t f", t=ET),
                                      both("out_b"), ALU.add).then_inc(s_dve, 1)
                    dve.wait_ge(s_dve, chain.next())
                    for t in range(ET):
                        last = dve.tensor_scalar(hs2[:, t, :], hs2[:, t, :], ecol[:, 22 + t:23 + t], None, ALU.mult)
                    last.then_inc(E.hs2, 1)
                    wide_in(1, "g1_b")
                    wide_norm(1)
                    wide_silu(1)
                    dve.wait_ge(E.g2_ps, g + 1)
                    dve.tensor_tensor(gate, bank[6][:, :].rearrange("p (t f) -> p t f", t=ET), both("g2_b"), ALU.add)\
                        .then_inc(E.gate_in, 1)
                    dve.wait_ge(E.fused, g + 1)
                    dve.nop(nofuse=True)
                    for t in range(ET):
                        stats(fused[:, t, :], est[:, 2, t, :], E.fvar)
                    for t in range(ET):
                        dve.wait_ge(E.frstd, g * ET + (t + 1))
                        dve.tensor_scalar(fused[:, t, :], fused[:, t, :], est[:, 2, t, 6:7], est[:, 2, t, 9:10],
                                          ALU.subtract, ALU.mult).then_inc(E.fnorm, 1)
                chain.leave(EG)
                dve.wait_ge(E.x, T)

            for i, signal in enumerate((s_sides, s_sides, s_h, s_packed, s_sums)):
                dve.memset(credits[:, 3 + i:4 + i], 0.0).then_inc(signal, 1)
            for it in range(GT):
                last = dve.memset(bank[GT + it][:, :], 0.0)
            last.then_inc(s_const, 1)
            for l in range(last_layer + 1):
                if l == 3:
                    dense2()
                fold_weights(l)
                if l == 0:
                    with dve.Fori(0, PAIRS) as tt:
                        pack(tt)
                else:
                    dve.wait_ge(s_quot, l * H * NG + CREDIT)
                    with dve.Fori(0, PAIRS) as tt:
                        chain.enter(tt, NORM_LINKS[l] + (4 if l == 3 else 0))
                        norm(l, tt)
                        if l == 3:
                            tanh_scores(tt)
                    chain.leave(PAIRS)
                stats(l)
                attention(l)
            if last_layer == 2:
                dense2()
            dve.wait_ge(s_quot, (last_layer + 1) * H * NG + CREDIT)
            with dve.Fori(0, PAIRS) as tt:
                chain.enter(tt, NORM_LINKS[last_layer + 1])
                norm(last_layer + 1, tt)
            chain.leave(PAIRS)


def kernel(**inputs):
    import numpy as _np
    import concourse.bacc as _bacc
    from concourse import mybir as _mybir
    from concourse.bass_utils import run_bass_kernel_spmd as _run

    nc = _bacc.Bacc("TRN2", target_bir_lowering=False, num_devices=1)
    arrays, args = {}, {}
    for name, a in inputs.items():
        a = _np.ascontiguousarray(a)
        arrays[f"in_{name}_dram"] = a
        args[name] = nc.dram_tensor(f"in_{name}_dram", a.shape, _mybir.dt.from_np(a.dtype),
                                    kind="ExternalInput").ap()
    out = nc.dram_tensor("out_0_dram", (N, F), F32, kind="ExternalOutput").ap()
    gnn_kernel(nc, args, out)
    r = _run(nc, [arrays], core_ids=[0])
    return r.results[0]["out_0_dram"]
```

```python
from contextlib import ExitStack

import concourse.bass as bass
from concourse import mybir

ds = bass.ds
ALU = mybir.AluOpType
ACT = mybir.ActivationFunctionType
AX = mybir.AxisListType
RMAX = bass.bass_isa.ReduceOp.max
F32 = mybir.dt.float32
BF16 = mybir.dt.bfloat16
FP8 = mybir.dt.float8e4
U8 = mybir.dt.uint8
U32 = mybir.dt.uint32
I32 = mybir.dt.int32

P = 128
N = 4096
F = 256
T = N // P
QT = 4
QUADS = T // QT
H = 4
D = F // H
C = D + 1
PARTS = 3
KW = PARTS * C
GT = 4
GI = GT * P
NG = N // GI
BITS = 8
Q = T // BITS
WORDS = GI // 4
ONE = 0x40404040
BIG = 2.0 ** 60
SLOPES = (0.01, 0.2, 0.2)
EPS = 1e-5
CHUNK = 8
FIRST_CHUNKS = T // CHUNK
CHUNKS = FIRST_CHUNKS + H * NG
UNITS = NG * BITS
DI = 512
SD = 128
ET = 2
EI = ET * P
EG = T // ET
CREDIT = 2


NORM_LINKS = {1: 4, 2: 2, 3: 1, 4: 2}


class Chain:

    def __init__(self, sem):
        self.sem, self.start, self.local, self.base = sem, 0, 0, 0

    def enter(self, i, per):
        self.base, self.per, self.local = self.start + i * per, per, 0

    def settle(self):
        self.start += self.local
        self.base, self.local = self.start, 0

    def leave(self, trips):
        assert self.local == self.per, (self.local, self.per)
        self.start += trips * self.per
        self.base, self.local = self.start, 0

    def next(self):
        self.local += 1
        return self.base + self.local


def gnn_kernel(nc, A, out, last_layer=3):
    with ExitStack() as ctx:
        def sb(name, shape, dt=F32):
            return ctx.enter_context(nc.sbuf_tensor(name, shape, dt))

        def sem(name):
            return ctx.enter_context(nc.semaphore(name))

        packed = sb("packed", [P, Q, N // 4], U32)
        x = sb("x", [P, T, F])
        h = sb("h", [P, T, F])
        values = sb("values", [P, 2, T, 2 * KW], BF16)
        above = sb("above", [P, 2, Q, GI], FP8)
        rings = sb("rings", [P, CHUNK * 2 * C + 2 * (2 * Q * WORDS)], U32)
        ring = rings[:, CHUNK * 2 * C:].rearrange("p (o s q w) -> p o s q w", o=2, s=2, q=Q)
        edge = rings[:, 0:2 * Q * WORDS].rearrange("p (s q w) -> p s q w", s=2, q=Q)
        pos = ring[:, 0]
        neg = ring[:, 1]
        srow = sb("srow", [P, 2, GI])
        arena = sb("arena", [P, T * F])
        weights = sb("weights", [P, 2, F + 2 * H])
        avec = sb("avec", [P, 2, F])
        bvec = sb("bvec", [P, F])
        scores = sb("scores", [P, 2 * H, T])
        kscores = sb("kscores", [P, H, T])
        kpass = sb("kpass", [P, 2, T])
        emul = sb("emul", [P, 2, H, T])
        cmul = sb("cmul", [P, 2, H, T])
        zrow = sb("zrow", [P, 3, H, T])
        smax = sb("smax", [P, 2, H])
        srcT = sb("srcT", [P, P])
        sums = sb("sums", [P, 2, GT, 2, C])
        quot = sb("quot", [P, 3, GT, C])
        vtmp_pool = sb("vtmp_pool", [P, 2, CHUNK, C])
        vtmp_dve = rings[:, 0:CHUNK * 2 * C].bitcast(F32).rearrange("p (a n c) -> p a n c", a=2, c=C)
        prod = neg[:, :].rearrange("p s q w -> p (s q w)").bitcast(F32)[:, 0:2 * F].rearrange("p (s f) -> p s f", s=2)
        lnst = sb("lnst", [P, QT, 16])
        exponents = sb("exponents", [P, 1 + GT])
        minus_half, minus_one = exponents[:, 0:1], exponents[:, 1:1 + GT].unsqueeze(2)
        credits = sb("credits", [P, 16])
        ident = sb("ident", [P, P])
        powers = sb("powers", [P, BITS, P], BF16)

        adj_in = arena[:, 0:4096].bitcast(I32).rearrange("p (s n) -> p s n", s=2)
        adj_bf = arena[:, 4096:6144].bitcast(BF16).rearrange("p (s n) -> p s n", s=2)
        attn2 = arena[:, :].rearrange("p (t f) -> p t f", f=F)
        packed_bytes = packed[:, :, :].bitcast(U8)

        vroom = values[:, :, :, :].rearrange("p s t c -> p (s t c)").bitcast(F32)
        rroom = rings[:, :].bitcast(F32)
        aroom = above[:, :, :, :].rearrange("p s q n -> p (s q n)").bitcast(F32)
        sroom = srow[:, :, :].rearrange("p s n -> p (s n)")
        tiles_room = vroom[:, T * KW:]
        low, ex, xs, xT = (tiles_room[:, i * QT * F:(i + 1) * QT * F] for i in range(4))
        low, ex, xs = (m.rearrange("p (t f) -> p t f", t=QT) for m in (low, ex, xs))
        xT = xT.rearrange("p (t k n) -> p t k n", t=QT, k=2)
        proom = vtmp_pool[:, :, :, :].rearrange("p a n c -> p (a n c)")

        class Room:

            def __init__(self, view):
                self.view, self.at = view, 0

            def take(self, *shape):
                n = 1
                for d in shape:
                    n *= d
                piece = self.view[:, self.at:self.at + n]
                self.at += n
                assert self.at <= self.view.shape[1]
                names = "abc"[:len(shape)]
                if len(shape) == 1:
                    return piece
                return piece.rearrange(f"p ({' '.join(names)}) -> p {' '.join(names)}", **dict(zip(names, shape)))

        room = Room(vroom)
        m_fe1, m_fe2 = room.take(2, DI), room.take(4, F)
        m_bcdt, m_abp = room.take(2, 3 * SD), room.take(F)
        m_hz, m_out = room.take(2, 2 * DI), room.take(4, F)
        m_g1, m_g2 = room.take(4, DI), room.take(4, F)
        wide, wide_tanh, wideT = room.take(ET, DI), room.take(ET, DI), room.take(ET, 4, P)
        room = Room(arena[:, :])
        row_widths = {"b_bcdt": 3 * SD, "cp_w": SD, "out_b": F, "fe1_b": DI, "fe_ln_g": DI, "fe_ln_b": DI,
                      "fe2_b": F, "g1_b": DI, "g_ln_g": DI, "g_ln_b": DI, "g2_b": F, "ln_g": F, "ln_b": F,
                      "A": SD}
        row = {name: room.take(w) for name, w in row_widths.items()}
        hatt, hs2, henh, gate, fused = (room.take(ET, F) for _ in range(5))
        whs = room.take(ET, F)
        room = Room(rroom)
        whT, hsT, uT = room.take(2, EI), room.take(2, EI), room.take(4, EI)
        bcdt, baT = room.take(ET, 3 * SD), room.take(EI)
        room = Room(aroom)
        z_tanh, h_part = room.take(2, EI), room.take(2, EI)
        room = Room(sroom)
        z_part, dt_exp = room.take(2, EI), room.take(ET, SD)
        room = Room(proom)
        ba, c_prod, est, base = room.take(ET, SD), room.take(SD), room.take(3, ET, 16), room.take(ET, F)
        wide_g = Room(sums[:, :, :, :, :].rearrange("p a t k c -> p (a t k c)")).take(ET, DI)
        wide_g_tanh = [powers[:, :, :].bitcast(F32).rearrange("p k n -> p (k n)")[:, 0:DI],
                       quot[:, :, :, :].rearrange("p a t c -> p (a t c)")[:, 0:DI]]
        ecol = sb("ecol", [P, 32])
        c_abp, c_hz, c_hz_half = ecol[:, 0:2], ecol[:, 2:10], ecol[:, 10:14]
        c_d, c_cp, top_dt, sum_dt, inv_dt, one_c = (ecol[:, i:i + 1] for i in (14, 15, 16, 18, 20, 22))
        c_d_twice = ecol[:, 28:29]
        attn_dram = nc.dram_tensor("attn_dram", [N, F], F32)[:, :]

        bank = [ctx.enter_context(nc.psum_tensor(f"bank{i}", [P, 512], F32)) for i in range(8)]

        src_dram = [nc.dram_tensor(f"src_dram{l}", [H * T, P], F32)[:, :] for l in range(3)]

        s_x = sem("x_loaded")
        s_w = sem("weights_loaded")
        s_wfix = sem("weights_fixed")
        s_adj = [sem("adj_loaded0"), sem("adj_loaded1")]
        s_adjbf = sem("adj_is_bf16")
        s_packmm = sem("pack_matmul")
        s_packed = sem("packed_stored")
        s_const = sem("constants_made")
        s_dve = sem("dve_chain")
        s_pool = sem("pool_chain")
        s_elumin = sem("elu_min")
        s_eluexp = sem("elu_exp")
        s_var = sem("variance_made")
        s_rstd = sem("rstd_made")
        s_xmade = sem("x_made")
        s_xkept = sem("x_kept")
        s_xtps = sem("xt_in_psum")
        s_xt = sem("xt_made")
        s_hps = sem("h_in_psum")
        s_h = sem("h_made")
        s_tanhin = sem("tanh_in_made")
        s_tanh = sem("tanh_made")
        s_srcps = sem("src_in_psum")
        s_src = sem("src_transposed")
        s_srcst = sem("src_stored")
        s_pmax = sem("partition_max")
        s_max = sem("max_made")
        s_shift = sem("shifts_made")
        s_exps = sem("exps_made")
        s_emul = sem("layer3_weights_made")
        s_vfirst = sem("dve_values_made")
        s_vals = sem("values_made")
        s_srow = [sem("srow_loaded0"), sem("srow_loaded1")]
        s_above = sem("above_made")
        s_sides = sem("sides_made")
        s_unit = sem("unit_multiplied")
        s_sums = sem("sums_made")
        s_quot = sem("quotients_made")
        s_out = sem("out_stored")

        s_kpass = sem("pass_scores_made")


        class E:
            pass
        E.weights, E.rows, E.stored = sem("e_weights_loaded"), sem("e_rows_loaded"), sem("e_attention_stored")
        E.hatt, E.whs, E.ready = sem("e_attention_loaded"), sem("e_wh_staged"), sem("e_constants_ready")
        E.whT_ps, E.whT = sem("e_whT_in_psum"), sem("e_whT_made")
        E.bc_ps, E.top, E.exp, E.ba = (sem(n) for n in ("e_bcdt_in_psum", "e_dt_max", "e_dt_exp", "e_ba_made"))
        E.baT_ps, E.baT, E.ab_ps, E.hsT = (sem(n) for n in ("e_baT_in_psum", "e_baT_made", "e_abT_in_psum",
                                                            "e_hsT_made"))
        E.hz_ps, E.z_tanh, E.uT = (sem(n) for n in ("e_hz_in_psum", "e_z_tanh", "e_uT_made"))
        E.out_ps, E.hs2, E.parts = sem("e_out_in_psum"), sem("e_hs2_made"), sem("e_parts_made")

        def wide_count(i, old):
            return i * (2 * ET) - (ET if old else 0)

        def T_count(i, n):
            return i * (3 * ET) - (2 - n) * ET

        E.wide_ps, E.var, E.rstd, E.norm = (sem(n) for n in ("e_wide_in_psum", "e_wide_var", "e_wide_rstd",
                                                             "e_wide_normed"))
        E.lin, E.tanh, E.silu = (sem(n) for n in ("e_wide_scaled", "e_wide_tanh", "e_wide_silu"))
        E.T_ps, E.T = sem("e_wideT_in_psum"), sem("e_wideT_made")
        E.fe2_ps, E.henh, E.g2_ps, E.gate_in, E.gate = (sem(n) for n in (
            "e_fe2_in_psum", "e_henh_made", "e_g2_in_psum", "e_gate_in", "e_gate_tanh"))
        E.fused, E.fvar, E.frstd, E.fnorm, E.x = (sem(n) for n in (
            "e_fused", "e_fused_var", "e_fused_rstd", "e_fused_normed", "e_x_made"))

        block = ctx.enter_context(nc.Block())
        SUMS = NG * H + 1

        @block.sync
        def _(sp):
            def load_vector(dst, src):
                sp.dma_start(dst, src.partition_broadcast(P)).then_inc(s_w, 16)

            def load_weights(l):
                if l == 0:
                    for k in range(2):
                        sp.dma_start(weights[:, k, 0:F].rearrange("p (h d) -> p h d", h=H),
                                     A["L0_gnn_W"][:, k * P:(k + 1) * P, :].rearrange("h p d -> p h d"))\
                            .then_inc(s_w, 16)
                    for s in range(2):
                        for hd in range(H):
                            load_vector(avec[:, s, hd * D:(hd + 1) * D], A["L0_gnn_a"][hd, s * D:(s + 1) * D, 0])
                    return
                sp.dma_start(weights[:, :, 0:F], A[f"L{l}_gnn_W"].rearrange("(k p) f -> p k f", p=P))\
                    .then_inc(s_w, 16)
                if l == 1:
                    for s, name in enumerate(("L1_gnn_a1", "L1_gnn_a2")):
                        for hd in range(H):
                            load_vector(avec[:, s, hd * D:(hd + 1) * D], A[name])
                elif l == 2:
                    load_vector(avec[:, 0, :], A["L2_gnn_a_src"][:, 0])
                    load_vector(avec[:, 1, :], A["L2_gnn_a_dst"][:, 0])
                else:
                    load_vector(avec[:, 0, :], A["L3_gnn_a"][:, 0])
                    load_vector(bvec[:, :], A["L3_gnn_b"])

            def score_rows(l):
                sp.wait_ge(s_src, l + 1)
                sp.dma_start(src_dram[l], srcT[:, :]).then_inc(s_srcst, 16)
                sp.wait_ge(s_srcst, 16 * (l + 1))
                flat = src_dram[l].rearrange("a b -> (a b)")

                def load(slot, grp):
                    sp.dma_start(srow[:, slot, :], flat[ds(grp * GI, GI)].partition_broadcast(P))\
                        .then_inc(s_srow[slot], 16)

                first = 0
                if l == 0:
                    load(0, 0)
                    load(1, 1)
                    first = 1
                with sp.Fori(first, H * NG // 2) as gg:
                    for slot in range(2):
                        sp.wait_ge(s_above, (gg * 2 + (l * H * NG + slot - 1)) * BITS)
                        load(slot, gg * 2 + slot)

            def dense2():
                sp.wait_ge(s_quot, 3 * H * NG + CREDIT)
                sp.dma_start(attn_dram.rearrange("(t p) f -> p t f", p=P), attn2).then_inc(E.stored, 16)
                sp.wait_ge(s_vals, 3 * CHUNKS)
                sp.wait_ge(s_unit, 3 * H * UNITS + CREDIT)
                for name, m in (("W_bcdt", m_bcdt), ("fe1_w", m_fe1), ("W_hz", m_hz), ("fe2_w", m_fe2),
                                ("out_w", m_out), ("g1_w", m_g1), ("g2_w", m_g2)):
                    sp.dma_start(m, A[f"L2_gnn_{name}"].rearrange("(k p) f -> p k f", p=P)).then_inc(E.weights, 16)
                sp.dma_start(m_abp, A["L2_gnn_abp_w"]).then_inc(E.weights, 16)
                for name, c in (("abp_b", c_abp), ("b_hz", c_hz)):
                    sp.dma_start(c, A[f"L2_gnn_{name}"].rearrange("(c p) -> p c", p=P),
                                 allow_slow_non_contiguous=True).then_inc(E.rows, 16)
                for name, c in (("D", c_d), ("cp_b", c_cp)):
                    sp.dma_start(c, A[f"L2_gnn_{name}"].partition_broadcast(P)).then_inc(E.rows, 16)
                sp.wait_ge(E.stored, 16)
                for name, r in row.items():
                    src = A[f"L2_gnn_{name}"]
                    src = src[:, 0] if name == "cp_w" else src
                    sp.dma_start(r, src.partition_broadcast(P)).then_inc(E.rows, 16)

                def load_attention(g):
                    sp.dma_start(hatt, attn_dram[ds(g * EI, EI), :].rearrange("(t p) f -> p t f", p=P))\
                        .then_inc(E.hatt, 16)

                load_attention(0)
                with sp.Fori(1, EG) as g:
                    sp.wait_ge(E.T_ps, g * (3 * ET) - 2 * ET + ET)
                    sp.wait_ge(E.parts, g)
                    load_attention(g)

            sp.dma_start(x[:, :, :], A["x"].rearrange("(t p) f -> p t f", p=P)).then_inc(s_x, 16)
            load_weights(0)
            for half in range(2):
                sp.dma_start(adj_in[:, half, :], A["adj"][0:P, half * 2048:(half + 1) * 2048])\
                    .then_inc(s_adj[half], 16)
            with sp.Fori(1, T) as t:
                for half in range(2):
                    sp.wait_ge(s_adjbf, t * 2 + (half - 1))
                    sp.dma_start(adj_in[:, half, :], A["adj"][ds(t * P, P), half * 2048:(half + 1) * 2048])\
                        .then_inc(s_adj[half], 16)
            for l in range(4):
                if l < 3:
                    score_rows(l)
                if l < min(3, last_layer):
                    sp.wait_ge(s_h, T * (l + 1) + 1)
                    load_weights(l + 1)
                if l == 2:
                    dense2()
                if l == last_layer:
                    break
            with sp.Fori(0, QUADS) as q:
                sp.wait_ge(s_xmade, q * QT + (T * (last_layer + 1) + QT))
                sp.dma_start(out[ds(q * (QT * P), QT * P), :].rearrange("(t p) f -> p t f", p=P),
                             x[:, ds(q * QT, QT), :]).then_inc(s_out, 16)
            sp.wait_ge(s_out, 16 * QUADS)

        loaded_weights = [16 * 10, 16 * 19, 16 * 22, 16 * 25]

        def value_parts(eng, chain, vtmp, kind, j0, n, p, slot):
            big, rest = vtmp[:, 0, 0:n, :], vtmp[:, 1, 0:n, :]
            e = emul[:, kind, ds(p, 1), ds(j0, n)].rearrange("p a n -> p n a")
            part = [values[:, slot, ds(j0, n), kind * KW + i * C:kind * KW + (i + 1) * C] for i in range(PARTS)]
            eng.tensor_copy(big[:, :, D:C], e)
            eng.tensor_tensor(big[:, :, 0:D], h[:, ds(j0, n), ds(p * D, D)],
                              e.to_broadcast([P, n, D]), ALU.mult).then_inc(chain.sem, 1)
            eng.wait_ge(chain.sem, chain.next())
            eng.nop(nofuse=True)
            eng.tensor_copy(part[0], big).then_inc(chain.sem, 1)
            eng.wait_ge(chain.sem, chain.next())
            eng.nop(nofuse=True)
            eng.tensor_tensor(rest, big, part[0], ALU.subtract).then_inc(chain.sem, 1)
            eng.wait_ge(chain.sem, chain.next())
            eng.nop(nofuse=True)
            eng.tensor_copy(part[1], rest).then_inc(chain.sem, 1)
            eng.wait_ge(chain.sem, chain.next())
            eng.nop(nofuse=True)
            return eng.tensor_tensor(part[2], rest, part[1], ALU.subtract)

        VALUE_LINKS = 4

        @block.gpsimd
        def _(pool):
            chain = Chain(s_pool)
            pool.memset(exponents[:, 1:1 + GT], -1.0)
            for i, signal in enumerate((s_quot, s_quot)):
                pool.memset(credits[:, i:i + 1], 0.0).then_inc(signal, 1)
            pool.memset(ident[:, :], 0.0).then_inc(s_pool, 1)
            pool.wait_ge(s_pool, chain.next())
            pool.affine_select(out=ident[:, :], in_=ident[:, :], compare_op=ALU.not_equal, fill=1.0,
                               base=0, pattern=[[-1, P]], channel_multiplier=1).then_inc(s_pool, 1)
            pool.wait_ge(s_pool, chain.next())
            pool.memset(minus_half, -0.5).then_inc(s_pool, 1)
            pool.wait_ge(s_pool, chain.next())
            for k in range(BITS):
                last = pool.tensor_scalar(powers[:, k, :], ident[:, :], float(2 ** k), None, ALU.mult)
            last.then_inc(s_const, 1)
            chain.settle()

            def rstd_of_quads(l):
                def make_rstd(q):
                    pool.wait_ge(s_var, q + ((l - 1) * QUADS + 1))
                    pool.nop(nofuse=True)
                    pool.tensor_scalar(lnst[:, :, 8:9], lnst[:, :, 7:8], EPS, None, ALU.add).then_inc(s_pool, 1)
                    pool.wait_ge(s_pool, chain.next())
                    pool.tensor_tensor(lnst[:, :, 9:10], lnst[:, :, 8:9],
                                       minus_half.unsqueeze(2).to_broadcast([P, QT, 1]), ALU.pow)\
                        .then_inc(s_rstd, 1)

                def keep(q):
                    if l <= last_layer:
                        pool.wait_ge(s_xmade, q * QT + (l * T + QT))
                        pool.nop(nofuse=True)
                        pool.tensor_copy(x[:, ds(q * QT, QT), :], xs).then_inc(s_xkept, 1)

                make_rstd(0)
                chain.settle()
                with pool.Fori(1, QUADS) as q:
                    chain.enter(q - 1, 1)
                    keep(q - 1)
                    make_rstd(q)
                chain.leave(QUADS - 1)
                keep(QUADS - 1)

            def stage_x():
                pool.wait_ge(s_x, 16)
                with pool.Fori(0, QUADS) as q:
                    pool.wait_ge(s_xtps, q * 2 + 1)
                    pool.nop(nofuse=True)
                    pool.tensor_copy(xs, x[:, ds(q * QT, QT), :]).then_inc(s_xmade, QT)

            def global_max(l):
                n = H if l < 3 else 1
                pool.wait_ge(s_pmax, l + 1)
                pool.partition_all_reduce(smax[:, 1, 0:n], smax[:, 0, 0:n], P, RMAX).then_inc(s_max, 1)

            def first_values(l):
                if l < 3:
                    pool.wait_ge(s_exps, l + 1)
                else:
                    pool.wait_ge(s_emul, 1)
                with pool.Fori(0, FIRST_CHUNKS) as c:
                    chain.enter(c, VALUE_LINKS)
                    value_parts(pool, chain, vtmp_pool, 0, c * CHUNK, CHUNK, 0, 0).then_inc(s_vals, 1)
                chain.leave(FIRST_CHUNKS)

            def attention(l):
                kinds = 2 if l < 3 else 1
                per_group = VALUE_LINKS * kinds + (3 if l < 3 else 2)
                target = attn2 if l == 2 else h
                with pool.Fori(0, H // 2) as pp:
                    for slot in range(2):
                        p = pp * 2 + slot
                        nxt = p + 1 if slot == 0 else (2 - pp * 2)
                        pool.wait_ge(s_unit, p * UNITS + (CREDIT + l * H * UNITS))
                        pool.nop(nofuse=True)
                        with pool.Fori(0, NG // 2) as gg:
                            for par in range(2):
                                g = gg * 2 + par
                                chain.enter(p * NG + g, per_group)
                                for kind in range(kinds):
                                    made = value_parts(pool, chain, vtmp_pool, kind, g * GT, GT, nxt, 1 - slot)
                                made.then_inc(s_vals, 1)
                                pool.wait_ge(s_sums, p * NG + g + (l * SUMS + 3))
                                pool.nop(nofuse=True)
                                dst = target[:, ds(g * GT, GT), ds(p * D, D)]
                                if l < 3:
                                    c = [cmul[:, s, ds(p, 1), ds(g * GT, GT)].rearrange("p a n -> p n a")
                                         .to_broadcast([P, GT, C]) for s in range(2)]
                                    pool.tensor_tensor(quot[:, 0], sums[:, par, :, 0, :], c[0], ALU.mult)
                                    pool.tensor_tensor(quot[:, 1], sums[:, par, :, 1, :], c[1], ALU.mult)\
                                        .then_inc(s_pool, 1)
                                    pool.wait_ge(s_pool, chain.next())
                                    pool.nop(nofuse=True)
                                    pool.tensor_tensor(quot[:, 2], quot[:, 0], quot[:, 1], ALU.add).then_inc(s_pool, 1)
                                    pool.wait_ge(s_pool, chain.next())
                                    pool.nop(nofuse=True)
                                    total, inverse = quot[:, 2], quot[:, 0, :, 0:1]
                                    pool.tensor_tensor(inverse, total[:, :, D:C], minus_one, ALU.pow)\
                                        .then_inc(s_pool, 1)
                                    pool.wait_ge(s_pool, chain.next())
                                    pool.nop(nofuse=True)
                                else:
                                    total, inverse = sums[:, par, :, 0, :], quot[:, 1, :, 0:1]
                                    pool.tensor_scalar(quot[:, 0, :, 0:1], total[:, :, D:C],
                                                       2e-38, None, ALU.max).then_inc(s_pool, 1)
                                    pool.wait_ge(s_pool, chain.next())
                                    pool.nop(nofuse=True)
                                    pool.tensor_tensor(inverse, quot[:, 0, :, 0:1], minus_one, ALU.pow)\
                                        .then_inc(s_pool, 1)
                                    pool.wait_ge(s_pool, chain.next())
                                    pool.nop(nofuse=True)
                                done = pool.tensor_tensor(dst, total[:, :, 0:D],
                                                          inverse.to_broadcast([P, GT, D]), ALU.mult)
                                done.then_inc(s_quot, 1)
                chain.leave(H * NG)

            def rstd(stats, waits, at, signal):
                pool.wait_ge(waits, at)
                pool.nop(nofuse=True)
                pool.tensor_scalar(stats[:, 8:9], stats[:, 7:8], EPS, None, ALU.add).then_inc(s_pool, 1)
                pool.wait_ge(s_pool, chain.next())
                pool.nop(nofuse=True)
                pool.tensor_tensor(stats[:, 9:10], stats[:, 8:9], minus_half, ALU.pow).then_inc(signal, 1)

            def dense2():
                pool.wait_ge(E.stored, 16)
                pool.wait_ge(E.rows, 16 * (4 + len(row)))

                def scale_wide(at, tiles, gain, shift):
                    for t in range(ET):
                        pool.wait_ge(E.norm, at + (t + 1))
                        pool.tensor_tensor(tiles[:, t, :], tiles[:, t, :], row[gain], ALU.mult).then_inc(s_pool, 1)
                        pool.wait_ge(s_pool, chain.next())
                        pool.tensor_tensor(tiles[:, t, :], tiles[:, t, :], row[shift], ALU.add).then_inc(E.lin, 1)

                def step(i, new, old):
                    if old:
                        for t in range(ET):
                            rstd(est[:, 1, t, :], E.var, wide_count(i, 1) + (t + 1), E.rstd)
                        scale_wide(wide_count(i, 1), wide_g, "g_ln_g", "g_ln_b")
                    if new:
                        for t in range(ET):
                            rstd(est[:, 0, t, :], E.var, wide_count(i, 0) + (t + 1), E.rstd)
                        scale_wide(wide_count(i, 0), wide, "fe_ln_g", "fe_ln_b")
                    if old:
                        pool.wait_ge(E.hatt, i * 16)
                        pool.wait_ge(E.henh, i)
                        pool.tensor_tensor(fused, hatt, hs2, ALU.subtract)
                        pool.tensor_tensor(base, henh, hs2, ALU.add).then_inc(E.parts, 1)
                        pool.wait_ge(E.gate, i)
                        pool.nop(nofuse=True)
                        pool.tensor_scalar(gate, gate, 0.5, 0.5, ALU.mult, ALU.add).then_inc(s_pool, 1)
                        pool.wait_ge(s_pool, chain.next())
                        pool.tensor_tensor(fused, fused, gate, ALU.mult).then_inc(s_pool, 1)
                        pool.wait_ge(s_pool, chain.next())
                        pool.tensor_tensor(fused, fused, base, ALU.add).then_inc(E.fused, 1)
                        for t in range(ET):
                            rstd(est[:, 2, t, :], E.fvar, (i - 1) * ET + (t + 1), E.frstd)
                        for t in range(ET):
                            pool.wait_ge(E.fnorm, (i - 1) * ET + (t + 1))
                            pool.tensor_tensor(fused[:, t, :], fused[:, t, :], row["ln_g"], ALU.mult)\
                                .then_inc(s_pool, 1)
                            pool.wait_ge(s_pool, chain.next())
                            pool.tensor_tensor(fused[:, t, :], fused[:, t, :], row["ln_b"], ALU.add)\
                                .then_inc(s_pool, 1)
                            xt = x[:, ds((i - 1) * ET + t, 1), :]
                            pool.wait_ge(s_pool, chain.next())
                            pool.nop(nofuse=True)
                            pool.tensor_tensor(xt, xt, fused[:, t:t + 1, :], ALU.add).then_inc(E.x, 1)

                step(0, True, False)
                chain.settle()
                with pool.Fori(1, EG) as i:
                    chain.enter(i - 1, 2 * ET + 2 * ET + 2 + 3 * ET)
                    step(i, True, True)
                chain.leave(EG - 1)
                step(EG, False, True)
                chain.settle()

            for l in range(last_layer + 1):
                if l == 3:
                    dense2()
                if l > 0:
                    rstd_of_quads(l)
                else:
                    stage_x()
                global_max(l)
                first_values(l)
                attention(l)
            if last_layer == 2:
                dense2()
            rstd_of_quads(last_layer + 1)

        @block.scalar
        def _(act):
            def dense(l, q):
                for half in range(2):
                    act.wait_ge(s_xtps, q * 2 + (l * 2 * QUADS + half + 2))
                    act.activation(xT[:, 2 * half:2 * half + 2].rearrange("p t k n -> p (t k n)"), bank[half][:, :],
                                   ACT.Copy).then_inc(s_xt, 1)
                for i in range(QT):
                    act.wait_ge(s_hps, q * QT + (l * T + i + 1))
                    to_h = act.activation(h[:, ds(q * QT + i, 1), :], bank[2 + i][:, 0:F].unsqueeze(1), ACT.Copy)
                    if l < 3:
                        to_h = act.activation(scores[:, :, ds(q * QT + i, 1)],
                                              bank[2 + i][:, F:F + 2 * H].unsqueeze(2), ACT.Copy)
                    to_h.then_inc(s_h, 1)

            def tanh_rows(q):
                act.wait_ge(s_tanhin, q + 1)
                for i in range(QT):
                    last = act.activation(ex[:, i, :], low[:, i, :], ACT.Tanh,
                                          accum_out=scores[:, 0, ds(q * QT + i, 1)])
                last.then_inc(s_tanh, 1)

            def elu_exp(q):
                act.wait_ge(s_elumin, q + 1)
                act.activation(ex, low, ACT.Exp).then_inc(s_eluexp, 1)

            def stats(l):
                if l < 3:
                    act.wait_ge(s_srcps, l + 1)
                    act.activation(srcT[:, :], bank[4][:, 0:P], ACT.Copy).then_inc(s_src, 1)
                act.wait_ge(s_shift, l + 1)
                e, c = (m[:, :, :, :].rearrange("p k h t -> p k (h t)") for m in (emul, cmul))
                if l < 3:
                    act.activation(e[:, 1], e[:, 0], ACT.Exp, scale=SLOPES[l])
                    act.activation(e[:, 0], e[:, 0], ACT.Exp)
                    act.activation(c, c, ACT.Exp).then_inc(s_exps, 1)
                else:
                    act.activation(emul[:, 0, 0, :], emul[:, 0, 0, :], ACT.Exp).then_inc(s_exps, 1)

            def attention(l):
                with act.Fori(0, H // 2) as pp:
                    for slot in range(2):
                        p = pp * 2 + slot
                        act.activation(kpass[:, slot:slot + 1, :], kscores[:, ds(p, 1), :], ACT.Copy)\
                            .then_inc(s_kpass, 1)
                        act.wait_ge(s_kpass, p + (l * H + 1))
                        act.nop(nofuse=True)
                        with act.Fori(0, NG // 2) as gg:
                            for par in range(2):
                                act.wait_ge(s_srow[par], (p * (NG // 2) + gg + (l * H * NG // 2 + 1)) * 16)
                                act.nop(nofuse=True)
                                for k in range(BITS):
                                    act.wait_ge(s_sides, (p * NG + gg * 2) * BITS + (l * H * UNITS + par * BITS + k - 1 + CREDIT))
                                    act.nop(nofuse=True)
                                    for q in range(Q):
                                        last = act.activation(
                                            above[:, k % 2, q, :], srow[:, par, :], ACT.Relu, scale=BIG,
                                            bias=kpass[:, slot, q * BITS + k:q * BITS + k + 1], saturate=False)
                                    last.then_inc(s_above, 1)

            def dense2():
                act.wait_ge(E.ready, 1)

                def copy_T(at, scale):
                    for t in range(ET):
                        act.wait_ge(E.T_ps, at + (t + 1))
                        act.activation(wideT[:, t].rearrange("p k n -> p (k n)"), bank[(7, 5)[t]][:, :],
                                       ACT.Copy, scale=scale).then_inc(E.T, 1)

                def tanhs(at, out_tiles, tiles):
                    for t in range(ET):
                        act.wait_ge(E.lin, at + (t + 1))
                        act.activation(out_tiles[t], tiles[:, t, :], ACT.Tanh, scale=0.5).then_inc(E.tanh, 1)

                def gates(i, b):
                    act.wait_ge(E.hz_ps, i * 4 + b + 1)
                    if b >= 2:
                        act.wait_ge(E.uT, i * 4 + (b - 1))
                    act.activation(h_part[:, b % 2, :], bank[1 + b % 2][:, 0:EI], ACT.Identity,
                                   bias=c_hz[:, b:b + 1])
                    act.activation(z_part[:, b % 2, :], bank[1 + b % 2][:, EI:2 * EI], ACT.Identity,
                                   bias=c_hz[:, 4 + b:5 + b])
                    act.activation(z_tanh[:, b % 2, :], bank[1 + b % 2][:, EI:2 * EI], ACT.Tanh, scale=0.5,
                                   bias=c_hz_half[:, b:b + 1]).then_inc(E.z_tanh, 1)

                def step(i, new, old):
                    if new:
                        act.activation(whs, h[:, ds(i * ET, ET), :], ACT.Copy).then_inc(E.whs, 1)
                        act.wait_ge(E.whT_ps, i + 1)
                        act.activation(whT.rearrange("p k n -> p (k n)"), bank[0][:, :], ACT.Copy).then_inc(E.whT, 1)
                    if old:
                        if new:
                            act.wait_ge(E.fe2_ps, i)
                        copy_T(T_count(i, 0), 1.0)
                    if new:
                        for t in range(ET):
                            act.wait_ge(E.top, i * ET + t + 1)
                            act.activation(dt_exp[:, t, :], bcdt[:, t, 2 * SD:3 * SD], ACT.Exp,
                                           bias=ecol[:, 16 + t:17 + t], accum_out=ecol[:, 18 + t:19 + t])\
                                .then_inc(E.exp, 1)
                        act.wait_ge(E.baT_ps, i + 1)
                        act.activation(baT, bank[5][:, 0:EI], ACT.Copy).then_inc(E.baT, 1)
                        for b in range(2):
                            gates(i, b)
                    if old:
                        tanhs(wide_count(i, 1), wide_g_tanh, wide_g)
                    if new:
                        for b in range(2, 4):
                            gates(i, b)
                        tanhs(wide_count(i, 0), [wide_tanh[:, t, :] for t in range(ET)], wide)
                    if old:
                        act.wait_ge(E.wide_ps, wide_count(i, 1) + ET)
                        copy_T(T_count(i, 1), 0.5)
                    if new:
                        if old:
                            act.wait_ge(E.g2_ps, i)
                        copy_T(T_count(i, 2), 0.5)
                    if old:
                        act.wait_ge(E.gate_in, i)
                        act.activation(gate, gate, ACT.Tanh, scale=0.5).then_inc(E.gate, 1)

                step(0, True, False)
                with act.Fori(1, EG) as i:
                    step(i, True, True)
                step(EG, False, True)

            for l in range(last_layer + 1):
                if l == 3:
                    dense2()
                if l == 1:
                    elu_exp(0)
                    with act.Fori(1, QUADS) as q:
                        elu_exp(q)
                        dense(l, q - 1)
                    dense(l, QUADS - 1)
                elif l == 3:
                    dense(l, 0)
                    with act.Fori(1, QUADS) as q:
                        tanh_rows(q - 1)
                        dense(l, q)
                    tanh_rows(QUADS - 1)
                else:
                    with act.Fori(0, QUADS) as q:
                        dense(l, q)
                stats(l)
                if l < 3:
                    attention(l)
            if last_layer == 2:
                dense2()
            if last_layer == 0:
                with act.Fori(0, QUADS) as q:
                    elu_exp(q)

        @block.tensor
        def _(pe):
            def dense(l, q):
                for half in range(2):
                    for i in (2 * half, 2 * half + 1):
                        pe.wait_ge(s_xmade, q * QT + (l * T + i + 1))
                        for k in range(2):
                            last = pe.transpose(bank[half][:, (i % 2 * 2 + k) * P:(i % 2 * 2 + k + 1) * P],
                                                xs[:, i, k * P:(k + 1) * P], ident[:, :])
                    last.then_inc(s_xtps, 1)
                pe.wait_ge(s_h, q * QT + (l * T + 1))
                width = F + 2 * H if l < 3 else F
                for i in range(QT):
                    pe.wait_ge(s_xt, q * 2 + (l * 2 * QUADS + i // 2 + 1))
                    for k in range(2):
                        last = pe.matmul(bank[2 + i][:, 0:width], xT[:, i, k, :], weights[:, k, 0:width],
                                         start=(k == 0), stop=(k == 1))
                    last.then_inc(s_hps, 1)

            def pack(t):
                for half in range(2):
                    pe.wait_ge(s_adjbf, t * 2 + half + 1)
                    pe.wait_ge(s_packed, t * 2 + (half + 1))
                    pe.nop(nofuse=True)
                    for q in range(2):
                        for k in range(BITS):
                            j = q * BITS + k
                            last = pe.matmul(bank[6 + half][:, q * P:(q + 1) * P],
                                             adj_bf[:, half, j * P:(j + 1) * P], powers[:, k, :],
                                             start=(k == 0), stop=(k == BITS - 1))
                    last.then_inc(s_packmm, 1)

            def src_rows(l):
                pe.wait_ge(s_h, T * (l + 1) + 1)
                pe.transpose(bank[4][:, 0:P], scores[:, 0:H, :].rearrange("p h t -> p (h t)"), ident[:, :])\
                    .then_inc(s_srcps, 1)

            def attention(l):
                if l < 3:
                    pe.wait_ge(s_vfirst, l + 1)
                with pe.Fori(0, H // 2) as pp:
                    for slot in range(2):
                        p = pp * 2 + slot
                        pe.wait_ge(s_vals, p * NG + (l * CHUNKS + FIRST_CHUNKS))
                        pe.nop(nofuse=True)
                        with pe.Fori(0, NG // 2) as gg:
                            for par in range(2):
                                pe.wait_ge(s_sums, p * NG + gg * 2 + (l * SUMS + par + 1))
                                pe.nop(nofuse=True)
                                for k in range(BITS):
                                    pe.wait_ge(s_sides, (p * NG + gg * 2) * BITS + (l * H * UNITS + par * BITS + k + 1 + CREDIT))
                                    pe.nop(nofuse=True)
                                    for q in range(Q):
                                        v = values[:, slot, q * BITS + k, :]
                                        first, final = (k == 0 and q == 0), (k == BITS - 1 and q == Q - 1)
                                        for it in range(GT):
                                            acc = bank[GT * par + it]
                                            rows = slice(it * P, (it + 1) * P)
                                            if l < 3:
                                                last = pe.matmul(acc[:, 0:KW], pos[:, k % 2, q, :].bitcast(FP8)[:, rows],
                                                                 v[:, 0:KW], start=first, stop=final,
                                                                 skip_group_check=True)
                                                last = pe.matmul(acc[:, KW:2 * KW],
                                                                 neg[:, k % 2, q, :].bitcast(FP8)[:, rows],
                                                                 v[:, KW:2 * KW], start=False, stop=final,
                                                                 skip_group_check=True)
                                            else:
                                                last = pe.matmul(acc[:, 0:KW],
                                                                 edge[:, k % 2, q, :].bitcast(FP8)[:, rows],
                                                                 v[:, 0:KW], start=first, stop=final)
                                    last.then_inc(s_unit, 1)

            def dense2():
                pe.wait_ge(E.weights, 16 * 8)

                def product(dst, lhsT, rhs):
                    for k in range(len(lhsT)):
                        last = pe.matmul(dst, lhsT[k], rhs[k], start=(k == 0), stop=(k == len(lhsT) - 1))
                    return last

                def rows(m, t):
                    return [m[:, k, t * P:(t + 1) * P] for k in range(m.shape[1])]

                def blocks(m, a=None, b=None):
                    return [m[:, k, a:b] for k in range(m.shape[1])]

                def transposes(t, sources):
                    for i, src in enumerate(sources):
                        last = pe.transpose(bank[(7, 5)[t]][:, i * P:(i + 1) * P], src, ident[:, :])
                    last.then_inc(E.T_ps, 1)

                def cut(tile, n):
                    return [tile[:, i * P:(i + 1) * P] for i in range(n)]

                def g1_product(i, t):
                    pe.wait_ge(E.T, T_count(i, 0) + (t + 1))
                    product(bank[3 + t][:, :], blocks(wideT[:, t]), blocks(m_g1)).then_inc(E.wide_ps, 1)

                def step(i, new, old):
                    if new:
                        pe.wait_ge(E.whs, i + 1)
                        if old:
                            pe.wait_ge(E.hs2, i)
                        for k in range(2):
                            for t in range(ET):
                                last = pe.transpose(bank[0][:, k * EI + t * P:k * EI + (t + 1) * P],
                                                    whs[:, t, k * P:(k + 1) * P], ident[:, :])
                        last.then_inc(E.whT_ps, 1)
                    if old:
                        pe.wait_ge(E.hatt, i * 16)
                        pe.wait_ge(E.hs2, i)
                        if new:
                            pe.wait_ge(E.T, T_count(i, 0))
                        for t in range(ET):
                            transposes(t, cut(hatt[:, t, :], 2) + cut(hs2[:, t, :], 2))
                    if new:
                        if old:
                            pe.wait_ge(E.henh, i)
                        pe.wait_ge(E.whT, i + 1)
                        for t in range(ET):
                            product(bank[1 + t][:, 0:3 * SD], rows(whT, t), blocks(m_bcdt)).then_inc(E.bc_ps, 1)
                    if old:
                        g1_product(i, 0)
                    if new:
                        if old:
                            pe.wait_ge(E.T, T_count(i, 0) + ET)
                        pe.wait_ge(E.ba, (i + 1) * ET)
                        for t in range(ET):
                            last = pe.transpose(bank[5][:, t * P:(t + 1) * P], ba[:, t, :], ident[:, :])
                        last.then_inc(E.baT_ps, 1)
                    if old:
                        g1_product(i, 1)
                    if new:
                        pe.wait_ge(E.baT, i + 1)
                        for b in range(2):
                            last = pe.matmul(bank[6][:, b * EI:(b + 1) * EI], m_abp[:, b * P:(b + 1) * P], baT,
                                             start=True, stop=True)
                        last.then_inc(E.ab_ps, 1)
                        for t in range(ET):
                            if old:
                                pe.wait_ge(E.var, wide_count(i, 1) + (t + 1))
                            product(bank[3 + t][:, :], rows(whT, t), blocks(m_fe1)).then_inc(E.wide_ps, 1)
                        pe.wait_ge(E.hsT, i + 1)
                        for b in range(4):
                            if b >= 2:
                                pe.wait_ge(E.z_tanh, i * 4 + (b - 1))
                            for part in range(2):
                                c = part * DI + b * P
                                last = product(bank[1 + b % 2][:, part * EI:(part + 1) * EI],
                                               blocks(m_hz, c, c + P), blocks(hsT))
                            last.then_inc(E.hz_ps, 1)
                    if old:
                        for t in range(ET):
                            pe.wait_ge(E.silu, wide_count(i, 1) + (t + 1))
                            transposes(t, cut(wide_g[:, t, :], 4))
                        for t in range(ET):
                            pe.wait_ge(E.T, T_count(i, 1) + (t + 1))
                            last = product(bank[6][:, t * F:(t + 1) * F], blocks(wideT[:, t]), blocks(m_g2))
                        last.then_inc(E.g2_ps, 1)
                    if new:
                        pe.wait_ge(E.uT, (i + 1) * 4)
                        for t in range(ET):
                            last = product(bank[0][:, t * F:(t + 1) * F], rows(uT, t), blocks(m_out))
                        last.then_inc(E.out_ps, 1)
                        for t in range(ET):
                            pe.wait_ge(E.silu, wide_count(i, 0) + (t + 1))
                            transposes(t, cut(wide[:, t, :], 4))
                        for t in range(ET):
                            pe.wait_ge(E.T, T_count(i, 2) + (t + 1))
                            last = product(bank[2][:, t * F:(t + 1) * F], blocks(wideT[:, t]), blocks(m_fe2))
                        last.then_inc(E.fe2_ps, 1)

                step(0, True, False)
                with pe.Fori(1, EG) as i:
                    step(i, True, True)
                step(EG, False, True)

            pe.wait_ge(s_const, 2)
            pe.wait_ge(s_x, 16)
            for i, signal in enumerate((s_unit, s_unit, s_packmm, s_packmm, s_xtps)):
                pe.transpose(bank[i][:, 0:P], ident[:, :], ident[:, :]).then_inc(signal, 1)
            for l in range(last_layer + 1):
                if l == 3:
                    dense2()
                pe.wait_ge(s_wfix, l + 1)
                with pe.Fori(0, QUADS) as q:
                    dense(l, q)
                    if l == 0:
                        pack(q)
                if l < 3:
                    src_rows(l)
                if l == 0:
                    with pe.Fori(QUADS, T) as t:
                        pack(t)
                attention(l)
            if last_layer == 2:
                dense2()

        @block.vector
        def _(dve):
            chain = Chain(s_dve)

            def fold_weights(l):
                dve.wait_ge(s_w, loaded_weights[l])
                for k in range(2):
                    for s in range(2):
                        if l < 3:
                            product = prod[:, s, :]
                            dve.tensor_tensor(product, weights[:, k, 0:F], avec[:, s, :], ALU.mult).then_inc(s_dve, 1)
                            dve.wait_ge(s_dve, chain.next())
                            col = F + s * H
                            if l < 2:
                                dve.tensor_reduce(weights[:, k, col:col + H],
                                                  product.rearrange("p (h d) -> p h d", h=H), AX.X, ALU.add)\
                                    .then_inc(s_dve, 1)
                                dve.wait_ge(s_dve, chain.next())
                            else:
                                for hd in range(H):
                                    dve.tensor_reduce(weights[:, k, col + hd:col + hd + 1], product,
                                                      AX.X, ALU.add).then_inc(s_dve, 1)
                                    dve.wait_ge(s_dve, chain.next())
                chain.settle()
                dve.memset(credits[:, 8 + l:9 + l], 0.0).then_inc(s_wfix, 1)

            def pack(t):
                for half in range(2):
                    dve.wait_ge(s_adj[half], (t + 1) * 16)
                    dve.wait_ge(s_packmm, t * 2 + (half + 1))
                    dve.tensor_scalar(adj_bf[:, half, :], adj_in[:, half, :], 0, None, ALU.is_gt)\
                        .then_inc(s_adjbf, 1)
                for half in range(2):
                    dve.wait_ge(s_packmm, t * 2 + (half + 1 + CREDIT))
                    dve.tensor_copy(packed_bytes[:, 2 * half:2 * half + 2, ds(t * P, P)],
                                    bank[6 + half][:, 0:2 * P].rearrange("p (q n) -> p q n", q=2))\
                        .then_inc(s_packed, 1)

            def norm_first(l, q):
                if l == 1:
                    dve.tensor_scalar(low, h[:, ds(q * QT, QT), :], 0.0, None, ALU.min).then_inc(s_elumin, 1)

            def norm_stats(l, q):
                xq, hq = (m[:, ds(q * QT, QT), :] for m in (x, h))
                if l == 1:
                    dve.wait_ge(s_eluexp, q + 1)
                    dve.tensor_tensor(low, hq, low, ALU.subtract).then_inc(s_dve, 1)
                    dve.wait_ge(s_dve, chain.next())
                    dve.scalar_tensor_tensor(out=ex, in0=ex, scalar=-1.0, in1=low, op0=ALU.add, op1=ALU.add)\
                        .then_inc(s_dve, 1)
                    dve.wait_ge(s_dve, chain.next())
                    dve.tensor_tensor(xq, xq, ex, ALU.add).then_inc(s_dve, 1)
                    dve.wait_ge(s_dve, chain.next())
                    dve.nop(nofuse=True)
                elif l in (2, 4):
                    dve.tensor_tensor(xq, xq, hq, ALU.add).then_inc(s_dve, 1)
                    dve.wait_ge(s_dve, chain.next())
                    dve.nop(nofuse=True)
                for i in range(QT):
                    last = dve.bn_stats(lnst[:, i, 0:6], x[:, ds(q * QT + i, 1), :].squeeze(1))
                last.then_inc(s_dve, 1)
                dve.wait_ge(s_dve, chain.next())
                dve.nop(nofuse=True)
                for i in range(QT):
                    last = dve.bn_aggr(lnst[:, i, 6:8], lnst[:, i, 0:6])
                last.then_inc(s_var, 1)

            def normalize(l, q):
                if l <= last_layer:
                    dve.wait_ge(s_xtps, q * 2 + (l * 2 * QUADS + 1))
                    if isinstance(q, int) and q == 0:
                        if l > 1:
                            dve.wait_ge(s_xkept, (l - 1) * QUADS)
                    else:
                        dve.wait_ge(s_xkept, q + (l - 1) * QUADS)
                dve.wait_ge(s_rstd, q + ((l - 1) * QUADS + 1))
                for i in range(QT):
                    xt = x[:, ds(q * QT + i, 1), :]
                    normed = xs[:, i:i + 1, :] if l <= last_layer else xt
                    dve.tensor_scalar(normed, xt, lnst[:, i, 6:7], lnst[:, i, 9:10], ALU.subtract, ALU.mult)\
                        .then_inc(s_xmade, 1)

            def between(l):
                norm_first(l, 0)
                norm_stats(l, 0)
                if l == 3:
                    normalize(l, 0)
                    norm_stats(l, 1)
                    chain.settle()
                    with dve.Fori(2, QUADS) as q:
                        chain.enter(q - 2, NORM_LINKS[l] + 2)
                        normalize(l, q - 1)
                        tanh_in(q - 2)
                        norm_stats(l, q)
                        tanh_scores(q - 2)
                    chain.leave(QUADS - 2)
                    normalize(l, QUADS - 1)
                    for q in (QUADS - 2, QUADS - 1):
                        tanh_in(q)
                        tanh_scores(q)
                    chain.settle()
                    return
                chain.settle()
                with dve.Fori(1, QUADS) as q:
                    chain.enter(q - 1, NORM_LINKS[l])
                    norm_first(l, q)
                    normalize(l, q - 1)
                    norm_stats(l, q)
                chain.leave(QUADS - 1)
                normalize(l, QUADS - 1)

            def tanh_in(q):
                dve.wait_ge(s_h, q * QT + (3 * T + 1 + QT))
                dve.tensor_tensor(low, h[:, ds(q * QT, QT), :], bvec[:, :].unsqueeze(1).to_broadcast([P, QT, F]),
                                  ALU.add).then_inc(s_tanhin, 1)

            def tanh_scores(q):
                dve.wait_ge(s_tanh, q + 1)
                dve.tensor_tensor(low, ex, avec[:, 0:1, :].to_broadcast([P, QT, F]), ALU.mult).then_inc(s_dve, 1)
                dve.wait_ge(s_dve, chain.next())
                dve.tensor_reduce(scores[:, H, ds(q * QT, QT)], low, AX.X, ALU.add).then_inc(s_dve, 1)
                dve.wait_ge(s_dve, chain.next())

            def stats(l):
                n = H if l < 3 else 1
                if l < 3:
                    dve.wait_ge(s_h, T * (l + 1) + 1)
                src, dst = scores[:, 0:H, :], scores[:, H:H + n, :]
                dve.tensor_reduce(smax[:, 0, 0:n], dst, AX.X, ALU.max).then_inc(s_pmax, 1)
                dve.wait_ge(s_max, l + 1)
                top = smax[:, 1, 0:n].unsqueeze(2).to_broadcast([P, n, T])
                shifted = dve.tensor_tensor(emul[:, 0, 0:n, :], dst, top, ALU.subtract)
                if l == 3:
                    shifted.then_inc(s_shift, 1)
                    dve.tensor_scalar(zrow[:, 0, 0, :], scores[:, 0, :], 0.0, None, ALU.not_equal).then_inc(s_dve, 1)
                    dve.wait_ge(s_dve, chain.next())
                    dve.wait_ge(s_exps, 4)
                    for hd in range(1, H):
                        last = dve.tensor_tensor(emul[:, 0, hd, :], emul[:, 0, 0, :], zrow[:, 0, 0, :], ALU.mult)
                    last.then_inc(s_dve, 1)
                    dve.wait_ge(s_dve, chain.next())
                    dve.tensor_copy(emul[:, 0, 0, :], emul[:, 0, 1, :]).then_inc(s_emul, 1)
                    chain.settle()
                    return
                z, az, m = (zrow[:, i] for i in range(3))
                dve.tensor_tensor(z, src, top, ALU.add).then_inc(s_dve, 1)
                dve.wait_ge(s_dve, chain.next())
                dve.tensor_scalar(az, z, SLOPES[l], None, ALU.mult).then_inc(s_dve, 1)
                dve.wait_ge(s_dve, chain.next())
                dve.tensor_tensor(m, z, az, ALU.max).then_inc(s_dve, 1)
                dve.wait_ge(s_dve, chain.next())
                dve.tensor_tensor(cmul[:, 0], z, m, ALU.subtract)
                dve.tensor_tensor(cmul[:, 1], az, m, ALU.subtract)
                dve.tensor_scalar(kscores[:, :, :], dst, BIG, None, ALU.mult).then_inc(s_shift, 1)
                chain.settle()
                dve.wait_ge(s_exps, l + 1)
                with dve.Fori(0, FIRST_CHUNKS) as c:
                    chain.enter(c, VALUE_LINKS + 1)
                    if l == 0:
                        for i in range(2):
                            pack(c * 2 + (QUADS + i))
                    value_parts(dve, chain, vtmp_dve, 1, c * CHUNK, CHUNK, 0, 0).then_inc(s_dve, 1)
                    dve.wait_ge(s_dve, chain.next())
                chain.leave(FIRST_CHUNKS)
                dve.memset(credits[:, 12 + l:13 + l], 0.0).then_inc(s_vfirst, 1)

            def evacuate(l, par, count):
                kinds = 2 if l < 3 else 1
                dve.wait_ge(s_unit, count * BITS + (l * H * UNITS + CREDIT))
                dve.wait_ge(s_quot, count + (l * H * NG + CREDIT - 1))
                for it in range(GT):
                    parts = bank[GT * par + it][:, 0:kinds * KW].rearrange("p (k a c) -> p k c a", k=kinds, a=PARTS)
                    last = dve.tensor_reduce(sums[:, par, it, 0:kinds, :], parts, AX.X, ALU.add)
                last.then_inc(s_sums, 1)

            def attention(l):
                per_group = 2 * BITS if l < 3 else 0
                with dve.Fori(0, H // 2) as pp:
                    for slot in range(2):
                        p = pp * 2 + slot
                        with dve.Fori(0, NG // 2) as gg:
                            for par in range(2):
                                g = p * NG + gg * 2 + par
                                chain.enter(g, per_group)
                                for k in range(BITS):
                                    unit = g * BITS + (l * H * UNITS + k)
                                    r = k % 2
                                    shift = (6 - k, ALU.logical_shift_left) if k <= 6 else (1, ALU.logical_shift_right)
                                    words = packed[:, :, ds(gg * (2 * WORDS) + par * WORDS, WORDS)]
                                    if l == 3:
                                        dve.wait_ge(s_unit, unit - 1 + CREDIT)
                                    edges = dve.tensor_scalar(edge[:, r], words, shift[0], ONE, shift[1],
                                                              ALU.bitwise_and)
                                    if l == 3:
                                        edges.then_inc(s_sides, 1)
                                    else:
                                        edges.then_inc(s_dve, 1)
                                        dve.wait_ge(s_dve, chain.next())
                                        dve.wait_ge(s_above, unit + 1)
                                        dve.wait_ge(s_unit, unit - 1 + CREDIT)
                                        dve.tensor_tensor(pos[:, r], edge[:, r],
                                                          above[:, r].bitcast(U32), ALU.bitwise_and).then_inc(s_dve, 1)
                                        dve.wait_ge(s_dve, chain.next())
                                        dve.tensor_tensor(neg[:, r], edge[:, r], pos[:, r], ALU.bitwise_xor)\
                                            .then_inc(s_sides, 1)
                                    if k == 1:
                                        evacuate(l, 1 - par, g)
                if per_group:
                    chain.leave(H * NG)
                evacuate(l, 1, H * NG)

            def dense2():
                dve.wait_ge(E.rows, 16 * (4 + len(row)))
                dve.tensor_tensor(row["b_bcdt"][:, 2 * SD:], row["b_bcdt"][:, 2 * SD:], row["A"], ALU.add)\
                    .then_inc(s_dve, 1)
                dve.wait_ge(s_dve, chain.next())
                dve.tensor_scalar(ecol[:, 24:25], c_cp, 1.0, None, ALU.add).then_inc(s_dve, 1)
                dve.wait_ge(s_dve, chain.next())
                dve.tensor_scalar(c_d_twice, c_d, 2.0, None, ALU.mult)
                dve.tensor_scalar(c_hz_half, c_hz[:, 4:8], 0.5, None, ALU.mult).then_inc(E.ready, 1)
                chain.settle()

                def both(name):
                    return row[name].unsqueeze(1).to_broadcast([P, ET, row_widths[name]])

                def stats(tile, st, signal):
                    n = tile.shape[-1]
                    dve.bn_stats(st[:, 0:6], tile).then_inc(s_dve, 1)
                    dve.wait_ge(s_dve, chain.next())
                    dve.nop(nofuse=True)
                    dve.bn_aggr(st[:, 6:8], st[:, 0:6]).then_inc(signal, 1)

                def wide_in(at, which, tiles, bias):
                    for t in range(ET):
                        dve.wait_ge(E.wide_ps, at + (t + 1))
                        dve.tensor_tensor(tiles[:, t, :], bank[3 + t][:, :], row[bias], ALU.add).then_inc(s_dve, 1)
                        dve.wait_ge(s_dve, chain.next())
                        dve.nop(nofuse=True)
                        stats(tiles[:, t, :], est[:, which, t, :], E.var)

                def wide_norm(at, which, tiles):
                    for t in range(ET):
                        dve.wait_ge(E.rstd, at + (t + 1))
                        dve.tensor_scalar(tiles[:, t, :], tiles[:, t, :], est[:, which, t, 6:7],
                                          est[:, which, t, 9:10], ALU.subtract, ALU.mult).then_inc(E.norm, 1)

                def wide_silu(at, tanh_tiles, tiles):
                    for t in range(ET):
                        dve.wait_ge(E.tanh, at + (t + 1))
                        dve.scalar_tensor_tensor(out=tiles[:, t, :], in0=tanh_tiles[t], scalar=1.0,
                                                 in1=tiles[:, t, :], op0=ALU.add, op1=ALU.mult).then_inc(E.silu, 1)

                def gated(i, b):
                    dve.wait_ge(E.z_tanh, i * 4 + b + 1)
                    dve.scalar_tensor_tensor(out=z_part[:, b % 2, :], in0=z_tanh[:, b % 2, :], scalar=1.0,
                                             in1=z_part[:, b % 2, :], op0=ALU.add, op1=ALU.mult)\
                        .then_inc(s_dve, 1)
                    dve.wait_ge(s_dve, chain.next())
                    dve.scalar_tensor_tensor(out=uT[:, b, :], in0=z_part[:, b % 2, :], scalar=c_d_twice,
                                             in1=h_part[:, b % 2, :], op0=ALU.add, op1=ALU.mult)\
                        .then_inc(E.uT, 1)

                def step(i, new, old):
                    if new:
                        for t in range(ET):
                            dve.wait_ge(E.bc_ps, i * ET + t + 1)
                            dve.tensor_tensor(bcdt[:, t, :], bank[1 + t][:, 0:3 * SD], row["b_bcdt"], ALU.add)\
                                .then_inc(s_dve, 1)
                            dve.wait_ge(s_dve, chain.next())
                            dve.tensor_reduce(ecol[:, 16 + t:17 + t], bcdt[:, t, 2 * SD:3 * SD], AX.X, ALU.max,
                                              negate=True).then_inc(E.top, 1)
                        for t in range(ET):
                            dve.wait_ge(E.exp, i * ET + t + 1)
                            dve.reciprocal(ecol[:, 20 + t:21 + t], ecol[:, 18 + t:19 + t]).then_inc(s_dve, 1)
                            dve.wait_ge(s_dve, chain.next())
                            dve.scalar_tensor_tensor(out=ba[:, t, :], in0=dt_exp[:, t, :],
                                                     scalar=ecol[:, 20 + t:21 + t], in1=bcdt[:, t, 0:SD],
                                                     op0=ALU.mult, op1=ALU.mult).then_inc(E.ba, 1)
                    if old:
                        wide_in(wide_count(i, 1), 1, wide_g, "g1_b")
                    if new:
                        dve.wait_ge(E.ab_ps, i + 1)
                        for b in range(2):
                            last = dve.scalar_tensor_tensor(out=hsT[:, b, :], in0=bank[6][:, b * EI:(b + 1) * EI],
                                                            scalar=c_abp[:, b:b + 1], in1=whT[:, b, :],
                                                            op0=ALU.add, op1=ALU.mult)
                        last.then_inc(E.hsT, 1)
                    if old:
                        wide_norm(wide_count(i, 1), 1, wide_g)
                    if new:
                        for t in range(ET):
                            dve.tensor_tensor(c_prod, bcdt[:, t, SD:2 * SD], row["cp_w"], ALU.mult)\
                                .then_inc(s_dve, 1)
                            dve.wait_ge(s_dve, chain.next())
                            dve.tensor_reduce(ecol[:, 26 + t:27 + t], c_prod, AX.X, ALU.add).then_inc(s_dve, 1)
                            dve.wait_ge(s_dve, chain.next())
                            dve.tensor_tensor(ecol[:, 22 + t:23 + t], ecol[:, 26 + t:27 + t],
                                              ecol[:, 24:25], ALU.add).then_inc(s_dve, 1)
                            dve.wait_ge(s_dve, chain.next())
                        wide_in(wide_count(i, 0), 0, wide, "fe1_b")
                        wide_norm(wide_count(i, 0), 0, wide)
                        for b in range(2):
                            gated(i, b)
                    if old:
                        wide_silu(wide_count(i, 1), wide_g_tanh, wide_g)
                    if new:
                        for b in range(2, 4):
                            gated(i, b)
                        wide_silu(wide_count(i, 0), [wide_tanh[:, t, :] for t in range(ET)], wide)
                    if old:
                        dve.wait_ge(E.g2_ps, i)
                        dve.tensor_tensor(gate, bank[6][:, :].rearrange("p (t f) -> p t f", t=ET), both("g2_b"),
                                          ALU.add).then_inc(E.gate_in, 1)
                    if new:
                        dve.wait_ge(E.out_ps, i + 1)
                        if old:
                            dve.wait_ge(E.parts, i)
                        dve.scalar_tensor_tensor(out=hs2, in0=bank[0][:, :].rearrange("p (t f) -> p t f", t=ET),
                                                 scalar=0.5, in1=both("out_b"), op0=ALU.mult, op1=ALU.add)\
                            .then_inc(s_dve, 1)
                        dve.wait_ge(s_dve, chain.next())
                        for t in range(ET):
                            last = dve.tensor_scalar(hs2[:, t, :], hs2[:, t, :], ecol[:, 22 + t:23 + t], None,
                                                     ALU.mult)
                        last.then_inc(E.hs2, 1)
                        dve.wait_ge(E.fe2_ps, i + 1)
                        dve.tensor_tensor(henh, bank[2][:, :].rearrange("p (t f) -> p t f", t=ET), both("fe2_b"),
                                          ALU.add).then_inc(E.henh, 1)
                    if old:
                        dve.wait_ge(E.fused, i)
                        dve.nop(nofuse=True)
                        for t in range(ET):
                            stats(fused[:, t, :], est[:, 2, t, :], E.fvar)
                        for t in range(ET):
                            dve.wait_ge(E.frstd, (i - 1) * ET + (t + 1))
                            dve.tensor_scalar(fused[:, t, :], fused[:, t, :], est[:, 2, t, 6:7],
                                              est[:, 2, t, 9:10], ALU.subtract, ALU.mult).then_inc(E.fnorm, 1)

                step(0, True, False)
                chain.settle()
                with dve.Fori(1, EG) as i:
                    chain.enter(i - 1, 10 * ET + 5)
                    step(i, True, True)
                chain.leave(EG - 1)
                step(EG, False, True)
                chain.settle()
                dve.wait_ge(E.x, T)

            for i, signal in enumerate((s_sides, s_sides, s_h, s_packed, s_packed)):
                dve.memset(credits[:, 3 + i:4 + i], 0.0).then_inc(signal, 1)
            for it in range(GT):
                last = dve.memset(bank[GT + it][:, :], 0.0)
            last.then_inc(s_const, 1)
            dve.memset(credits[:, 2:3], 0.0).then_inc(s_sums, 1)
            for l in range(last_layer + 1):
                if l == 3:
                    dense2()
                fold_weights(l)
                if l == 0:
                    with dve.Fori(0, QUADS) as t:
                        pack(t)
                else:
                    dve.wait_ge(s_quot, l * H * NG + CREDIT)
                    between(l)
                stats(l)
                if l == 0:
                    with dve.Fori(QUADS + 2 * FIRST_CHUNKS, T) as t:
                        pack(t)
                attention(l)
            if last_layer == 2:
                dense2()
            dve.wait_ge(s_quot, (last_layer + 1) * H * NG + CREDIT)
            between(last_layer + 1)


def kernel(**inputs):
    import numpy as _np
    import concourse.bacc as _bacc
    from concourse import mybir as _mybir
    from concourse.bass_utils import run_bass_kernel_spmd as _run

    nc = _bacc.Bacc("TRN2", target_bir_lowering=False, num_devices=1)
    arrays, args = {}, {}
    for name, a in inputs.items():
        a = _np.ascontiguousarray(a)
        arrays[f"in_{name}_dram"] = a
        args[name] = nc.dram_tensor(f"in_{name}_dram", a.shape, _mybir.dt.from_np(a.dtype),
                                    kind="ExternalInput").ap()
    out = nc.dram_tensor("out_0_dram", (N, F), F32, kind="ExternalOutput").ap()
    gnn_kernel(nc, args, out)
    r = _run(nc, [arrays], core_ids=[0])
    return r.results[0]["out_0_dram"]
```

```python
from contextlib import ExitStack

import concourse.bass as bass
from concourse import mybir

ds = bass.ds
ALU = mybir.AluOpType
ACT = mybir.ActivationFunctionType
AX = mybir.AxisListType
RMAX = bass.bass_isa.ReduceOp.max
F32 = mybir.dt.float32
BF16 = mybir.dt.bfloat16
FP8 = mybir.dt.float8e4
U8 = mybir.dt.uint8
U32 = mybir.dt.uint32
I32 = mybir.dt.int32

P = 128
N = 4096
F = 256
T = N // P
QT = 4
QUADS = T // QT
H = 4
D = F // H
C = D + 1
PARTS = 3
KW = PARTS * C
GT = 4
GI = GT * P
NG = N // GI
BITS = 8
Q = T // BITS
WORDS = GI // 4
ONE = 0x40404040
BIG = 2.0 ** 60
SLOPES = (0.01, 0.2, 0.2)
EPS = 1e-5
CHUNK = 8
FIRST_CHUNKS = T // CHUNK
POOL_CHUNKS = {0: 3, 1: 3, 2: 3, 3: 1}
UNITS = NG * BITS
PACKED_FIRST = QUADS
PACKING = (T - PACKED_FIRST) // GT
DI = 512
SD = 128
ET = 2
EI = ET * P
EG = T // ET
CREDIT = 2


NORM_LINKS = {1: 4, 2: 2, 3: 1, 4: 2}


def values_before(l):
    return sum(POOL_CHUNKS[m] + (H - 1) * NG for m in range(l))


class Chain:

    def __init__(self, sem):
        self.sem, self.start, self.local, self.base = sem, 0, 0, 0

    def enter(self, i, per):
        self.base, self.per, self.local = self.start + i * per, per, 0

    def settle(self):
        self.start += self.local
        self.base, self.local = self.start, 0

    def leave(self, trips):
        assert self.local == self.per, (self.local, self.per)
        self.start += trips * self.per
        self.base, self.local = self.start, 0

    def next(self):
        self.local += 1
        return self.base + self.local


def gnn_kernel(nc, A, out, last_layer=3):
    with ExitStack() as ctx:
        def sb(name, shape, dt=F32):
            return ctx.enter_context(nc.sbuf_tensor(name, shape, dt))

        def sem(name):
            return ctx.enter_context(nc.semaphore(name))

        packed = sb("packed", [P, Q, N // 4], U32)
        x = sb("x", [P, T, F])
        h = sb("h", [P, T, F])
        values = sb("values", [P, 2, T, 2 * KW], BF16)
        above = sb("above", [P, 2, Q, GI], FP8)
        rings = sb("rings", [P, CHUNK * 2 * C + 2 * (2 * Q * WORDS)], U32)
        ring = rings[:, CHUNK * 2 * C:].rearrange("p (o s q w) -> p o s q w", o=2, s=2, q=Q)
        edge = rings[:, 0:2 * Q * WORDS].rearrange("p (s q w) -> p s q w", s=2, q=Q)
        pos = ring[:, 0]
        neg = ring[:, 1]
        srow = sb("srow", [P, 2, GI])
        arena = sb("arena", [P, T * F])
        weights = sb("weights", [P, 2, F + 2 * H])
        avec = sb("avec", [P, 2, F])
        bvec = sb("bvec", [P, F])
        scores = sb("scores", [P, 2 * H, T])
        kscores = sb("kscores", [P, H, T])
        kpass = sb("kpass", [P, 2, T])
        emul = sb("emul", [P, 2, H, T])
        cmul = sb("cmul", [P, 2, H, T])
        zrow = sb("zrow", [P, 3, H, T])
        smax = sb("smax", [P, 2, H])
        srcT = sb("srcT", [P, P])
        sums = sb("sums", [P, 2, GT, 2, C])
        quot = sb("quot", [P, 3, GT, C])
        vtmp_pool = sb("vtmp_pool", [P, 2, CHUNK, C])
        vtmp_dve = rings[:, 0:CHUNK * 2 * C].bitcast(F32).rearrange("p (a n c) -> p a n c", a=2, c=C)
        prod = neg[:, :].rearrange("p s q w -> p (s q w)").bitcast(F32)[:, 0:2 * F].rearrange("p (s f) -> p s f", s=2)
        lnst = sb("lnst", [P, QT, 16])
        exponents = sb("exponents", [P, 1 + GT])
        minus_half, minus_one = exponents[:, 0:1], exponents[:, 1:1 + GT].unsqueeze(2)
        credits = sb("credits", [P, 16])
        ident = sb("ident", [P, P])
        powers = sb("powers", [P, BITS, P], BF16)

        adj_in = arena[:, 0:4096].bitcast(I32).rearrange("p (s n) -> p s n", s=2)
        adj_bf = arena[:, 4096:6144].bitcast(BF16).rearrange("p (s n) -> p s n", s=2)
        attn2 = arena[:, :].rearrange("p (t f) -> p t f", f=F)
        packed_bytes = packed[:, :, :].bitcast(U8)

        vroom = values[:, :, :, :].rearrange("p s t c -> p (s t c)").bitcast(F32)
        rroom = rings[:, :].bitcast(F32)
        aroom = above[:, :, :, :].rearrange("p s q n -> p (s q n)").bitcast(F32)
        sroom = srow[:, :, :].rearrange("p s n -> p (s n)")
        tiles_room = vroom[:, T * KW:]
        low, ex, xs, xT = (tiles_room[:, i * QT * F:(i + 1) * QT * F] for i in range(4))
        low, ex, xs = (m.rearrange("p (t f) -> p t f", t=QT) for m in (low, ex, xs))
        xT = xT.rearrange("p (t k n) -> p t k n", t=QT, k=2)
        proom = vtmp_pool[:, :, :, :].rearrange("p a n c -> p (a n c)")

        class Room:

            def __init__(self, view):
                self.view, self.at = view, 0

            def take(self, *shape):
                n = 1
                for d in shape:
                    n *= d
                piece = self.view[:, self.at:self.at + n]
                self.at += n
                assert self.at <= self.view.shape[1]
                names = "abc"[:len(shape)]
                if len(shape) == 1:
                    return piece
                return piece.rearrange(f"p ({' '.join(names)}) -> p {' '.join(names)}", **dict(zip(names, shape)))

        room = Room(vroom)
        m_fe1, m_fe2 = room.take(2, DI), room.take(4, F)
        m_bcdt, m_abp = room.take(2, 3 * SD), room.take(F)
        m_hz, m_out = room.take(2, 2 * DI), room.take(4, F)
        m_g1, m_g2 = room.take(4, DI), room.take(4, F)
        wide, wide_tanh, wideT = room.take(ET, DI), room.take(ET, DI), room.take(ET, 4, P)
        room = Room(arena[:, :])
        row_widths = {"b_bcdt": 3 * SD, "cp_w": SD, "out_b": F, "fe1_b": DI, "fe_ln_g": DI, "fe_ln_b": DI,
                      "fe2_b": F, "g1_b": DI, "g_ln_g": DI, "g_ln_b": DI, "g2_b": F, "ln_g": F, "ln_b": F,
                      "A": SD}
        row = {name: room.take(w) for name, w in row_widths.items()}
        hatt, hs2, henh, gate, fused = (room.take(ET, F) for _ in range(5))
        whs = room.take(ET, F)
        room = Room(rroom)
        whT, hsT, uT = room.take(2, EI), room.take(2, EI), room.take(4, EI)
        bcdt, baT = room.take(ET, 3 * SD), room.take(EI)
        room = Room(aroom)
        z_tanh, h_part = room.take(2, EI), room.take(2, EI)
        room = Room(sroom)
        z_part, dt_exp = room.take(2, EI), room.take(ET, SD)
        room = Room(proom)
        ba, c_prod, est, base = room.take(ET, SD), room.take(SD), room.take(3, ET, 16), room.take(ET, F)
        wide_g = Room(sums[:, :, :, :, :].rearrange("p a t k c -> p (a t k c)")).take(ET, DI)
        wide_g_tanh = [powers[:, :, :].bitcast(F32).rearrange("p k n -> p (k n)")[:, 0:DI],
                       quot[:, :, :, :].rearrange("p a t c -> p (a t c)")[:, 0:DI]]
        ecol = sb("ecol", [P, 32])
        c_abp, c_hz, c_hz_half = ecol[:, 0:2], ecol[:, 2:10], ecol[:, 10:14]
        c_d, c_cp, top_dt, sum_dt, inv_dt, one_c = (ecol[:, i:i + 1] for i in (14, 15, 16, 18, 20, 22))
        c_d_twice = ecol[:, 28:29]
        attn_dram = nc.dram_tensor("attn_dram", [N, F], F32)[:, :]

        bank = [ctx.enter_context(nc.psum_tensor(f"bank{i}", [P, 512], F32)) for i in range(8)]

        src_dram = [nc.dram_tensor(f"src_dram{l}", [H * T, P], F32)[:, :] for l in range(3)]

        s_x = sem("x_loaded")
        s_w = sem("weights_loaded")
        s_wfix = sem("weights_fixed")
        s_adj = [sem("adj_loaded0"), sem("adj_loaded1")]
        s_adjbf = sem("adj_is_bf16")
        s_packmm = sem("pack_matmul")
        s_packed = sem("packed_stored")
        s_const = sem("constants_made")
        s_dve = sem("dve_chain")
        s_pool = sem("pool_chain")
        s_elumin = sem("elu_min")
        s_eluexp = sem("elu_exp")
        s_var = sem("variance_made")
        s_rstd = sem("rstd_made")
        s_xmade = sem("x_made")
        s_xkept = sem("x_kept")
        s_xtps = sem("xt_in_psum")
        s_xt = sem("xt_made")
        s_hps = sem("h_in_psum")
        s_h = sem("h_made")
        s_tanhin = sem("tanh_in_made")
        s_tanh = sem("tanh_made")
        s_srcps = sem("src_in_psum")
        s_src = sem("src_transposed")
        s_srcst = sem("src_stored")
        s_pmax = sem("partition_max")
        s_max = sem("max_made")
        s_shift = sem("shifts_made")
        s_exps = sem("exps_made")
        s_emul = sem("layer3_weights_made")
        s_vfirst = sem("dve_values_made")
        s_vals = sem("values_made")
        s_srow = [sem("srow_loaded0"), sem("srow_loaded1")]
        s_above = sem("above_made")
        s_sides = sem("sides_made")
        s_unit = sem("unit_multiplied")
        s_sums = sem("sums_made")
        s_quot = sem("quotients_made")
        s_out = sem("out_stored")

        s_kpass = sem("pass_scores_made")


        class E:
            pass
        E.weights, E.rows, E.stored = sem("e_weights_loaded"), sem("e_rows_loaded"), sem("e_attention_stored")
        E.hatt, E.whs, E.ready = sem("e_attention_loaded"), sem("e_wh_staged"), sem("e_constants_ready")
        E.whT_ps, E.whT = sem("e_whT_in_psum"), sem("e_whT_made")
        E.bc_ps, E.top, E.exp, E.ba = (sem(n) for n in ("e_bcdt_in_psum", "e_dt_max", "e_dt_exp", "e_ba_made"))
        E.baT_ps, E.baT, E.ab_ps, E.hsT = (sem(n) for n in ("e_baT_in_psum", "e_baT_made", "e_abT_in_psum",
                                                            "e_hsT_made"))
        E.hz_ps, E.z_tanh, E.uT = (sem(n) for n in ("e_hz_in_psum", "e_z_tanh", "e_uT_made"))
        E.out_ps, E.hs2, E.parts = sem("e_out_in_psum"), sem("e_hs2_made"), sem("e_parts_made")

        def wide_count(i, old):
            return i * (2 * ET) - (ET if old else 0)

        def T_count(i, n):
            return i * (3 * ET) - (2 - n) * ET

        E.wide_ps, E.var, E.rstd, E.norm = (sem(n) for n in ("e_wide_in_psum", "e_wide_var", "e_wide_rstd",
                                                             "e_wide_normed"))
        E.lin, E.tanh, E.silu = (sem(n) for n in ("e_wide_scaled", "e_wide_tanh", "e_wide_silu"))
        E.T_ps, E.T = sem("e_wideT_in_psum"), sem("e_wideT_made")
        E.fe2_ps, E.henh, E.g2_ps, E.gate_in, E.gate = (sem(n) for n in (
            "e_fe2_in_psum", "e_henh_made", "e_g2_in_psum", "e_gate_in", "e_gate_tanh"))
        E.fused, E.fvar, E.frstd, E.fnorm, E.x = (sem(n) for n in (
            "e_fused", "e_fused_var", "e_fused_rstd", "e_fused_normed", "e_x_made"))

        block = ctx.enter_context(nc.Block())
        SUMS = NG * H + 1

        @block.sync
        def _(sp):
            def load_vector(dst, src):
                sp.dma_start(dst, src.partition_broadcast(P)).then_inc(s_w, 16)

            def load_weights(l):
                if l == 0:
                    for k in range(2):
                        sp.dma_start(weights[:, k, 0:F].rearrange("p (h d) -> p h d", h=H),
                                     A["L0_gnn_W"][:, k * P:(k + 1) * P, :].rearrange("h p d -> p h d"))\
                            .then_inc(s_w, 16)
                    for s in range(2):
                        for hd in range(H):
                            load_vector(avec[:, s, hd * D:(hd + 1) * D], A["L0_gnn_a"][hd, s * D:(s + 1) * D, 0])
                    return
                sp.dma_start(weights[:, :, 0:F], A[f"L{l}_gnn_W"].rearrange("(k p) f -> p k f", p=P))\
                    .then_inc(s_w, 16)
                if l == 1:
                    for s, name in enumerate(("L1_gnn_a1", "L1_gnn_a2")):
                        for hd in range(H):
                            load_vector(avec[:, s, hd * D:(hd + 1) * D], A[name])
                elif l == 2:
                    load_vector(avec[:, 0, :], A["L2_gnn_a_src"][:, 0])
                    load_vector(avec[:, 1, :], A["L2_gnn_a_dst"][:, 0])
                else:
                    load_vector(avec[:, 0, :], A["L3_gnn_a"][:, 0])
                    load_vector(bvec[:, :], A["L3_gnn_b"])

            def load_adj(t):
                for half in range(2):
                    sp.wait_ge(s_adjbf, t * 2 + (half - 1))
                    sp.dma_start(adj_in[:, half, :], A["adj"][ds(t * P, P), half * 2048:(half + 1) * 2048])\
                        .then_inc(s_adj[half], 16)

            def score_rows(l):
                sp.wait_ge(s_src, l + 1)
                sp.dma_start(src_dram[l], srcT[:, :]).then_inc(s_srcst, 16)
                sp.wait_ge(s_srcst, 16 * (l + 1))
                flat = src_dram[l].rearrange("a b -> (a b)")

                def load(slot, grp):
                    sp.dma_start(srow[:, slot, :], flat[ds(grp * GI, GI)].partition_broadcast(P))\
                        .then_inc(s_srow[slot], 16)

                def load_next(gg, slot):
                    sp.wait_ge(s_above, (gg * 2 + (l * H * NG + slot - 1)) * BITS)
                    load(slot, gg * 2 + slot)

                first = 0
                if l == 0:
                    load(0, 0)
                    load(1, 1)
                    with sp.Fori(0, PACKING // 2) as gg:
                        for slot in range(2):
                            for i in range(GT):
                                load_adj(gg * (2 * GT) + (PACKED_FIRST + slot * GT + i))
                            load_next(gg + 1, slot)
                    first = 1 + PACKING // 2
                with sp.Fori(first, H * NG // 2) as gg:
                    for slot in range(2):
                        load_next(gg, slot)

            def dense2():
                def store(begin, end):
                    sp.dma_start(attn_dram[:, begin:end].rearrange("(t p) f -> p t f", p=P),
                                 attn2[:, :, begin:end]).then_inc(E.stored, 16)

                def load(*matrices):
                    for name, m in matrices:
                        sp.dma_start(m, A[f"L2_gnn_{name}"].rearrange("(k p) f -> p k f", p=P))\
                            .then_inc(E.weights, 16)

                sp.wait_ge(s_quot, 3 * H * NG - NG + CREDIT)
                store(0, F - D)
                sp.wait_ge(s_vals, values_before(3))
                sp.wait_ge(s_unit, (3 * H - 1) * UNITS + CREDIT)
                load(("W_bcdt", m_bcdt), ("fe1_w", m_fe1), ("W_hz", m_hz), ("fe2_w", m_fe2), ("out_w", m_out))
                sp.wait_ge(s_quot, 3 * H * NG + CREDIT)
                store(F - D, F)
                sp.wait_ge(s_unit, 3 * H * UNITS + CREDIT)
                load(("g1_w", m_g1), ("g2_w", m_g2))
                sp.dma_start(m_abp, A["L2_gnn_abp_w"]).then_inc(E.weights, 16)
                for name, c in (("abp_b", c_abp), ("b_hz", c_hz)):
                    sp.dma_start(c, A[f"L2_gnn_{name}"].rearrange("(c p) -> p c", p=P),
                                 allow_slow_non_contiguous=True).then_inc(E.rows, 16)
                for name, c in (("D", c_d), ("cp_b", c_cp)):
                    sp.dma_start(c, A[f"L2_gnn_{name}"].partition_broadcast(P)).then_inc(E.rows, 16)
                sp.wait_ge(E.stored, 32)
                for name, r in row.items():
                    src = A[f"L2_gnn_{name}"]
                    src = src[:, 0] if name == "cp_w" else src
                    sp.dma_start(r, src.partition_broadcast(P)).then_inc(E.rows, 16)

                def load_attention(g):
                    sp.dma_start(hatt, attn_dram[ds(g * EI, EI), :].rearrange("(t p) f -> p t f", p=P))\
                        .then_inc(E.hatt, 16)

                load_attention(0)
                with sp.Fori(1, EG) as g:
                    sp.wait_ge(E.T_ps, g * (3 * ET) - 2 * ET + ET)
                    sp.wait_ge(E.parts, g)
                    load_attention(g)

            sp.dma_start(x[:, :, :], A["x"].rearrange("(t p) f -> p t f", p=P)).then_inc(s_x, 16)
            load_weights(0)
            for half in range(2):
                sp.dma_start(adj_in[:, half, :], A["adj"][0:P, half * 2048:(half + 1) * 2048])\
                    .then_inc(s_adj[half], 16)
            with sp.Fori(1, PACKED_FIRST) as t:
                load_adj(t)
            for l in range(4):
                if l < 3:
                    score_rows(l)
                if l < min(3, last_layer):
                    sp.wait_ge(s_h, T * (l + 1) + 1)
                    load_weights(l + 1)
                if l == 2:
                    dense2()
                if l == last_layer:
                    break
            with sp.Fori(0, QUADS) as q:
                sp.wait_ge(s_xmade, q * QT + (T * (last_layer + 1) + QT))
                sp.dma_start(out[ds(q * (QT * P), QT * P), :].rearrange("(t p) f -> p t f", p=P),
                             x[:, ds(q * QT, QT), :]).then_inc(s_out, 16)
            sp.wait_ge(s_out, 16 * QUADS)

        loaded_weights = [16 * 10, 16 * 19, 16 * 22, 16 * 25]

        def value_parts(eng, chain, vtmp, kind, j0, n, p, slot):
            big, rest = vtmp[:, 0, 0:n, :], vtmp[:, 1, 0:n, :]
            e = emul[:, kind, ds(p, 1), ds(j0, n)].rearrange("p a n -> p n a")
            part = [values[:, slot, ds(j0, n), kind * KW + i * C:kind * KW + (i + 1) * C] for i in range(PARTS)]
            eng.tensor_copy(big[:, :, D:C], e)
            eng.tensor_tensor(big[:, :, 0:D], h[:, ds(j0, n), ds(p * D, D)],
                              e.to_broadcast([P, n, D]), ALU.mult).then_inc(chain.sem, 1)
            eng.wait_ge(chain.sem, chain.next())
            eng.nop(nofuse=True)
            eng.tensor_copy(part[0], big).then_inc(chain.sem, 1)
            eng.wait_ge(chain.sem, chain.next())
            eng.nop(nofuse=True)
            eng.tensor_tensor(rest, big, part[0], ALU.subtract).then_inc(chain.sem, 1)
            eng.wait_ge(chain.sem, chain.next())
            eng.nop(nofuse=True)
            eng.tensor_copy(part[1], rest).then_inc(chain.sem, 1)
            eng.wait_ge(chain.sem, chain.next())
            eng.nop(nofuse=True)
            return eng.tensor_tensor(part[2], rest, part[1], ALU.subtract)

        VALUE_LINKS = 4

        @block.gpsimd
        def _(pool):
            chain = Chain(s_pool)
            pool.memset(exponents[:, 1:1 + GT], -1.0)
            for i, signal in enumerate((s_quot, s_quot)):
                pool.memset(credits[:, i:i + 1], 0.0).then_inc(signal, 1)
            pool.memset(ident[:, :], 0.0).then_inc(s_pool, 1)
            pool.wait_ge(s_pool, chain.next())
            pool.affine_select(out=ident[:, :], in_=ident[:, :], compare_op=ALU.not_equal, fill=1.0,
                               base=0, pattern=[[-1, P]], channel_multiplier=1).then_inc(s_pool, 1)
            pool.wait_ge(s_pool, chain.next())
            pool.memset(minus_half, -0.5).then_inc(s_pool, 1)
            pool.wait_ge(s_pool, chain.next())
            for k in range(BITS):
                last = pool.tensor_scalar(powers[:, k, :], ident[:, :], float(2 ** k), None, ALU.mult)
            last.then_inc(s_const, 1)
            chain.settle()

            def make_rstd(l, q):
                pool.wait_ge(s_var, q + ((l - 1) * QUADS + 1))
                pool.nop(nofuse=True)
                pool.tensor_scalar(lnst[:, :, 8:9], lnst[:, :, 7:8], EPS, None, ALU.add).then_inc(s_pool, 1)
                pool.wait_ge(s_pool, chain.next())
                pool.tensor_tensor(lnst[:, :, 9:10], lnst[:, :, 8:9],
                                   minus_half.unsqueeze(2).to_broadcast([P, QT, 1]), ALU.pow)\
                    .then_inc(s_rstd, 1)

            def rstd_of_quads(l):
                with pool.Fori(0, QUADS) as q:
                    chain.enter(q, 1)
                    make_rstd(l, q)
                chain.leave(QUADS)

            def stage_x():
                pool.wait_ge(s_x, 16)
                with pool.Fori(0, QUADS) as q:
                    pool.wait_ge(s_xtps, q * 2 + 1)
                    pool.nop(nofuse=True)
                    pool.tensor_copy(xs, x[:, ds(q * QT, QT), :]).then_inc(s_xmade, QT)

            def global_max(l):
                n = H if l < 3 else 1
                pool.wait_ge(s_pmax, l + 1)
                pool.partition_all_reduce(smax[:, 1, 0:n], smax[:, 0, 0:n], P, RMAX).then_inc(s_max, 1)

            def first_values(l):
                if l < 3:
                    pool.wait_ge(s_exps, l + 1)
                else:
                    pool.wait_ge(s_emul, 1)
                with pool.Fori(0, POOL_CHUNKS[l]) as c:
                    chain.enter(c, VALUE_LINKS)
                    value_parts(pool, chain, vtmp_pool, 0, c * CHUNK, CHUNK, 0, 0).then_inc(s_vals, 1)
                chain.leave(POOL_CHUNKS[l])

            def quotient(l, p, g, par):
                target = attn2 if l == 2 else h
                pool.wait_ge(s_sums, p * NG + g + (l * SUMS + 3))
                pool.nop(nofuse=True)
                dst = target[:, ds(g * GT, GT), ds(p * D, D)]
                if l < 3:
                    c = [cmul[:, s, ds(p, 1), ds(g * GT, GT)].rearrange("p a n -> p n a")
                         .to_broadcast([P, GT, C]) for s in range(2)]
                    pool.tensor_tensor(quot[:, 0], sums[:, par, :, 0, :], c[0], ALU.mult)
                    pool.tensor_tensor(quot[:, 1], sums[:, par, :, 1, :], c[1], ALU.mult)\
                        .then_inc(s_pool, 1)
                    pool.wait_ge(s_pool, chain.next())
                    pool.nop(nofuse=True)
                    pool.tensor_tensor(quot[:, 2], quot[:, 0], quot[:, 1], ALU.add).then_inc(s_pool, 1)
                    pool.wait_ge(s_pool, chain.next())
                    pool.nop(nofuse=True)
                    total, inverse = quot[:, 2], quot[:, 0, :, 0:1]
                    pool.tensor_tensor(inverse, total[:, :, D:C], minus_one, ALU.pow)\
                        .then_inc(s_pool, 1)
                    pool.wait_ge(s_pool, chain.next())
                    pool.nop(nofuse=True)
                else:
                    total, inverse = sums[:, par, :, 0, :], quot[:, 1, :, 0:1]
                    pool.tensor_scalar(quot[:, 0, :, 0:1], total[:, :, D:C],
                                       2e-38, None, ALU.max).then_inc(s_pool, 1)
                    pool.wait_ge(s_pool, chain.next())
                    pool.nop(nofuse=True)
                    pool.tensor_tensor(inverse, quot[:, 0, :, 0:1], minus_one, ALU.pow)\
                        .then_inc(s_pool, 1)
                    pool.wait_ge(s_pool, chain.next())
                    pool.nop(nofuse=True)
                done = pool.tensor_tensor(dst, total[:, :, 0:D],
                                          inverse.to_broadcast([P, GT, D]), ALU.mult)
                done.then_inc(s_quot, 1)

            def attention(l):
                kinds = 2 if l < 3 else 1
                per_group = VALUE_LINKS * kinds + (3 if l < 3 else 2)
                for p in range(H if l < 3 else H - 1):
                    links = per_group - (0 if p < H - 1 else VALUE_LINKS * kinds)
                    if p < H - 1:
                        pool.wait_ge(s_unit, p * UNITS + (CREDIT + l * H * UNITS))
                    with pool.Fori(0, NG // 2) as gg:
                        for par in range(2):
                            g = gg * 2 + par
                            chain.enter(g, links)
                            if p < H - 1:
                                for kind in range(kinds):
                                    made = value_parts(pool, chain, vtmp_pool, kind, g * GT, GT, p + 1, 1 - p % 2)
                                made.then_inc(s_vals, 1)
                            quotient(l, p, g, par)
                    chain.leave(NG)
                if l < 3:
                    return
                quotient(3, H - 1, 0, 0)
                quotient(3, H - 1, 1, 1)
                make_rstd(4, 0)
                chain.settle()
                with pool.Fori(1, NG // 2) as gg:
                    chain.enter(gg - 1, 2 * (2 + 1))
                    for par in range(2):
                        quotient(3, H - 1, gg * 2 + par, par)
                        make_rstd(4, gg * 2 + (par - 1))
                chain.leave(NG // 2 - 1)
                make_rstd(4, QUADS - 1)
                chain.settle()

            def rstd(stats, waits, at, signal):
                pool.wait_ge(waits, at)
                pool.nop(nofuse=True)
                pool.tensor_scalar(stats[:, 8:9], stats[:, 7:8], EPS, None, ALU.add).then_inc(s_pool, 1)
                pool.wait_ge(s_pool, chain.next())
                pool.nop(nofuse=True)
                pool.tensor_tensor(stats[:, 9:10], stats[:, 8:9], minus_half, ALU.pow).then_inc(signal, 1)

            def dense2():
                pool.wait_ge(E.stored, 32)
                pool.wait_ge(E.rows, 16 * (4 + len(row)))

                def scale_wide(at, tiles, gain, shift):
                    for t in range(ET):
                        pool.wait_ge(E.norm, at + (t + 1))
                        pool.tensor_tensor(tiles[:, t, :], tiles[:, t, :], row[gain], ALU.mult).then_inc(s_pool, 1)
                        pool.wait_ge(s_pool, chain.next())
                        pool.tensor_tensor(tiles[:, t, :], tiles[:, t, :], row[shift], ALU.add).then_inc(E.lin, 1)

                def step(i, new, old):
                    if old:
                        for t in range(ET):
                            rstd(est[:, 1, t, :], E.var, wide_count(i, 1) + (t + 1), E.rstd)
                        scale_wide(wide_count(i, 1), wide_g, "g_ln_g", "g_ln_b")
                    if new:
                        for t in range(ET):
                            rstd(est[:, 0, t, :], E.var, wide_count(i, 0) + (t + 1), E.rstd)
                        scale_wide(wide_count(i, 0), wide, "fe_ln_g", "fe_ln_b")
                    if old:
                        pool.wait_ge(E.hatt, i * 16)
                        pool.wait_ge(E.henh, i)
                        pool.tensor_tensor(fused, hatt, hs2, ALU.subtract)
                        pool.tensor_tensor(base, henh, hs2, ALU.add).then_inc(E.parts, 1)
                        pool.wait_ge(E.gate, i)
                        pool.nop(nofuse=True)
                        pool.tensor_scalar(gate, gate, 0.5, 0.5, ALU.mult, ALU.add).then_inc(s_pool, 1)
                        pool.wait_ge(s_pool, chain.next())
                        pool.tensor_tensor(fused, fused, gate, ALU.mult).then_inc(s_pool, 1)
                        pool.wait_ge(s_pool, chain.next())
                        pool.tensor_tensor(fused, fused, base, ALU.add).then_inc(E.fused, 1)
                        for t in range(ET):
                            rstd(est[:, 2, t, :], E.fvar, (i - 1) * ET + (t + 1), E.frstd)
                        for t in range(ET):
                            pool.wait_ge(E.fnorm, (i - 1) * ET + (t + 1))
                            pool.tensor_tensor(fused[:, t, :], fused[:, t, :], row["ln_g"], ALU.mult)\
                                .then_inc(s_pool, 1)
                            pool.wait_ge(s_pool, chain.next())
                            pool.tensor_tensor(fused[:, t, :], fused[:, t, :], row["ln_b"], ALU.add)\
                                .then_inc(s_pool, 1)
                            xt = x[:, ds((i - 1) * ET + t, 1), :]
                            pool.wait_ge(s_pool, chain.next())
                            pool.nop(nofuse=True)
                            pool.tensor_tensor(xt, xt, fused[:, t:t + 1, :], ALU.add).then_inc(E.x, 1)

                step(0, True, False)
                chain.settle()
                with pool.Fori(1, EG) as i:
                    chain.enter(i - 1, 2 * ET + 2 * ET + 2 + 3 * ET)
                    step(i, True, True)
                chain.leave(EG - 1)
                step(EG, False, True)
                chain.settle()

            for l in range(last_layer + 1):
                if l == 3:
                    dense2()
                if l > 0:
                    rstd_of_quads(l)
                else:
                    stage_x()
                global_max(l)
                first_values(l)
                attention(l)
            if last_layer == 2:
                dense2()
            if last_layer < 3:
                rstd_of_quads(last_layer + 1)

        @block.scalar
        def _(act):
            def dense(l, q):
                for half in range(2):
                    act.wait_ge(s_xtps, q * 2 + (l * 2 * QUADS + half + 2))
                    act.activation(xT[:, 2 * half:2 * half + 2].rearrange("p t k n -> p (t k n)"), bank[half][:, :],
                                   ACT.Copy).then_inc(s_xt, 1)
                if l > 0:
                    act.wait_ge(s_xmade, q * QT + (l * T + QT))
                    act.activation(x[:, ds(q * QT, QT), :], xs, ACT.Copy).then_inc(s_xkept, 1)
                for i in range(QT):
                    act.wait_ge(s_hps, q * QT + (l * T + i + 1))
                    to_h = act.activation(h[:, ds(q * QT + i, 1), :], bank[2 + i][:, 0:F].unsqueeze(1), ACT.Copy)
                    if l < 3:
                        to_h = act.activation(scores[:, :, ds(q * QT + i, 1)],
                                              bank[2 + i][:, F:F + 2 * H].unsqueeze(2), ACT.Copy)
                    to_h.then_inc(s_h, 1)

            def tanh_rows(q):
                act.wait_ge(s_tanhin, q + 1)
                for i in range(QT):
                    last = act.activation(ex[:, i, :], low[:, i, :], ACT.Tanh,
                                          accum_out=scores[:, 0, ds(q * QT + i, 1)])
                last.then_inc(s_tanh, 1)

            def elu_exp(q):
                act.wait_ge(s_elumin, q + 1)
                act.activation(ex, low, ACT.Exp).then_inc(s_eluexp, 1)

            def stats(l):
                if l < 3:
                    act.wait_ge(s_srcps, l + 1)
                    act.activation(srcT[:, :], bank[4][:, 0:P], ACT.Copy).then_inc(s_src, 1)
                act.wait_ge(s_shift, l + 1)
                e, c = (m[:, :, :, :].rearrange("p k h t -> p k (h t)") for m in (emul, cmul))
                if l < 3:
                    act.activation(e[:, 1], e[:, 0], ACT.Exp, scale=SLOPES[l])
                    act.activation(e[:, 0], e[:, 0], ACT.Exp)
                    act.activation(c, c, ACT.Exp).then_inc(s_exps, 1)
                else:
                    act.activation(emul[:, 0, 0, :], emul[:, 0, 0, :], ACT.Exp).then_inc(s_exps, 1)

            def attention(l):
                with act.Fori(0, H // 2) as pp:
                    for slot in range(2):
                        p = pp * 2 + slot
                        act.activation(kpass[:, slot:slot + 1, :], kscores[:, ds(p, 1), :], ACT.Copy)\
                            .then_inc(s_kpass, 1)
                        act.wait_ge(s_kpass, p + (l * H + 1))
                        act.nop(nofuse=True)
                        with act.Fori(0, NG // 2) as gg:
                            for par in range(2):
                                act.wait_ge(s_srow[par], (p * (NG // 2) + gg + (l * H * NG // 2 + 1)) * 16)
                                act.nop(nofuse=True)
                                for k in range(BITS):
                                    act.wait_ge(s_sides, (p * NG + gg * 2) * BITS
                                                + (l * H * UNITS + par * BITS + k - 1 + CREDIT))
                                    act.nop(nofuse=True)
                                    for q in range(Q):
                                        last = act.activation(
                                            above[:, k % 2, q, :], srow[:, par, :], ACT.Relu, scale=BIG,
                                            bias=kpass[:, slot, q * BITS + k:q * BITS + k + 1], saturate=False)
                                    last.then_inc(s_above, 1)

            def dense2():
                act.wait_ge(E.ready, 1)

                def copy_T(at, scale):
                    for t in range(ET):
                        act.wait_ge(E.T_ps, at + (t + 1))
                        act.activation(wideT[:, t].rearrange("p k n -> p (k n)"), bank[(7, 5)[t]][:, :],
                                       ACT.Copy, scale=scale).then_inc(E.T, 1)

                def tanhs(at, out_tiles, tiles):
                    for t in range(ET):
                        act.wait_ge(E.lin, at + (t + 1))
                        act.activation(out_tiles[t], tiles[:, t, :], ACT.Tanh, scale=0.5).then_inc(E.tanh, 1)

                def gates(i, b):
                    act.wait_ge(E.hz_ps, i * 4 + b + 1)
                    if b >= 2:
                        act.wait_ge(E.uT, i * 4 + (b - 1))
                    act.activation(h_part[:, b % 2, :], bank[1 + b % 2][:, 0:EI], ACT.Identity,
                                   bias=c_hz[:, b:b + 1])
                    act.activation(z_part[:, b % 2, :], bank[1 + b % 2][:, EI:2 * EI], ACT.Identity,
                                   bias=c_hz[:, 4 + b:5 + b])
                    act.activation(z_tanh[:, b % 2, :], bank[1 + b % 2][:, EI:2 * EI], ACT.Tanh, scale=0.5,
                                   bias=c_hz_half[:, b:b + 1]).then_inc(E.z_tanh, 1)

                def step(i, new, old):
                    if new:
                        act.activation(whs, h[:, ds(i * ET, ET), :], ACT.Copy).then_inc(E.whs, 1)
                        act.wait_ge(E.whT_ps, i + 1)
                        act.activation(whT.rearrange("p k n -> p (k n)"), bank[0][:, :], ACT.Copy).then_inc(E.whT, 1)
                    if old:
                        if new:
                            act.wait_ge(E.fe2_ps, i)
                        copy_T(T_count(i, 0), 1.0)
                    if new:
                        for t in range(ET):
                            act.wait_ge(E.top, i * ET + t + 1)
                            act.activation(dt_exp[:, t, :], bcdt[:, t, 2 * SD:3 * SD], ACT.Exp,
                                           bias=ecol[:, 16 + t:17 + t], accum_out=ecol[:, 18 + t:19 + t])\
                                .then_inc(E.exp, 1)
                        act.wait_ge(E.baT_ps, i + 1)
                        act.activation(baT, bank[5][:, 0:EI], ACT.Copy).then_inc(E.baT, 1)
                        for b in range(2):
                            gates(i, b)
                    if old:
                        tanhs(wide_count(i, 1), wide_g_tanh, wide_g)
                        act.wait_ge(E.wide_ps, wide_count(i, 1) + ET)
                        copy_T(T_count(i, 1), 0.5)
                    if new:
                        for b in range(2, 4):
                            gates(i, b)
                        tanhs(wide_count(i, 0), [wide_tanh[:, t, :] for t in range(ET)], wide)
                    if new:
                        if old:
                            act.wait_ge(E.g2_ps, i)
                        copy_T(T_count(i, 2), 0.5)
                    if old:
                        act.wait_ge(E.gate_in, i)
                        act.activation(gate, gate, ACT.Tanh, scale=0.5).then_inc(E.gate, 1)

                step(0, True, False)
                with act.Fori(1, EG) as i:
                    step(i, True, True)
                step(EG, False, True)

            for l in range(last_layer + 1):
                if l == 3:
                    dense2()
                if l == 1:
                    elu_exp(0)
                    with act.Fori(1, QUADS) as q:
                        elu_exp(q)
                        dense(l, q - 1)
                    dense(l, QUADS - 1)
                elif l == 3:
                    dense(l, 0)
                    with act.Fori(1, QUADS) as q:
                        tanh_rows(q - 1)
                        dense(l, q)
                    tanh_rows(QUADS - 1)
                else:
                    with act.Fori(0, QUADS) as q:
                        dense(l, q)
                stats(l)
                if l < 3:
                    attention(l)
            if last_layer == 2:
                dense2()
            if last_layer == 0:
                with act.Fori(0, QUADS) as q:
                    elu_exp(q)

        @block.tensor
        def _(pe):
            def dense(l, q):
                for half in range(2):
                    for i in (2 * half, 2 * half + 1):
                        pe.wait_ge(s_xmade, q * QT + (l * T + i + 1))
                        for k in range(2):
                            last = pe.transpose(bank[half][:, (i % 2 * 2 + k) * P:(i % 2 * 2 + k + 1) * P],
                                                xs[:, i, k * P:(k + 1) * P], ident[:, :])
                    last.then_inc(s_xtps, 1)
                pe.wait_ge(s_h, q * QT + (l * T + 1))
                width = F + 2 * H if l < 3 else F
                for i in range(QT):
                    pe.wait_ge(s_xt, q * 2 + (l * 2 * QUADS + i // 2 + 1))
                    for k in range(2):
                        last = pe.matmul(bank[2 + i][:, 0:width], xT[:, i, k, :], weights[:, k, 0:width],
                                         start=(k == 0), stop=(k == 1))
                    last.then_inc(s_hps, 1)

            def pack(t):
                for half in range(2):
                    pe.wait_ge(s_adjbf, t * 2 + half + 1)
                    pe.wait_ge(s_packed, t * 2 + (half + 1))
                    pe.nop(nofuse=True)
                    for q in range(2):
                        for k in range(BITS):
                            j = q * BITS + k
                            last = pe.matmul(bank[6 + half][:, q * P:(q + 1) * P],
                                             adj_bf[:, half, j * P:(j + 1) * P], powers[:, k, :],
                                             start=(k == 0), stop=(k == BITS - 1))
                    last.then_inc(s_packmm, 1)

            def src_rows(l):
                pe.wait_ge(s_h, T * (l + 1) + 1)
                pe.transpose(bank[4][:, 0:P], scores[:, 0:H, :].rearrange("p h t -> p (h t)"), ident[:, :])\
                    .then_inc(s_srcps, 1)

            def group(l, slot, par, at, packing=None):
                for k in range(BITS):
                    pe.wait_ge(s_sides, at * BITS + (l * H * UNITS + k + 1 + CREDIT))
                    pe.nop(nofuse=True)
                    for q in range(Q):
                        v = values[:, slot, q * BITS + k, :]
                        first, final = (k == 0 and q == 0), (k == BITS - 1 and q == Q - 1)
                        for it in range(GT):
                            acc = bank[GT * par + it]
                            rows = slice(it * P, (it + 1) * P)
                            if l < 3:
                                pe.matmul(acc[:, 0:KW], pos[:, k % 2, q, :].bitcast(FP8)[:, rows], v[:, 0:KW],
                                          start=first, stop=final, skip_group_check=True)
                                last = pe.matmul(acc[:, KW:2 * KW], neg[:, k % 2, q, :].bitcast(FP8)[:, rows],
                                                 v[:, KW:2 * KW], start=False, stop=final, skip_group_check=True)
                            else:
                                last = pe.matmul(acc[:, 0:KW], edge[:, k % 2, q, :].bitcast(FP8)[:, rows],
                                                 v[:, 0:KW], start=first, stop=final)
                    last.then_inc(s_unit, 1)
                    if packing is not None and k % 2 == 0:
                        pack(packing + k // 2)

            def one_pass(l, slot, p):
                pe.wait_ge(s_vals, p * NG + (values_before(l) + POOL_CHUNKS[l]))
                pe.nop(nofuse=True)
                with pe.Fori(0, NG // 2) as gg:
                    for par in range(2):
                        pe.wait_ge(s_sums, p * NG + gg * 2 + (l * SUMS + par + 1))
                        pe.nop(nofuse=True)
                        group(l, slot, par, p * NG + gg * 2 + par)

            def attention(l):
                pe.wait_ge(s_vfirst, sum(FIRST_CHUNKS - POOL_CHUNKS[m] for m in range(l + 1)))
                if l > 0:
                    with pe.Fori(0, H // 2) as pp:
                        for slot in range(2):
                            one_pass(l, slot, pp * 2 + slot)
                    return
                pe.wait_ge(s_vals, POOL_CHUNKS[0])
                for begin, end in ((0, PACKING), (PACKING, NG)):
                    with pe.Fori(begin, end) as g:
                        pe.wait_ge(s_sums, g + 2)
                        pe.nop(nofuse=True)
                        group(0, 0, 0, g, g * GT + PACKED_FIRST if begin == 0 else None)
                pe.wait_ge(s_sums, NG + 2)
                for p in range(1, H):
                    one_pass(0, p % 2, p)

            def dense2():
                pe.wait_ge(E.weights, 16 * 8)

                def product(dst, lhsT, rhs):
                    for k in range(len(lhsT)):
                        last = pe.matmul(dst, lhsT[k], rhs[k], start=(k == 0), stop=(k == len(lhsT) - 1))
                    return last

                def rows(m, t):
                    return [m[:, k, t * P:(t + 1) * P] for k in range(m.shape[1])]

                def blocks(m, a=None, b=None):
                    return [m[:, k, a:b] for k in range(m.shape[1])]

                def transposes(t, sources):
                    for i, src in enumerate(sources):
                        last = pe.transpose(bank[(7, 5)[t]][:, i * P:(i + 1) * P], src, ident[:, :])
                    last.then_inc(E.T_ps, 1)

                def cut(tile, n):
                    return [tile[:, i * P:(i + 1) * P] for i in range(n)]

                def g1_product(i, t):
                    pe.wait_ge(E.T, T_count(i, 0) + (t + 1))
                    product(bank[3 + t][:, :], blocks(wideT[:, t]), blocks(m_g1)).then_inc(E.wide_ps, 1)

                def step(i, new, old):
                    if new:
                        pe.wait_ge(E.whs, i + 1)
                        if old:
                            pe.wait_ge(E.hs2, i)
                        for k in range(2):
                            for t in range(ET):
                                last = pe.transpose(bank[0][:, k * EI + t * P:k * EI + (t + 1) * P],
                                                    whs[:, t, k * P:(k + 1) * P], ident[:, :])
                        last.then_inc(E.whT_ps, 1)
                    if old:
                        pe.wait_ge(E.hatt, i * 16)
                        pe.wait_ge(E.hs2, i)
                        if new:
                            pe.wait_ge(E.T, T_count(i, 0))
                        for t in range(ET):
                            transposes(t, cut(hatt[:, t, :], 2) + cut(hs2[:, t, :], 2))
                    if new:
                        if old:
                            pe.wait_ge(E.henh, i)
                        pe.wait_ge(E.whT, i + 1)
                        for t in range(ET):
                            product(bank[1 + t][:, 0:3 * SD], rows(whT, t), blocks(m_bcdt)).then_inc(E.bc_ps, 1)
                    if old:
                        g1_product(i, 0)
                    if new:
                        if old:
                            pe.wait_ge(E.T, T_count(i, 0) + ET)
                        pe.wait_ge(E.ba, (i + 1) * ET)
                        for t in range(ET):
                            last = pe.transpose(bank[5][:, t * P:(t + 1) * P], ba[:, t, :], ident[:, :])
                        last.then_inc(E.baT_ps, 1)
                    if old:
                        g1_product(i, 1)
                    if new:
                        pe.wait_ge(E.baT, i + 1)
                        for b in range(2):
                            last = pe.matmul(bank[6][:, b * EI:(b + 1) * EI], m_abp[:, b * P:(b + 1) * P], baT,
                                             start=True, stop=True)
                        last.then_inc(E.ab_ps, 1)
                        for t in range(ET):
                            if old:
                                pe.wait_ge(E.var, wide_count(i, 1) + (t + 1))
                            product(bank[3 + t][:, :], rows(whT, t), blocks(m_fe1)).then_inc(E.wide_ps, 1)
                        pe.wait_ge(E.hsT, i + 1)
                        for b in range(4):
                            if b >= 2:
                                pe.wait_ge(E.z_tanh, i * 4 + (b - 1))
                            for part in range(2):
                                c = part * DI + b * P
                                last = product(bank[1 + b % 2][:, part * EI:(part + 1) * EI],
                                               blocks(m_hz, c, c + P), blocks(hsT))
                            last.then_inc(E.hz_ps, 1)
                    if old:
                        for t in range(ET):
                            pe.wait_ge(E.silu, wide_count(i, 1) + (t + 1))
                            transposes(t, cut(wide_g[:, t, :], 4))
                        for t in range(ET):
                            pe.wait_ge(E.T, T_count(i, 1) + (t + 1))
                            last = product(bank[6][:, t * F:(t + 1) * F], blocks(wideT[:, t]), blocks(m_g2))
                        last.then_inc(E.g2_ps, 1)
                    if new:
                        pe.wait_ge(E.uT, (i + 1) * 4)
                        for t in range(ET):
                            last = product(bank[0][:, t * F:(t + 1) * F], rows(uT, t), blocks(m_out))
                        last.then_inc(E.out_ps, 1)
                        for t in range(ET):
                            pe.wait_ge(E.silu, wide_count(i, 0) + (t + 1))
                            transposes(t, cut(wide[:, t, :], 4))
                        for t in range(ET):
                            pe.wait_ge(E.T, T_count(i, 2) + (t + 1))
                            last = product(bank[2][:, t * F:(t + 1) * F], blocks(wideT[:, t]), blocks(m_fe2))
                        last.then_inc(E.fe2_ps, 1)

                step(0, True, False)
                with pe.Fori(1, EG) as i:
                    step(i, True, True)
                step(EG, False, True)

            pe.wait_ge(s_const, 2)
            pe.wait_ge(s_x, 16)
            for i, signal in enumerate((s_unit, s_unit, s_packmm, s_packmm, s_xtps)):
                pe.transpose(bank[i][:, 0:P], ident[:, :], ident[:, :]).then_inc(signal, 1)
            for l in range(last_layer + 1):
                if l == 3:
                    dense2()
                pe.wait_ge(s_wfix, l + 1)
                with pe.Fori(0, QUADS) as q:
                    dense(l, q)
                    if l == 0:
                        pack(q)
                if l < 3:
                    src_rows(l)
                attention(l)
            if last_layer == 2:
                dense2()

        @block.vector
        def _(dve):
            chain = Chain(s_dve)

            def fold_weights(l):
                dve.wait_ge(s_w, loaded_weights[l])
                for k in range(2):
                    for s in range(2):
                        if l < 3:
                            product = prod[:, s, :]
                            dve.tensor_tensor(product, weights[:, k, 0:F], avec[:, s, :], ALU.mult).then_inc(s_dve, 1)
                            dve.wait_ge(s_dve, chain.next())
                            col = F + s * H
                            if l < 2:
                                dve.tensor_reduce(weights[:, k, col:col + H],
                                                  product.rearrange("p (h d) -> p h d", h=H), AX.X, ALU.add)\
                                    .then_inc(s_dve, 1)
                                dve.wait_ge(s_dve, chain.next())
                            else:
                                for hd in range(H):
                                    dve.tensor_reduce(weights[:, k, col + hd:col + hd + 1], product,
                                                      AX.X, ALU.add).then_inc(s_dve, 1)
                                    dve.wait_ge(s_dve, chain.next())
                chain.settle()
                dve.memset(credits[:, 8 + l:9 + l], 0.0).then_inc(s_wfix, 1)

            def convert(t):
                for half in range(2):
                    dve.wait_ge(s_adj[half], (t + 1) * 16)
                    dve.wait_ge(s_packmm, t * 2 + (half + 1))
                    dve.tensor_scalar(adj_bf[:, half, :], adj_in[:, half, :], 0, None, ALU.is_gt)\
                        .then_inc(s_adjbf, 1)

            def store_packed(t):
                for half in range(2):
                    dve.wait_ge(s_packmm, t * 2 + (half + 1 + CREDIT))
                    dve.tensor_copy(packed_bytes[:, 2 * half:2 * half + 2, ds(t * P, P)],
                                    bank[6 + half][:, 0:2 * P].rearrange("p (q n) -> p q n", q=2))\
                        .then_inc(s_packed, 1)

            def pack(t):
                convert(t)
                store_packed(t)

            def norm_first(l, q):
                if l == 1:
                    dve.tensor_scalar(low, h[:, ds(q * QT, QT), :], 0.0, None, ALU.min).then_inc(s_elumin, 1)

            def norm_stats(l, q):
                xq, hq = (m[:, ds(q * QT, QT), :] for m in (x, h))
                if l == 1:
                    dve.wait_ge(s_eluexp, q + 1)
                    dve.tensor_tensor(low, hq, low, ALU.subtract).then_inc(s_dve, 1)
                    dve.wait_ge(s_dve, chain.next())
                    dve.scalar_tensor_tensor(out=ex, in0=ex, scalar=-1.0, in1=low, op0=ALU.add, op1=ALU.add)\
                        .then_inc(s_dve, 1)
                    dve.wait_ge(s_dve, chain.next())
                    dve.tensor_tensor(xq, xq, ex, ALU.add).then_inc(s_dve, 1)
                    dve.wait_ge(s_dve, chain.next())
                    dve.nop(nofuse=True)
                elif l in (2, 4):
                    dve.tensor_tensor(xq, xq, hq, ALU.add).then_inc(s_dve, 1)
                    dve.wait_ge(s_dve, chain.next())
                    dve.nop(nofuse=True)
                for i in range(QT):
                    last = dve.bn_stats(lnst[:, i, 0:6], x[:, ds(q * QT + i, 1), :].squeeze(1))
                last.then_inc(s_dve, 1)
                dve.wait_ge(s_dve, chain.next())
                dve.nop(nofuse=True)
                for i in range(QT):
                    last = dve.bn_aggr(lnst[:, i, 6:8], lnst[:, i, 0:6])
                last.then_inc(s_var, 1)

            def normalize(l, q):
                if l <= last_layer:
                    dve.wait_ge(s_xtps, q * 2 + (l * 2 * QUADS + 1))
                    if isinstance(q, int) and q == 0:
                        if l > 1:
                            dve.wait_ge(s_xkept, (l - 1) * QUADS)
                    else:
                        dve.wait_ge(s_xkept, q + (l - 1) * QUADS)
                dve.wait_ge(s_rstd, q + ((l - 1) * QUADS + 1))
                for i in range(QT):
                    xt = x[:, ds(q * QT + i, 1), :]
                    normed = xs[:, i:i + 1, :] if l <= last_layer else xt
                    dve.tensor_scalar(normed, xt, lnst[:, i, 6:7], lnst[:, i, 9:10], ALU.subtract, ALU.mult)\
                        .then_inc(s_xmade, 1)

            def between(l):
                norm_first(l, 0)
                norm_stats(l, 0)
                if l == 3:
                    normalize(l, 0)
                    norm_stats(l, 1)
                    chain.settle()
                    with dve.Fori(2, QUADS) as q:
                        chain.enter(q - 2, NORM_LINKS[l] + 2)
                        normalize(l, q - 1)
                        tanh_in(q - 2)
                        norm_stats(l, q)
                        tanh_scores(q - 2)
                    chain.leave(QUADS - 2)
                    normalize(l, QUADS - 1)
                    for q in (QUADS - 2, QUADS - 1):
                        tanh_in(q)
                        tanh_scores(q)
                    chain.settle()
                    return
                chain.settle()
                with dve.Fori(1, QUADS) as q:
                    chain.enter(q - 1, NORM_LINKS[l])
                    norm_first(l, q)
                    normalize(l, q - 1)
                    norm_stats(l, q)
                chain.leave(QUADS - 1)
                normalize(l, QUADS - 1)

            def tanh_in(q):
                dve.wait_ge(s_h, q * QT + (3 * T + 1 + QT))
                dve.tensor_tensor(low, h[:, ds(q * QT, QT), :], bvec[:, :].unsqueeze(1).to_broadcast([P, QT, F]),
                                  ALU.add).then_inc(s_tanhin, 1)

            def tanh_scores(q):
                dve.wait_ge(s_tanh, q + 1)
                dve.tensor_tensor(low, ex, avec[:, 0:1, :].to_broadcast([P, QT, F]), ALU.mult).then_inc(s_dve, 1)
                dve.wait_ge(s_dve, chain.next())
                dve.tensor_reduce(scores[:, H, ds(q * QT, QT)], low, AX.X, ALU.add).then_inc(s_dve, 1)
                dve.wait_ge(s_dve, chain.next())

            def rest_of_first_values(l):
                with dve.Fori(POOL_CHUNKS[l], FIRST_CHUNKS) as c:
                    chain.enter(c - POOL_CHUNKS[l], VALUE_LINKS)
                    value_parts(dve, chain, vtmp_dve, 0, c * CHUNK, CHUNK, 0, 0).then_inc(s_vfirst, 1)
                chain.leave(FIRST_CHUNKS - POOL_CHUNKS[l])
                dve.wait_ge(s_vfirst, sum(FIRST_CHUNKS - POOL_CHUNKS[m] for m in range(l + 1)))

            def stats(l):
                n = H if l < 3 else 1
                if l < 3:
                    dve.wait_ge(s_h, T * (l + 1) + 1)
                src, dst = scores[:, 0:H, :], scores[:, H:H + n, :]
                dve.tensor_reduce(smax[:, 0, 0:n], dst, AX.X, ALU.max).then_inc(s_pmax, 1)
                dve.wait_ge(s_max, l + 1)
                top = smax[:, 1, 0:n].unsqueeze(2).to_broadcast([P, n, T])
                shifted = dve.tensor_tensor(emul[:, 0, 0:n, :], dst, top, ALU.subtract)
                if l == 3:
                    shifted.then_inc(s_shift, 1)
                    dve.tensor_scalar(zrow[:, 0, 0, :], scores[:, 0, :], 0.0, None, ALU.not_equal).then_inc(s_dve, 1)
                    dve.wait_ge(s_dve, chain.next())
                    dve.wait_ge(s_exps, 4)
                    for hd in range(1, H):
                        last = dve.tensor_tensor(emul[:, 0, hd, :], emul[:, 0, 0, :], zrow[:, 0, 0, :], ALU.mult)
                    last.then_inc(s_dve, 1)
                    dve.wait_ge(s_dve, chain.next())
                    dve.tensor_copy(emul[:, 0, 0, :], emul[:, 0, 1, :]).then_inc(s_emul, 1)
                    chain.settle()
                    dve.wait_ge(s_emul, 1)
                    rest_of_first_values(l)
                    return
                z, az, m = (zrow[:, i] for i in range(3))
                dve.tensor_tensor(z, src, top, ALU.add).then_inc(s_dve, 1)
                dve.wait_ge(s_dve, chain.next())
                dve.tensor_scalar(az, z, SLOPES[l], None, ALU.mult).then_inc(s_dve, 1)
                dve.wait_ge(s_dve, chain.next())
                dve.tensor_tensor(m, z, az, ALU.max).then_inc(s_dve, 1)
                dve.wait_ge(s_dve, chain.next())
                dve.tensor_tensor(cmul[:, 0], z, m, ALU.subtract)
                dve.tensor_tensor(cmul[:, 1], az, m, ALU.subtract)
                dve.tensor_scalar(kscores[:, :, :], dst, BIG, None, ALU.mult).then_inc(s_shift, 1)
                chain.settle()
                dve.wait_ge(s_exps, l + 1)
                with dve.Fori(0, FIRST_CHUNKS) as c:
                    chain.enter(c, VALUE_LINKS + 1)
                    value_parts(dve, chain, vtmp_dve, 1, c * CHUNK, CHUNK, 0, 0).then_inc(s_dve, 1)
                    dve.wait_ge(s_dve, chain.next())
                chain.leave(FIRST_CHUNKS)
                rest_of_first_values(l)

            def evacuate(l, half, slot, count):
                kinds = 2 if l < 3 else 1
                dve.wait_ge(s_unit, count * BITS + (l * H * UNITS + CREDIT))
                dve.wait_ge(s_quot, count + (l * H * NG + CREDIT - 1))
                for it in range(GT):
                    parts = bank[GT * half + it][:, 0:kinds * KW].rearrange("p (k a c) -> p k c a", k=kinds, a=PARTS)
                    last = dve.tensor_reduce(sums[:, slot, it, 0:kinds, :], parts, AX.X, ALU.add)
                last.then_inc(s_sums, 1)

            LINKS = {0: 2 * BITS, 1: 2 * BITS, 2: 2 * BITS, 3: 0}

            def output_norm(q, k):
                xq, hq = (m[:, ds(q * QT, QT), :] for m in (x, h))
                if k == 2:
                    dve.wait_ge(s_quot, q + (4 * H * NG - NG + 1 + CREDIT))
                    dve.tensor_tensor(xq, xq, hq, ALU.add).then_inc(s_dve, 1)
                elif k == 3:
                    dve.wait_ge(s_dve, chain.next())
                    dve.nop(nofuse=True)
                    for i in range(QT):
                        last = dve.bn_stats(lnst[:, i, 0:6], x[:, ds(q * QT + i, 1), :].squeeze(1))
                    last.then_inc(s_dve, 1)
                elif k == 4:
                    dve.wait_ge(s_dve, chain.next())
                    dve.nop(nofuse=True)
                    for i in range(QT):
                        last = dve.bn_aggr(lnst[:, i, 6:8], lnst[:, i, 0:6])
                    last.then_inc(s_var, 1)
                elif k in (6, 7):
                    dve.wait_ge(s_rstd, q + (3 * QUADS + 1))
                    for i in (0, 1) if k == 6 else (2, 3):
                        xt = x[:, ds(q * QT + i, 1), :]
                        dve.tensor_scalar(xt, xt, lnst[:, i, 6:7], lnst[:, i, 9:10], ALU.subtract, ALU.mult)\
                            .then_inc(s_xmade, 1)

            def group(l, g, gg, par, banks_before, packing=None, norm=None):
                if norm is None:
                    chain.enter(g, LINKS[l])
                else:
                    chain.enter(norm, 2)
                for k in range(BITS):
                    unit = g * BITS + (l * H * UNITS + k)
                    r = k % 2
                    shift = (6 - k, ALU.logical_shift_left) if k <= 6 else (1, ALU.logical_shift_right)
                    words = packed[:, :, ds(gg * (2 * WORDS) + par * WORDS, WORDS)]
                    if l == 3:
                        dve.wait_ge(s_unit, unit - 1 + CREDIT)
                        dve.tensor_scalar(edge[:, r], words, shift[0], ONE, shift[1], ALU.bitwise_and)\
                            .then_inc(s_sides, 1)
                    else:
                        dve.tensor_scalar(edge[:, r], words, shift[0], ONE, shift[1], ALU.bitwise_and)\
                            .then_inc(s_dve, 1)
                        dve.wait_ge(s_dve, chain.next())
                        dve.wait_ge(s_above, unit + 1)
                        dve.wait_ge(s_unit, unit - 1 + CREDIT)
                        dve.tensor_tensor(pos[:, r], edge[:, r], above[:, r].bitcast(U32), ALU.bitwise_and)\
                            .then_inc(s_dve, 1)
                        dve.wait_ge(s_dve, chain.next())
                        dve.tensor_tensor(neg[:, r], edge[:, r], pos[:, r], ALU.bitwise_xor).then_inc(s_sides, 1)
                    if k == (1 if packing is None else 0) and banks_before is not None:
                        evacuate(l, banks_before, 1 - par, g)
                    if packing is not None and k % 2 == 0:
                        convert(packing + k // 2)
                    if packing is not None and k % 2 == 1:
                        store_packed(packing + k // 2)
                    if norm is not None:
                        output_norm(norm, k)

            def one_pass(l, p, first=0):
                with dve.Fori(first, NG // 2) as gg:
                    for par in range(2):
                        group(l, p * NG + gg * 2 + par, gg, par, 1 - par)

            def attention(l):
                if l == 0:
                    for begin, end in ((0, PACKING // 2), (PACKING // 2, NG // 2)):
                        with dve.Fori(begin, end) as gg:
                            for par in range(2):
                                group(0, gg * 2 + par, gg, par, 0,
                                      gg * (2 * GT) + (PACKED_FIRST + par * GT) if begin == 0 else None)
                    evacuate(0, 0, 1, NG)
                    group(0, NG, 0, 0, None)
                    group(0, NG + 1, 0, 1, 0)
                    one_pass(0, 1, 1)
                    with dve.Fori(2, H) as p:
                        one_pass(0, p)
                elif l < 3:
                    with dve.Fori(0, H) as p:
                        one_pass(l, p)
                else:
                    with dve.Fori(0, H - 1) as p:
                        one_pass(l, p)
                    last_pass = (H - 1) * NG
                    for par in range(2):
                        group(3, last_pass + par, 0, par, 1 - par)
                    with dve.Fori(1, NG // 2) as gg:
                        for par in range(2):
                            group(3, gg * 2 + (last_pass + par), gg, par, 1 - par, norm=gg * 2 + (par - 2))
                    chain.leave(NG - 2)
                    evacuate(3, 1, 1, H * NG)
                    for q in (QUADS - 2, QUADS - 1):
                        for k in range(BITS):
                            output_norm(q, k)
                    chain.settle()
                    return
                if LINKS[l]:
                    chain.leave(H * NG)
                evacuate(l, 1, 1, H * NG)

            def dense2():
                dve.wait_ge(E.rows, 16 * (4 + len(row)))
                dve.tensor_tensor(row["b_bcdt"][:, 2 * SD:], row["b_bcdt"][:, 2 * SD:], row["A"], ALU.add)\
                    .then_inc(s_dve, 1)
                dve.wait_ge(s_dve, chain.next())
                dve.tensor_scalar(ecol[:, 24:25], c_cp, 1.0, None, ALU.add).then_inc(s_dve, 1)
                dve.wait_ge(s_dve, chain.next())
                dve.tensor_scalar(c_d_twice, c_d, 2.0, None, ALU.mult)
                dve.tensor_scalar(c_hz_half, c_hz[:, 4:8], 0.5, None, ALU.mult).then_inc(E.ready, 1)
                chain.settle()

                def both(name):
                    return row[name].unsqueeze(1).to_broadcast([P, ET, row_widths[name]])

                def stats(tile, st, signal):
                    n = tile.shape[-1]
                    dve.bn_stats(st[:, 0:6], tile).then_inc(s_dve, 1)
                    dve.wait_ge(s_dve, chain.next())
                    dve.nop(nofuse=True)
                    dve.bn_aggr(st[:, 6:8], st[:, 0:6]).then_inc(signal, 1)

                def wide_in(at, which, tiles, bias):
                    for t in range(ET):
                        dve.wait_ge(E.wide_ps, at + (t + 1))
                        dve.tensor_tensor(tiles[:, t, :], bank[3 + t][:, :], row[bias], ALU.add).then_inc(s_dve, 1)
                        dve.wait_ge(s_dve, chain.next())
                        dve.nop(nofuse=True)
                        stats(tiles[:, t, :], est[:, which, t, :], E.var)

                def wide_norm(at, which, tiles):
                    for t in range(ET):
                        dve.wait_ge(E.rstd, at + (t + 1))
                        dve.tensor_scalar(tiles[:, t, :], tiles[:, t, :], est[:, which, t, 6:7],
                                          est[:, which, t, 9:10], ALU.subtract, ALU.mult).then_inc(E.norm, 1)

                def wide_silu(at, tanh_tiles, tiles):
                    for t in range(ET):
                        dve.wait_ge(E.tanh, at + (t + 1))
                        dve.scalar_tensor_tensor(out=tiles[:, t, :], in0=tanh_tiles[t], scalar=1.0,
                                                 in1=tiles[:, t, :], op0=ALU.add, op1=ALU.mult).then_inc(E.silu, 1)

                def gated(i, b):
                    dve.wait_ge(E.z_tanh, i * 4 + b + 1)
                    dve.scalar_tensor_tensor(out=z_part[:, b % 2, :], in0=z_tanh[:, b % 2, :], scalar=1.0,
                                             in1=z_part[:, b % 2, :], op0=ALU.add, op1=ALU.mult)\
                        .then_inc(s_dve, 1)
                    dve.wait_ge(s_dve, chain.next())
                    dve.scalar_tensor_tensor(out=uT[:, b, :], in0=z_part[:, b % 2, :], scalar=c_d_twice,
                                             in1=h_part[:, b % 2, :], op0=ALU.add, op1=ALU.mult)\
                        .then_inc(E.uT, 1)

                def step(i, new, old):
                    if new:
                        for t in range(ET):
                            dve.wait_ge(E.bc_ps, i * ET + t + 1)
                            dve.tensor_tensor(bcdt[:, t, :], bank[1 + t][:, 0:3 * SD], row["b_bcdt"], ALU.add)\
                                .then_inc(s_dve, 1)
                            dve.wait_ge(s_dve, chain.next())
                            dve.tensor_reduce(ecol[:, 16 + t:17 + t], bcdt[:, t, 2 * SD:3 * SD], AX.X, ALU.max,
                                              negate=True).then_inc(E.top, 1)
                        for t in range(ET):
                            dve.wait_ge(E.exp, i * ET + t + 1)
                            dve.reciprocal(ecol[:, 20 + t:21 + t], ecol[:, 18 + t:19 + t]).then_inc(s_dve, 1)
                            dve.wait_ge(s_dve, chain.next())
                            dve.scalar_tensor_tensor(out=ba[:, t, :], in0=dt_exp[:, t, :],
                                                     scalar=ecol[:, 20 + t:21 + t], in1=bcdt[:, t, 0:SD],
                                                     op0=ALU.mult, op1=ALU.mult).then_inc(E.ba, 1)
                    if old:
                        wide_in(wide_count(i, 1), 1, wide_g, "g1_b")
                    if new:
                        dve.wait_ge(E.ab_ps, i + 1)
                        for b in range(2):
                            last = dve.scalar_tensor_tensor(out=hsT[:, b, :], in0=bank[6][:, b * EI:(b + 1) * EI],
                                                            scalar=c_abp[:, b:b + 1], in1=whT[:, b, :],
                                                            op0=ALU.add, op1=ALU.mult)
                        last.then_inc(E.hsT, 1)
                    if old:
                        wide_norm(wide_count(i, 1), 1, wide_g)
                    if new:
                        for t in range(ET):
                            dve.tensor_tensor(c_prod, bcdt[:, t, SD:2 * SD], row["cp_w"], ALU.mult)\
                                .then_inc(s_dve, 1)
                            dve.wait_ge(s_dve, chain.next())
                            dve.tensor_reduce(ecol[:, 26 + t:27 + t], c_prod, AX.X, ALU.add).then_inc(s_dve, 1)
                            dve.wait_ge(s_dve, chain.next())
                            dve.tensor_tensor(ecol[:, 22 + t:23 + t], ecol[:, 26 + t:27 + t],
                                              ecol[:, 24:25], ALU.add).then_inc(s_dve, 1)
                            dve.wait_ge(s_dve, chain.next())
                        wide_in(wide_count(i, 0), 0, wide, "fe1_b")
                        wide_norm(wide_count(i, 0), 0, wide)
                    if old:
                        wide_silu(wide_count(i, 1), wide_g_tanh, wide_g)
                    if new:
                        for b in range(4):
                            gated(i, b)
                        wide_silu(wide_count(i, 0), [wide_tanh[:, t, :] for t in range(ET)], wide)
                    if old:
                        dve.wait_ge(E.g2_ps, i)
                        dve.tensor_tensor(gate, bank[6][:, :].rearrange("p (t f) -> p t f", t=ET), both("g2_b"),
                                          ALU.add).then_inc(E.gate_in, 1)
                    if new:
                        dve.wait_ge(E.out_ps, i + 1)
                        if old:
                            dve.wait_ge(E.parts, i)
                        dve.scalar_tensor_tensor(out=hs2, in0=bank[0][:, :].rearrange("p (t f) -> p t f", t=ET),
                                                 scalar=0.5, in1=both("out_b"), op0=ALU.mult, op1=ALU.add)\
                            .then_inc(s_dve, 1)
                        dve.wait_ge(s_dve, chain.next())
                        for t in range(ET):
                            last = dve.tensor_scalar(hs2[:, t, :], hs2[:, t, :], ecol[:, 22 + t:23 + t], None,
                                                     ALU.mult)
                        last.then_inc(E.hs2, 1)
                        dve.wait_ge(E.fe2_ps, i + 1)
                        dve.tensor_tensor(henh, bank[2][:, :].rearrange("p (t f) -> p t f", t=ET), both("fe2_b"),
                                          ALU.add).then_inc(E.henh, 1)
                    if old:
                        dve.wait_ge(E.fused, i)
                        dve.nop(nofuse=True)
                        for t in range(ET):
                            stats(fused[:, t, :], est[:, 2, t, :], E.fvar)
                        for t in range(ET):
                            dve.wait_ge(E.frstd, (i - 1) * ET + (t + 1))
                            dve.tensor_scalar(fused[:, t, :], fused[:, t, :], est[:, 2, t, 6:7],
                                              est[:, 2, t, 9:10], ALU.subtract, ALU.mult).then_inc(E.fnorm, 1)

                step(0, True, False)
                chain.settle()
                with dve.Fori(1, EG) as i:
                    chain.enter(i - 1, 10 * ET + 5)
                    step(i, True, True)
                chain.leave(EG - 1)
                step(EG, False, True)
                chain.settle()
                dve.wait_ge(E.x, T)

            for i, signal in enumerate((s_sides, s_sides, s_h, s_packed, s_packed)):
                dve.memset(credits[:, 3 + i:4 + i], 0.0).then_inc(signal, 1)
            for it in range(GT):
                dve.memset(bank[it][:, :], 0.0)
                last = dve.memset(bank[GT + it][:, :], 0.0)
            last.then_inc(s_const, 1)
            dve.memset(credits[:, 2:3], 0.0).then_inc(s_sums, 1)
            for l in range(last_layer + 1):
                if l == 3:
                    dense2()
                fold_weights(l)
                if l == 0:
                    with dve.Fori(0, QUADS) as t:
                        pack(t)
                else:
                    dve.wait_ge(s_quot, l * H * NG + CREDIT)
                    between(l)
                stats(l)
                attention(l)
            if last_layer == 2:
                dense2()
            if last_layer < 3:
                dve.wait_ge(s_quot, (last_layer + 1) * H * NG + CREDIT)
                between(last_layer + 1)


def kernel(**inputs):
    import numpy as _np
    import concourse.bacc as _bacc
    from concourse import mybir as _mybir
    from concourse.bass_utils import run_bass_kernel_spmd as _run

    nc = _bacc.Bacc("TRN2", target_bir_lowering=False, num_devices=1)
    arrays, args = {}, {}
    for name, a in inputs.items():
        a = _np.ascontiguousarray(a)
        arrays[f"in_{name}_dram"] = a
        args[name] = nc.dram_tensor(f"in_{name}_dram", a.shape, _mybir.dt.from_np(a.dtype),
                                    kind="ExternalInput").ap()
    out = nc.dram_tensor("out_0_dram", (N, F), F32, kind="ExternalOutput").ap()
    gnn_kernel(nc, args, out)
    r = _run(nc, [arrays], core_ids=[0])
    return r.results[0]["out_0_dram"]
```
